# Optimizing a Trainium2 kernel written in Bass

```python
import numpy as np
import jax
import jax.numpy as jnp

def _softmax(x, axis=-1):
    return jax.nn.softmax(x, axis=axis)
def _gelu(x):
    return jax.nn.gelu(x, approximate=True)
def _silu(x):
    return jax.nn.silu(x)
def _sigmoid(x):
    return jax.nn.sigmoid(x)
def _layernorm(x, axis=-1, eps=1e-5):
    m = jnp.mean(x, axis=axis, keepdims=True)
    v = jnp.var(x, axis=axis, keepdims=True)
    return (x - m) / jnp.sqrt(v + eps)
def _scatter_add(tgt, idx, src, axis=0):
    return tgt.at[idx].add(src)
def _segment_sum(src, seg, n):
    return jax.ops.segment_sum(src, seg, n)

kernel_name = 'mk_metaformer_d2_conv_nchw256_30fcbb'

def setup_inputs(seed: int = 0):
    np.random.seed(seed)
    _w = jnp.asarray
    def _rec_inputs():
        import jax
        import jax.numpy as jnp
        _gk = jax.random.key(seed)
        x = -0.0005207 + 1.001 * jax.random.normal(jax.random.fold_in(_gk, 1), (2, 256, 64, 64), jnp.float32)
        return x
    x = _rec_inputs()
    def _L0_conv_setup():
        import jax, jax.numpy as jnp
        import numpy as np
        from jax import lax
        DIM = 256
        D_STATE = 16
        D_CONV = 4
        EXPAND = 2
        D_INNER = EXPAND * DIM
        DT_RANK = (DIM + 15) // 16
        key = jax.random.key(seed)
        ks = jax.random.split(key, 12)
        B, H, W = (2, 64, 64)

        def rn(k, shape, scale):
            return jax.random.normal(k, shape, jnp.float32) * scale
        x = rn(ks[0], (B, DIM, H, W), 1.0)
        gamma = jnp.ones((DIM,), jnp.float32)
        beta = jnp.zeros((DIM,), jnp.float32)
        W_in = rn(ks[1], (2 * D_INNER, DIM), DIM ** (-0.5))
        conv_w = rn(ks[2], (D_INNER, 1, D_CONV), D_CONV ** (-0.5))
        conv_b = rn(ks[3], (D_INNER,), 0.02)
        W_xp = rn(ks[4], (DT_RANK + 2 * D_STATE, D_INNER), D_INNER ** (-0.5))
        W_dt = rn(ks[5], (D_INNER, DT_RANK), DT_RANK ** (-0.5))
        b_dt = jnp.log(jnp.expm1(jax.random.uniform(ks[6], (D_INNER,), jnp.float32, 0.001, 0.1)))
        A_log = jnp.log(jnp.tile(jnp.arange(1, D_STATE + 1, dtype=jnp.float32)[None, :], (D_INNER, 1)))
        D = jnp.ones((D_INNER,), jnp.float32)
        W_out = rn(ks[7], (DIM, D_INNER), D_INNER ** (-0.5))
        W1 = rn(ks[8], (4 * DIM, DIM), DIM ** (-0.5))
        b1 = jnp.zeros((4 * DIM,), jnp.float32)
        W2 = rn(ks[9], (DIM, 4 * DIM), (4 * DIM) ** (-0.5))
        b2 = jnp.zeros((DIM,), jnp.float32)
        return dict(x=x, gamma=gamma, beta=beta, W_in=W_in, conv_w=conv_w, conv_b=conv_b, W_xp=W_xp, W_dt=W_dt, b_dt=b_dt, A_log=A_log, D=D, W_out=W_out, W1=W1, b1=b1, W2=W2, b2=b2)
    _L0_conv_all = _L0_conv_setup()
    _L0_conv_in = {k: v for k, v in _L0_conv_all.items() if k in ('gamma', 'beta', 'W_in', 'conv_w', 'conv_b', 'W_xp', 'W_dt', 'b_dt', 'A_log', 'D', 'W_out', 'W1', 'b1', 'W2', 'b2', )}
    del _L0_conv_all

    def _L0_ffn_setup():
        import jax, jax.numpy as jnp
        import numpy as np
        B, N, D = (16, 4096, 256)
        NUM_EXPERTS, TOP_K, HEADS = (4, 2, 4)
        N_EDGES = 1048576
        LN_EPS = 1e-05

        def _layernorm(x, g, b):
            mu = x.mean(-1, keepdims=True)
            var = ((x - mu) ** 2).mean(-1, keepdims=True)
            return (x - mu) * jax.lax.rsqrt(var + LN_EPS) * g + b

        def _forward(x, edge_index, W_gat, att_src, att_dst, b_gat, ln_gamma, ln_beta, W1, b1, W2, b2):
            Bc, Nc, Dc = x.shape
            M = Bc * Nc
            x_flat = x.reshape(M, Dc)
            h = (x_flat @ W_gat).reshape(M, HEADS, NUM_EXPERTS)
            loops = jnp.arange(M, dtype=edge_index.dtype)
            src = jnp.concatenate([edge_index[0], loops])
            dst = jnp.concatenate([edge_index[1], loops])
            a_src = (h * att_src).sum(-1)
            a_dst = (h * att_dst).sum(-1)
            e = jax.nn.leaky_relu(a_src[src] + a_dst[dst], negative_slope=0.2)
            e_max = jax.ops.segment_max(e, dst, num_segments=M)
            ee = jnp.exp(e - e_max[dst])
            denom = jax.ops.segment_sum(ee, dst, num_segments=M)
            alpha = ee / (denom[dst] + 1e-16)
            msg = h[src] * alpha[:, :, None]
            agg = jax.ops.segment_sum(msg, dst, num_segments=M).reshape(M, HEADS * NUM_EXPERTS) + b_gat
            scores = _layernorm(agg, ln_gamma, ln_beta).reshape(M, HEADS, NUM_EXPERTS).mean(1)
            scores = scores.reshape(Bc, Nc, NUM_EXPERTS)
            topk_s, topk_i = jax.lax.top_k(scores, TOP_K)
            w = jax.nn.softmax(topk_s, axis=-1)
            out = jnp.zeros_like(x)
            for ei in range(NUM_EXPERTS):
                g = jnp.where(topk_i == ei, w, 0.0).sum(-1)
                hh = jax.nn.gelu(x @ W1[ei] + b1[ei], approximate=False)
                out = out + g[..., None] * (hh @ W2[ei] + b2[ei])
            return out
        key = jax.random.key(seed)
        ks = jax.random.split(key, 8)
        s = 0.05
        return {'x': jax.random.normal(ks[0], (B, N, D), jnp.float32), 'W_gat': jax.random.normal(ks[1], (D, HEADS * NUM_EXPERTS), jnp.float32) * s, 'att_src': jax.random.normal(ks[2], (HEADS, NUM_EXPERTS), jnp.float32) * s, 'att_dst': jax.random.normal(ks[3], (HEADS, NUM_EXPERTS), jnp.float32) * s, 'b_gat': jnp.zeros((HEADS * NUM_EXPERTS,), jnp.float32), 'ln_gamma': jnp.ones((HEADS * NUM_EXPERTS,), jnp.float32), 'ln_beta': jnp.zeros((HEADS * NUM_EXPERTS,), jnp.float32), 'W1': jax.random.normal(ks[4], (NUM_EXPERTS, D, 2 * D), jnp.float32) * s, 'b1': jnp.zeros((NUM_EXPERTS, 2 * D), jnp.float32), 'W2': jax.random.normal(ks[5], (NUM_EXPERTS, 2 * D, D), jnp.float32) * s, 'b2': jnp.zeros((NUM_EXPERTS, D), jnp.float32), 'edge_index': jax.random.randint(ks[6], (2, N_EDGES), 0, B * N, jnp.int32)}
    _L0_ffn_all = _L0_ffn_setup()
    _L0_ffn_in = {k: v for k, v in _L0_ffn_all.items() if k in ('W_gat', 'att_src', 'att_dst', 'b_gat', 'ln_gamma', 'ln_beta', 'W1', 'b1', 'W2', 'b2', 'edge_index', )}
    del _L0_ffn_all

    def _L1_conv_setup():
        import jax, jax.numpy as jnp
        import numpy as np
        BT = np.array([[4, 0, -5, 0, 1, 0], [0, -4, -4, 1, 1, 0], [0, 4, -4, -1, 1, 0], [0, -2, -1, 2, 1, 0], [0, 2, -1, -2, 1, 0], [0, 4, 0, -5, 0, 1]], dtype=np.float32)
        G = np.array([[1 / 4, 0, 0], [-1 / 6, -1 / 6, -1 / 6], [-1 / 6, 1 / 6, -1 / 6], [1 / 24, 1 / 12, 1 / 6], [1 / 24, -1 / 12, 1 / 6], [0, 0, 1]], dtype=np.float32)
        AT = np.array([[1, 1, 1, 1, 1, 0], [0, 1, -1, 2, -2, 0], [0, 1, 1, 4, 4, 0], [0, 1, -1, 8, -8, 1]], dtype=np.float32)
        PADDING = 1
        KERNEL = 3
        IN_TILE = 6
        OUT_TILE = 4
        GROUPS = 1

        def winograd_forward(x, weight, bias, mask):
            BTj, Gj, ATj = (jnp.asarray(BT), jnp.asarray(G), jnp.asarray(AT))
            x = jnp.pad(x, ((0, 0), (0, 0), (PADDING, PADDING), (PADDING, PADDING)))
            N, C, H, W = x.shape
            out_w = H - KERNEL + 1
            pad_extra = -out_w % OUT_TILE
            if pad_extra:
                x = jnp.pad(x, ((0, 0), (0, 0), (0, pad_extra), (0, pad_extra)))
            Hp = x.shape[2]
            nT = (Hp - IN_TILE) // OUT_TILE + 1
            idx = (jnp.arange(nT) * OUT_TILE)[:, None] + jnp.arange(IN_TILE)
            tiles = x[:, :, idx, :]
            tiles = tiles[:, :, :, :, idx]
            tiles = tiles.transpose(0, 1, 2, 4, 3, 5)
            xt = jnp.einsum('ti,nchwij,uj->nchwtu', BTj, tiles, BTj)
            wt = jnp.einsum('ti,ocij,uj->octu', Gj, weight, Gj)
            wt = wt * (1.0 - mask)
            O = wt.shape[0]
            Og, Cg = (O // GROUPS, C // GROUPS)
            wtg = wt.reshape(GROUPS, Og, Cg, IN_TILE, IN_TILE)
            xtg = xt.reshape(N, GROUPS, Cg, nT, nT, IN_TILE, IN_TILE)
            yt = jnp.einsum('goctu,ngchwtu->ngohwtu', wtg, xtg)
            yt = yt.reshape(N, O, nT, nT, IN_TILE, IN_TILE)
            y = jnp.einsum('pt,nohwtu,qu->nohwpq', ATj, yt, ATj)
            y = y.transpose(0, 1, 2, 4, 3, 5).reshape(N, O, nT * OUT_TILE, nT * OUT_TILE)
            y = y + bias[None, :, None, None]
            return y[:, :, :out_w, :out_w]
        key = jax.random.key(seed)
        k1, k2, k3 = jax.random.split(key, 3)
        N, C, H, W = (32, 256, 56, 56)
        O = 256
        x = jax.random.normal(k1, (N, C, H, W), jnp.float32)
        weight = jax.random.normal(k2, (O, C // GROUPS, KERNEL, KERNEL), jnp.float32) * 0.02
        bias = jax.random.normal(k3, (O,), jnp.float32) * 0.01
        mask = jnp.zeros((O, C // GROUPS, IN_TILE, IN_TILE), jnp.float32)
        return {'x': x, 'weight': weight, 'bias': bias, 'mask': mask}
    _L1_conv_all = _L1_conv_setup()
    _L1_conv_in = {k: v for k, v in _L1_conv_all.items() if k in ('weight', 'bias', 'mask', )}
    del _L1_conv_all

    def _L1_ffn_setup():
        import jax, jax.numpy as jnp
        import numpy as np
        B, N, D = (16, 4096, 256)
        NUM_EXPERTS, TOP_K, HEADS = (4, 2, 4)
        N_EDGES = 1048576
        LN_EPS = 1e-05

        def _layernorm(x, g, b):
            mu = x.mean(-1, keepdims=True)
            var = ((x - mu) ** 2).mean(-1, keepdims=True)
            return (x - mu) * jax.lax.rsqrt(var + LN_EPS) * g + b

        def _forward(x, edge_index, W_gat, att_src, att_dst, b_gat, ln_gamma, ln_beta, W1, b1, W2, b2):
            Bc, Nc, Dc = x.shape
            M = Bc * Nc
            x_flat = x.reshape(M, Dc)
            h = (x_flat @ W_gat).reshape(M, HEADS, NUM_EXPERTS)
            loops = jnp.arange(M, dtype=edge_index.dtype)
            src = jnp.concatenate([edge_index[0], loops])
            dst = jnp.concatenate([edge_index[1], loops])
            a_src = (h * att_src).sum(-1)
            a_dst = (h * att_dst).sum(-1)
            e = jax.nn.leaky_relu(a_src[src] + a_dst[dst], negative_slope=0.2)
            e_max = jax.ops.segment_max(e, dst, num_segments=M)
            ee = jnp.exp(e - e_max[dst])
            denom = jax.ops.segment_sum(ee, dst, num_segments=M)
            alpha = ee / (denom[dst] + 1e-16)
            msg = h[src] * alpha[:, :, None]
            agg = jax.ops.segment_sum(msg, dst, num_segments=M).reshape(M, HEADS * NUM_EXPERTS) + b_gat
            scores = _layernorm(agg, ln_gamma, ln_beta).reshape(M, HEADS, NUM_EXPERTS).mean(1)
            scores = scores.reshape(Bc, Nc, NUM_EXPERTS)
            topk_s, topk_i = jax.lax.top_k(scores, TOP_K)
            w = jax.nn.softmax(topk_s, axis=-1)
            out = jnp.zeros_like(x)
            for ei in range(NUM_EXPERTS):
                g = jnp.where(topk_i == ei, w, 0.0).sum(-1)
                hh = jax.nn.gelu(x @ W1[ei] + b1[ei], approximate=False)
                out = out + g[..., None] * (hh @ W2[ei] + b2[ei])
            return out
        key = jax.random.key(seed)
        ks = jax.random.split(key, 8)
        s = 0.05
        return {'x': jax.random.normal(ks[0], (B, N, D), jnp.float32), 'W_gat': jax.random.normal(ks[1], (D, HEADS * NUM_EXPERTS), jnp.float32) * s, 'att_src': jax.random.normal(ks[2], (HEADS, NUM_EXPERTS), jnp.float32) * s, 'att_dst': jax.random.normal(ks[3], (HEADS, NUM_EXPERTS), jnp.float32) * s, 'b_gat': jnp.zeros((HEADS * NUM_EXPERTS,), jnp.float32), 'ln_gamma': jnp.ones((HEADS * NUM_EXPERTS,), jnp.float32), 'ln_beta': jnp.zeros((HEADS * NUM_EXPERTS,), jnp.float32), 'W1': jax.random.normal(ks[4], (NUM_EXPERTS, D, 2 * D), jnp.float32) * s, 'b1': jnp.zeros((NUM_EXPERTS, 2 * D), jnp.float32), 'W2': jax.random.normal(ks[5], (NUM_EXPERTS, 2 * D, D), jnp.float32) * s, 'b2': jnp.zeros((NUM_EXPERTS, D), jnp.float32), 'edge_index': jax.random.randint(ks[6], (2, N_EDGES), 0, B * N, jnp.int32)}
    _L1_ffn_all = _L1_ffn_setup()
    _L1_ffn_in = {k: v for k, v in _L1_ffn_all.items() if k in ('W_gat', 'att_src', 'att_dst', 'b_gat', 'ln_gamma', 'ln_beta', 'W1', 'b1', 'W2', 'b2', 'edge_index', )}
    del _L1_ffn_all

    return {
        "x": x,
        "L0_conv_gamma": _L0_conv_in["gamma"],
        "L0_conv_beta": _L0_conv_in["beta"],
        "L0_conv_W_in": _L0_conv_in["W_in"],
        "L0_conv_conv_w": _L0_conv_in["conv_w"],
        "L0_conv_conv_b": _L0_conv_in["conv_b"],
        "L0_conv_W_xp": _L0_conv_in["W_xp"],
        "L0_conv_W_dt": _L0_conv_in["W_dt"],
        "L0_conv_b_dt": _L0_conv_in["b_dt"],
        "L0_conv_A_log": _L0_conv_in["A_log"],
        "L0_conv_D": _L0_conv_in["D"],
        "L0_conv_W_out": _L0_conv_in["W_out"],
        "L0_conv_W1": _L0_conv_in["W1"],
        "L0_conv_b1": _L0_conv_in["b1"],
        "L0_conv_W2": _L0_conv_in["W2"],
        "L0_conv_b2": _L0_conv_in["b2"],
        "L0_ffn_W_gat": _L0_ffn_in["W_gat"],
        "L0_ffn_att_src": _L0_ffn_in["att_src"],
        "L0_ffn_att_dst": _L0_ffn_in["att_dst"],
        "L0_ffn_b_gat": _L0_ffn_in["b_gat"],
        "L0_ffn_ln_gamma": _L0_ffn_in["ln_gamma"],
        "L0_ffn_ln_beta": _L0_ffn_in["ln_beta"],
        "L0_ffn_W1": _L0_ffn_in["W1"],
        "L0_ffn_b1": _L0_ffn_in["b1"],
        "L0_ffn_W2": _L0_ffn_in["W2"],
        "L0_ffn_b2": _L0_ffn_in["b2"],
        "L0_ffn_edge_index": _L0_ffn_in["edge_index"],
        "L1_conv_weight": _L1_conv_in["weight"],
        "L1_conv_bias": _L1_conv_in["bias"],
        "L1_conv_mask": _L1_conv_in["mask"],
        "L1_ffn_W_gat": _L1_ffn_in["W_gat"],
        "L1_ffn_att_src": _L1_ffn_in["att_src"],
        "L1_ffn_att_dst": _L1_ffn_in["att_dst"],
        "L1_ffn_b_gat": _L1_ffn_in["b_gat"],
        "L1_ffn_ln_gamma": _L1_ffn_in["ln_gamma"],
        "L1_ffn_ln_beta": _L1_ffn_in["ln_beta"],
        "L1_ffn_W1": _L1_ffn_in["W1"],
        "L1_ffn_b1": _L1_ffn_in["b1"],
        "L1_ffn_W2": _L1_ffn_in["W2"],
        "L1_ffn_b2": _L1_ffn_in["b2"],
        "L1_ffn_edge_index": _L1_ffn_in["edge_index"],
    }

def reference(x, L0_conv_gamma, L0_conv_beta, L0_conv_W_in, L0_conv_conv_w, L0_conv_conv_b, L0_conv_W_xp, L0_conv_W_dt, L0_conv_b_dt, L0_conv_A_log, L0_conv_D, L0_conv_W_out, L0_conv_W1, L0_conv_b1, L0_conv_W2, L0_conv_b2, L0_ffn_W_gat, L0_ffn_att_src, L0_ffn_att_dst, L0_ffn_b_gat, L0_ffn_ln_gamma, L0_ffn_ln_beta, L0_ffn_W1, L0_ffn_b1, L0_ffn_W2, L0_ffn_b2, L0_ffn_edge_index, L1_conv_weight, L1_conv_bias, L1_conv_mask, L1_ffn_W_gat, L1_ffn_att_src, L1_ffn_att_dst, L1_ffn_b_gat, L1_ffn_ln_gamma, L1_ffn_ln_beta, L1_ffn_W1, L1_ffn_b1, L1_ffn_W2, L1_ffn_b2, L1_ffn_edge_index):
    import jax
    import jax.numpy as jnp
    def _L0_conv_ref(x, gamma, beta, W_in, conv_w, conv_b, W_xp, W_dt, b_dt, A_log, D, W_out, W1, b1, W2, b2):
        import jax, jax.numpy as jnp
        import numpy as np
        from jax import lax
        DIM = 256
        D_STATE = 16
        D_CONV = 4
        EXPAND = 2
        D_INNER = EXPAND * DIM
        DT_RANK = (DIM + 15) // 16
        B, C, H, W = x.shape
        L = H * W
        DI, N = A_log.shape
        R = W_dt.shape[1]
        y = x.transpose(0, 2, 3, 1).reshape(B, L, C)
        mu = y.mean(-1, keepdims=True)
        var = ((y - mu) ** 2).mean(-1, keepdims=True)
        yn = (y - mu) * lax.rsqrt(var + 1e-05) * gamma + beta
        xz = yn @ W_in.T
        xm, z = (xz[..., :DI], xz[..., DI:])
        xc = xm.transpose(0, 2, 1)
        xc = lax.conv_general_dilated(xc, conv_w, window_strides=(1,), padding=[(conv_w.shape[-1] - 1, 0)], dimension_numbers=('NCH', 'OIH', 'NCH'), feature_group_count=DI)
        u = jax.nn.silu(xc + conv_b[None, :, None]).transpose(0, 2, 1)
        proj = u @ W_xp.T
        dt = jax.nn.softplus(proj[..., :R] @ W_dt.T + b_dt)
        Bm = proj[..., R:R + N]
        Cm = proj[..., R + N:]
        A = -jnp.exp(A_log)

        def step(h, inp):
            dt_t, B_t, C_t, u_t = inp
            dA = jnp.exp(dt_t[:, :, None] * A)
            h = dA * h + (dt_t * u_t)[:, :, None] * B_t[:, None, :]
            return (h, jnp.einsum('bdn,bn->bd', h, C_t))
        h0 = jnp.zeros((B, DI, N), dt.dtype)
        _, ys = lax.scan(step, h0, (dt.transpose(1, 0, 2), Bm.transpose(1, 0, 2), Cm.transpose(1, 0, 2), u.transpose(1, 0, 2)))
        ym = (ys.transpose(1, 0, 2) + u * D) * jax.nn.silu(z)
        y2 = ym @ W_out.T + yn
        y3 = jax.nn.gelu(y2 @ W1.T + b1, approximate=False) @ W2.T + b2 + y2
        return y3.reshape(B, H, W, C).transpose(0, 3, 1, 2)

    def _L0_ffn_ref(x, W_gat, att_src, att_dst, b_gat, ln_gamma, ln_beta, W1, b1, W2, b2, edge_index):
        import jax, jax.numpy as jnp
        import numpy as np
        B, N, D = (16, 4096, 256)
        NUM_EXPERTS, TOP_K, HEADS = (4, 2, 4)
        N_EDGES = 1048576
        LN_EPS = 1e-05

        def _layernorm(x, g, b):
            mu = x.mean(-1, keepdims=True)
            var = ((x - mu) ** 2).mean(-1, keepdims=True)
            return (x - mu) * jax.lax.rsqrt(var + LN_EPS) * g + b

        def _forward(x, edge_index, W_gat, att_src, att_dst, b_gat, ln_gamma, ln_beta, W1, b1, W2, b2):
            Bc, Nc, Dc = x.shape
            M = Bc * Nc
            x_flat = x.reshape(M, Dc)
            h = (x_flat @ W_gat).reshape(M, HEADS, NUM_EXPERTS)
            loops = jnp.arange(M, dtype=edge_index.dtype)
            src = jnp.concatenate([edge_index[0], loops])
            dst = jnp.concatenate([edge_index[1], loops])
            a_src = (h * att_src).sum(-1)
            a_dst = (h * att_dst).sum(-1)
            e = jax.nn.leaky_relu(a_src[src] + a_dst[dst], negative_slope=0.2)
            e_max = jax.ops.segment_max(e, dst, num_segments=M)
            ee = jnp.exp(e - e_max[dst])
            denom = jax.ops.segment_sum(ee, dst, num_segments=M)
            alpha = ee / (denom[dst] + 1e-16)
            msg = h[src] * alpha[:, :, None]
            agg = jax.ops.segment_sum(msg, dst, num_segments=M).reshape(M, HEADS * NUM_EXPERTS) + b_gat
            scores = _layernorm(agg, ln_gamma, ln_beta).reshape(M, HEADS, NUM_EXPERTS).mean(1)
            scores = scores.reshape(Bc, Nc, NUM_EXPERTS)
            topk_s, topk_i = jax.lax.top_k(scores, TOP_K)
            w = jax.nn.softmax(topk_s, axis=-1)
            out = jnp.zeros_like(x)
            for ei in range(NUM_EXPERTS):
                g = jnp.where(topk_i == ei, w, 0.0).sum(-1)
                hh = jax.nn.gelu(x @ W1[ei] + b1[ei], approximate=False)
                out = out + g[..., None] * (hh @ W2[ei] + b2[ei])
            return out
        return _forward(x, edge_index, W_gat, att_src, att_dst, b_gat, ln_gamma, ln_beta, W1, b1, W2, b2)

    def _L1_conv_ref(x, weight, bias, mask):
        import jax, jax.numpy as jnp
        import numpy as np
        BT = np.array([[4, 0, -5, 0, 1, 0], [0, -4, -4, 1, 1, 0], [0, 4, -4, -1, 1, 0], [0, -2, -1, 2, 1, 0], [0, 2, -1, -2, 1, 0], [0, 4, 0, -5, 0, 1]], dtype=np.float32)
        G = np.array([[1 / 4, 0, 0], [-1 / 6, -1 / 6, -1 / 6], [-1 / 6, 1 / 6, -1 / 6], [1 / 24, 1 / 12, 1 / 6], [1 / 24, -1 / 12, 1 / 6], [0, 0, 1]], dtype=np.float32)
        AT = np.array([[1, 1, 1, 1, 1, 0], [0, 1, -1, 2, -2, 0], [0, 1, 1, 4, 4, 0], [0, 1, -1, 8, -8, 1]], dtype=np.float32)
        PADDING = 1
        KERNEL = 3
        IN_TILE = 6
        OUT_TILE = 4
        GROUPS = 1

        def winograd_forward(x, weight, bias, mask):
            BTj, Gj, ATj = (jnp.asarray(BT), jnp.asarray(G), jnp.asarray(AT))
            x = jnp.pad(x, ((0, 0), (0, 0), (PADDING, PADDING), (PADDING, PADDING)))
            N, C, H, W = x.shape
            out_w = H - KERNEL + 1
            pad_extra = -out_w % OUT_TILE
            if pad_extra:
                x = jnp.pad(x, ((0, 0), (0, 0), (0, pad_extra), (0, pad_extra)))
            Hp = x.shape[2]
            nT = (Hp - IN_TILE) // OUT_TILE + 1
            idx = (jnp.arange(nT) * OUT_TILE)[:, None] + jnp.arange(IN_TILE)
            tiles = x[:, :, idx, :]
            tiles = tiles[:, :, :, :, idx]
            tiles = tiles.transpose(0, 1, 2, 4, 3, 5)
            xt = jnp.einsum('ti,nchwij,uj->nchwtu', BTj, tiles, BTj)
            wt = jnp.einsum('ti,ocij,uj->octu', Gj, weight, Gj)
            wt = wt * (1.0 - mask)
            O = wt.shape[0]
            Og, Cg = (O // GROUPS, C // GROUPS)
            wtg = wt.reshape(GROUPS, Og, Cg, IN_TILE, IN_TILE)
            xtg = xt.reshape(N, GROUPS, Cg, nT, nT, IN_TILE, IN_TILE)
            yt = jnp.einsum('goctu,ngchwtu->ngohwtu', wtg, xtg)
            yt = yt.reshape(N, O, nT, nT, IN_TILE, IN_TILE)
            y = jnp.einsum('pt,nohwtu,qu->nohwpq', ATj, yt, ATj)
            y = y.transpose(0, 1, 2, 4, 3, 5).reshape(N, O, nT * OUT_TILE, nT * OUT_TILE)
            y = y + bias[None, :, None, None]
            return y[:, :, :out_w, :out_w]
        return winograd_forward(x, weight, bias, mask)

    def _L1_ffn_ref(x, W_gat, att_src, att_dst, b_gat, ln_gamma, ln_beta, W1, b1, W2, b2, edge_index):
        import jax, jax.numpy as jnp
        import numpy as np
        B, N, D = (16, 4096, 256)
        NUM_EXPERTS, TOP_K, HEADS = (4, 2, 4)
        N_EDGES = 1048576
        LN_EPS = 1e-05

        def _layernorm(x, g, b):
            mu = x.mean(-1, keepdims=True)
            var = ((x - mu) ** 2).mean(-1, keepdims=True)
            return (x - mu) * jax.lax.rsqrt(var + LN_EPS) * g + b

        def _forward(x, edge_index, W_gat, att_src, att_dst, b_gat, ln_gamma, ln_beta, W1, b1, W2, b2):
            Bc, Nc, Dc = x.shape
            M = Bc * Nc
            x_flat = x.reshape(M, Dc)
            h = (x_flat @ W_gat).reshape(M, HEADS, NUM_EXPERTS)
            loops = jnp.arange(M, dtype=edge_index.dtype)
            src = jnp.concatenate([edge_index[0], loops])
            dst = jnp.concatenate([edge_index[1], loops])
            a_src = (h * att_src).sum(-1)
            a_dst = (h * att_dst).sum(-1)
            e = jax.nn.leaky_relu(a_src[src] + a_dst[dst], negative_slope=0.2)
            e_max = jax.ops.segment_max(e, dst, num_segments=M)
            ee = jnp.exp(e - e_max[dst])
            denom = jax.ops.segment_sum(ee, dst, num_segments=M)
            alpha = ee / (denom[dst] + 1e-16)
            msg = h[src] * alpha[:, :, None]
            agg = jax.ops.segment_sum(msg, dst, num_segments=M).reshape(M, HEADS * NUM_EXPERTS) + b_gat
            scores = _layernorm(agg, ln_gamma, ln_beta).reshape(M, HEADS, NUM_EXPERTS).mean(1)
            scores = scores.reshape(Bc, Nc, NUM_EXPERTS)
            topk_s, topk_i = jax.lax.top_k(scores, TOP_K)
            w = jax.nn.softmax(topk_s, axis=-1)
            out = jnp.zeros_like(x)
            for ei in range(NUM_EXPERTS):
                g = jnp.where(topk_i == ei, w, 0.0).sum(-1)
                hh = jax.nn.gelu(x @ W1[ei] + b1[ei], approximate=False)
                out = out + g[..., None] * (hh @ W2[ei] + b2[ei])
            return out
        return _forward(x, edge_index, W_gat, att_src, att_dst, b_gat, ln_gamma, ln_beta, W1, b1, W2, b2)

    def _gn(v, G=32, eps=1e-5):
        B_, C_, H_, W_ = v.shape
        g = v.reshape(B_, G, C_ // G, H_, W_)
        m = jnp.mean(g, axis=(2, 3, 4), keepdims=True)
        s = jnp.var(g, axis=(2, 3, 4), keepdims=True)
        return ((g - m) / jnp.sqrt(s + eps)).reshape(v.shape)

    def _ln_c(v, eps=1e-6):
        m = jnp.mean(v, axis=1, keepdims=True)
        s = jnp.var(v, axis=1, keepdims=True)
        return (v - m) / jnp.sqrt(s + eps)

    def _ln_t(v, eps=1e-5):
        m = jnp.mean(v, axis=-1, keepdims=True)
        s = jnp.var(v, axis=-1, keepdims=True)
        return (v - m) / jnp.sqrt(s + eps)

    def _to_tokens(v):
        B_, C_, H_, W_ = v.shape
        return v.reshape(B_, C_, H_ * W_).transpose(0, 2, 1)
    def _from_tokens(t, like):
        B_, C_, H_, W_ = like.shape
        return t.transpose(0, 2, 1).reshape(B_, C_, H_, W_)

    x = x + _L0_conv_ref(_ln_c(x), L0_conv_gamma, L0_conv_beta, L0_conv_W_in, L0_conv_conv_w, L0_conv_conv_b, L0_conv_W_xp, L0_conv_W_dt, L0_conv_b_dt, L0_conv_A_log, L0_conv_D, L0_conv_W_out, L0_conv_W1, L0_conv_b1, L0_conv_W2, L0_conv_b2)
    t = _to_tokens(x)
    t = t + _L0_ffn_ref(_ln_t(t), L0_ffn_W_gat, L0_ffn_att_src, L0_ffn_att_dst, L0_ffn_b_gat, L0_ffn_ln_gamma, L0_ffn_ln_beta, L0_ffn_W1, L0_ffn_b1, L0_ffn_W2, L0_ffn_b2, L0_ffn_edge_index)
    x = _from_tokens(t, x)
    x = x + _L1_conv_ref(_ln_c(x), L1_conv_weight, L1_conv_bias, L1_conv_mask)
    t = _to_tokens(x)
    t = t + _L1_ffn_ref(_ln_t(t), L1_ffn_W_gat, L1_ffn_att_src, L1_ffn_att_dst, L1_ffn_b_gat, L1_ffn_ln_gamma, L1_ffn_ln_beta, L1_ffn_W1, L1_ffn_b1, L1_ffn_W2, L1_ffn_b2, L1_ffn_edge_index)
    x = _from_tokens(t, x)
    return x


_drawn_inputs = setup_inputs


def setup_inputs(seed=0):
    import zlib

    import numpy as np

    out = dict(_drawn_inputs(seed))
    spreads = {'L0_conv_gamma': (1.0, 0.2),
     'L0_conv_beta': (0.0, 0.1),
     'L0_conv_D': (1.0, 0.2),
     'L0_conv_b1': (0.0, 0.1),
     'L0_conv_b2': (0.0, 0.1),
     'L0_ffn_b_gat': (0.0, 0.1),
     'L0_ffn_ln_gamma': (1.0, 0.2),
     'L0_ffn_ln_beta': (0.0, 0.1),
     'L0_ffn_b1': (0.0, 0.1),
     'L0_ffn_b2': (0.0, 0.1),
     'L1_ffn_b_gat': (0.0, 0.1),
     'L1_ffn_ln_gamma': (1.0, 0.2),
     'L1_ffn_ln_beta': (0.0, 0.1),
     'L1_ffn_b1': (0.0, 0.36),
     'L1_ffn_b2': (0.0, 0.269)}
    factors = {'L0_conv_conv_b': 3.904,
     'L0_ffn_att_src': 8.0,
     'L0_ffn_att_dst': 8.0,
     'L1_conv_bias': 3.48,
     'L1_ffn_att_src': 3.506,
     'L1_ffn_att_dst': 5.698}
    for name, (base, spread) in spreads.items():
        noise = np.random.default_rng([zlib.crc32(name.encode()), seed]).standard_normal(out[name].shape)
        drawn = base * np.exp(spread * noise) if base else spread * noise
        out[name] = jnp.asarray(drawn.astype(out[name].dtype))
    for name, factor in factors.items():
        out[name] = (out[name] * factor).astype(out[name].dtype)
    return out
```

```python
from contextlib import ExitStack

import numpy as np
import concourse.bass as bass
from concourse import mybir

F32 = mybir.dt.float32
BF16 = mybir.dt.bfloat16
I32 = mybir.dt.int32
U32 = mybir.dt.uint32
ALU = mybir.AluOpType
ACT = mybir.ActivationFunctionType
AX = mybir.AxisListType

P = 128
B, C, HW = 2, 256, 64
L = HW * HW
M = B * L
KB = C // P
T = 512
TI = L // T
DI, NS, R = 512, 16, 16
MB = DI // P
FF = 4 * C
FB = FF // P


class Phase:

    def __init__(self, nc, name):
        self.nc, self.name, self.ctx = nc, name, ExitStack()
        self.sems = []

    def __enter__(self):
        return self

    def sb(self, name, shape, dt=F32):
        return self.ctx.enter_context(self.nc.sbuf_tensor(f"{self.name}_{name}", shape, dt))

    def ps(self, name, shape, dt=F32):
        return self.ctx.enter_context(self.nc.psum_tensor(f"{self.name}_{name}", shape, dt))

    def sem(self, name):
        s = self.nc.alloc_semaphore(name=f"{self.name}_{name}")
        self.sems.append(s)
        return s

    def __exit__(self, *exc):
        if exc[0] is None:
            self.nc.all_engine_barrier()
            self.nc.clear_and_free_semaphores(self.sems)
            self.nc.all_engine_barrier()
        self.ctx.close()


def bcast(ap, n):
    return ap.rearrange("p (o t) -> p o t", o=1).to_broadcast([ap.shape[0], n, ap.shape[1]])


def mamba_phase(nc, w, x_in, x_out):
    with Phase(nc, "mamba") as ph:
        sb, ps, sem = ph.sb, ph.ps, ph.sem
        w_in = sb("w_in", [P, KB, 2 * DI])
        w_xp = sb("w_xp", [P, MB, R + 2 * NS])
        w_dt = sb("w_dt", [R, DI])
        w_out = sb("w_out", [P, MB, C])
        w_1 = sb("w_1", [P, KB, FF])
        w_2 = sb("w_2", [P, FB, C])
        gamma, beta = sb("gamma", [P, KB]), sb("beta", [P, KB])
        conv_w, conv_b = sb("conv_w", [P, MB, 4]), sb("conv_b", [P, MB])
        b_dt, d_skip = sb("b_dt", [P, MB]), sb("d_skip", [P, MB])
        b_1, b_2 = sb("b_1", [P, FB]), sb("b_2", [P, KB])
        a_neg, a_log = sb("a_neg", [P, MB, NS]), sb("a_log", [P, MB, NS])
        ones_mean, ident = sb("ones_mean", [P, P]), sb("ident", [P, P])
        eps_c, eps_n, one = sb("eps_c", [P, 1]), sb("eps_n", [P, 1]), sb("one", [P, 1])
        xt, xc, v, yn, sq = (sb(n, [P, KB, T]) for n in ("xt", "xc", "v", "yn", "sq"))
        y2, xo = v, sq
        lnv, rstd = sb("lnv", [P, T]), sb("rstd", [P, T])
        xm = sb("xm", [P, B, MB, T + 3])
        zs, cx, u, r_dt, dt, dtu, dbu = (sb(n, [P, MB, T]) for n in ("zs", "cx", "u", "r_dt", "dt", "dtu", "dbu"))
        ea, y = cx, r_dt
        prj = sb("prj", [R + 2 * NS, T])
        dA, hh, hc = (sb(n, [P, 2, MB, T]) for n in ("dA", "hh", "hc"))
        g1 = dA[:, :, :, :].rearrange("p a m t -> p (a m) t")
        state = sb("state", [P, B, NS, MB])
        bank = ps("bank", [P, 8, T])

        weights_in, a_exp, consts = sem("weights_in"), sem("a_exp"), sem("consts")
        x_in_s, x_stored, out_free = sem("x_in"), sem("x_stored"), sem("out_free")
        mean = [sem(f"mean{k}") for k in range(2)]
        cent = [sem(f"cent{k}") for k in range(2)]
        sqd = [sem(f"sqd{k}") for k in range(2)]
        var = [sem(f"var{k}") for k in range(2)]
        lns = [sem(f"lns{k}") for k in range(2)]
        rst = [sem(f"rst{k}") for k in range(2)]
        nrm = [sem(f"nrm{k}") for k in range(2)]
        yn_s, xz_s, xm_s, zs_s, conv_s, tail_s, u_s = (sem(n) for n in ("yn", "xz", "xm", "zs", "conv", "tail", "u"))
        proj_s, prj_s, dtp_s, dta_s, dte_s, dt_s, dtu_s = (sem(n) for n in ("proj", "prj", "dtp", "dta", "dte", "dt", "dtu"))
        abs_s = sem("abs")
        bc_s, dA_s, dbu_s, scan_s, save_s, hc_s, yacc_s = (sem(n) for n in ("bc", "dA", "dbu", "scan", "save", "hc", "yacc"))
        yd_s, ym_s, wo_s, y2_s, up_s, g1_s, dn_s, y3_s, x1_s = (sem(n) for n in ("yd", "ym", "wo", "y2", "up", "g1", "dn", "y3", "x1"))

        loads = [(w_in, w["W_inT"].rearrange("(k p) n -> p k n", p=P)), (w_xp, w["W_xpT"].rearrange("(k p) n -> p k n", p=P)),
                 (w_dt, w["W_dtT"]), (w_out, w["W_outT"].rearrange("(k p) n -> p k n", p=P)),
                 (w_1, w["W1T"].rearrange("(k p) n -> p k n", p=P)), (w_2, w["W2T"].rearrange("(k p) n -> p k n", p=P)),
                 (conv_w, w["conv_w"].rearrange("(k p) o n -> p k (o n)", p=P)),
                 (a_log, w["A_log"].rearrange("(k p) n -> p k n", p=P))]
        vectors = [(gamma, "gamma"), (beta, "beta"), (conv_b, "conv_b"), (b_dt, "b_dt"), (d_skip, "D"), (b_1, "b1"), (b_2, "b2")]
        n_loads = len(loads) + len(vectors)

        with nc.Block() as block:
            @block.sync
            def _(sp):
                for tile, src in loads:
                    sp.dma_start(tile[:], src).then_inc(weights_in, 16)
                with nc.allow_non_contiguous_dma(reason="short vectors"):
                    for tile, name in vectors:
                        sp.dma_start(tile[:], w[name].rearrange("(k p) -> p k", p=P)).then_inc(weights_in, 16)
                sp.sem_inc(out_free, 1)
                with sp.Fori(0, TI) as i:
                    for b in range(B):
                        s = i * B + b
                        sp.wait_ge(x1_s, s + 1)
                        sp.dma_start(xt[:], x_in[b].rearrange("(k p) t -> p k t", p=P)[:, :, bass.ds(i * T, T)]).then_inc(x_in_s, 16)
                        sp.wait_ge(x1_s, s + 2)
                        sp.dma_start(x_out[b].rearrange("(k p) t -> p k t", p=P)[:, :, bass.ds(i * T, T)], xo[:]).then_inc(x_stored, 16)
                        sp.wait_ge(x_stored, 16 * s + 16)
                        sp.sem_inc(out_free, 1)

            @block.gpsimd
            def _(pool):
                pool.memset(ident[:], 0.0).then_inc(consts, 1)
                pool.memset(ones_mean[:], 1.0 / C).then_inc(consts, 1)
                pool.memset(xm[:], 0.0).then_inc(consts, 1)
                pool.memset(state[:], 0.0).then_inc(consts, 1)
                pool.memset(eps_c[:], 1e-6).then_inc(consts, 1)
                pool.memset(eps_n[:], 1e-5).then_inc(consts, 1)
                pool.memset(one[:], 1.0).then_inc(consts, 1)
                pool.wait_ge(consts, 7)
                pool.affine_select(out=ident[:], in_=ident[:], compare_op=ALU.not_equal, fill=1.0, base=0,
                                   pattern=[[-1, P]], channel_multiplier=1).then_inc(consts, 1)
                with pool.Fori(0, TI) as i:
                    for b in range(B):
                        s = i * B + b
                        pool.wait_ge(hc_s, s * NS + 2)
                        pool.tensor_tensor(y[:], hc[:, 0], hc[:, 1], ALU.add).then_inc(yacc_s, 1)
                        for n in range(2, NS):
                            pool.wait_ge(hc_s, s * NS + n + 1)
                            pool.wait_ge(yacc_s, s * (NS - 1) + n - 1)
                            pool.tensor_tensor(y[:], y[:], hc[:, n % 2], ALU.add).then_inc(yacc_s, 1)

            @block.tensor
            def _(pe):
                pe.wait_ge(weights_in, 16 * n_loads)
                pe.wait_ge(consts, 8)
                with pe.Fori(0, TI) as i:
                    for b in range(B):
                        s = i * B + b
                        for k in range(2):
                            if k == 0:
                                pe.wait_ge(x_in_s, 16 * s + 16)
                            else:
                                pe.wait_ge(nrm[0], s + 1)
                            src = xt if k == 0 else v
                            for kb in range(KB):
                                mm = pe.matmul(bank[:, 0], ones_mean[:], src[:, kb], start=kb == 0, stop=kb == KB - 1)
                            mm.then_inc(mean[k], 1)
                            pe.wait_ge(sqd[k], s + 1)
                            for kb in range(KB):
                                mm = pe.matmul(bank[:, 1], ones_mean[:], sq[:, kb], start=kb == 0, stop=kb == KB - 1)
                            mm.then_inc(var[k], 1)
                        pe.wait_ge(yn_s, KB * (s + 1))
                        for m in range(2 * MB):
                            for kb in range(KB):
                                mm = pe.matmul(bank[:, m], w_in[:, kb, m * P:(m + 1) * P], yn[:, kb], start=kb == 0, stop=kb == KB - 1)
                            mm.then_inc(xz_s, 1)
                        pe.wait_ge(u_s, MB * (s + 1))
                        for m in range(MB):
                            mm = pe.matmul(bank[0:R + 2 * NS, 0], w_xp[:, m, :], u[:, m], start=m == 0, stop=m == MB - 1)
                        mm.then_inc(proj_s, 1)
                        pe.wait_ge(prj_s, s + 1)
                        for m in range(MB):
                            mm = pe.matmul(bank[:, 4 + m], w_dt[:, m * P:(m + 1) * P], prj[0:R, :], start=True, stop=True)
                        mm.then_inc(dtp_s, 1)
                        for n in range(NS):
                            if n >= 2:
                                pe.wait_ge(hc_s, s * NS + n - 1)
                            for c in range(2):
                                k = R + c * NS + n
                                mm = pe.matmul(bank[:, 2 * c + n % 2], ident[0:R + 2 * NS, k:k + 1].to_broadcast([R + 2 * NS, P]), prj[:],
                                               start=True, stop=True)
                            mm.then_inc(bc_s, 1)
                        pe.wait_ge(ym_s, s + 1)
                        for ob in range(KB):
                            for m in range(MB):
                                mm = pe.matmul(bank[:, 4 + ob], w_out[:, m, ob * P:(ob + 1) * P], y[:, m], start=m == 0, stop=m == MB - 1)
                        mm.then_inc(wo_s, 1)
                        pe.wait_ge(y2_s, s + 1)
                        for f in range(FB):
                            for kb in range(KB):
                                mm = pe.matmul(bank[:, f], w_1[:, kb, f * P:(f + 1) * P], y2[:, kb], start=kb == 0, stop=kb == KB - 1)
                            mm.then_inc(up_s, 1)
                        pe.wait_ge(g1_s, FB * (s + 1))
                        for ob in range(KB):
                            for f in range(FB):
                                mm = pe.matmul(bank[:, ob], w_2[:, f, ob * P:(ob + 1) * P], g1[:, f], start=f == 0, stop=f == FB - 1)
                        mm.then_inc(dn_s, 1)

            @block.scalar
            def _(act):
                act.wait_ge(weights_in, 16 * n_loads)
                act.wait_ge(consts, 8)
                act.activation(a_neg[:], a_log[:], ACT.Exp).then_inc(a_exp, 1)
                act.wait_ge(a_exp, 1)
                act.mul(a_neg[:], a_neg[:], -1.0).then_inc(a_exp, 1)
                act.wait_ge(a_exp, 2)
                with act.Fori(0, TI) as i:
                    for b in range(B):
                        s = i * B + b
                        for k in range(2):
                            act.wait_ge(cent[k], s + 1)
                            if k == 0:
                                act.wait_ge(out_free, s + 1)
                            act.activation(sq[:], xc[:], ACT.Square).then_inc(sqd[k], 1)
                            act.wait_ge(var[k], s + 1)
                            act.activation(lnv[:], bank[:, 1], ACT.Ln, bias=(eps_c if k == 0 else eps_n)[:]).then_inc(lns[k], 1)
                            act.wait_ge(lns[k], s + 1)
                            act.activation(rstd[:], lnv[:], ACT.Exp, scale=-0.5).then_inc(rst[k], 1)
                        act.wait_ge(nrm[1], s + 1)
                        for kb in range(KB):
                            act.activation(yn[:, kb], v[:, kb], ACT.Identity, scale=gamma[:, kb:kb + 1], bias=beta[:, kb:kb + 1]).then_inc(yn_s, 1)
                        act.wait_ge(tail_s, s + 1)
                        for m in range(MB):
                            act.wait_ge(xz_s, 2 * MB * s + m + 1)
                            act.copy(xm[:, b, m, 3:3 + T], bank[:, m]).then_inc(xm_s, 1)
                        for m in range(MB):
                            act.wait_ge(xz_s, 2 * MB * s + MB + m + 1)
                            act.activation(zs[:, m], bank[:, MB + m], ACT.Silu).then_inc(zs_s, 1)
                        for m in range(MB):
                            act.wait_ge(conv_s, 4 * MB * s + 3 * MB + m + 1)
                            act.activation(u[:, m], cx[:, m], ACT.Silu, bias=conv_b[:, m:m + 1]).then_inc(u_s, 1)
                        act.wait_ge(proj_s, s + 1)
                        act.copy(prj[:], bank[0:R + 2 * NS, 0]).then_inc(prj_s, 1)
                        act.wait_ge(dtp_s, s + 1)
                        act.wait_ge(u_s, MB * (s + 1))
                        for m in range(MB):
                            act.activation(ea[:, m], bank[:, 4 + m], ACT.Abs, bias=b_dt[:, m:m + 1]).then_inc(abs_s, 1)
                        act.wait_ge(abs_s, MB * (s + 1))
                        act.activation(ea[:], ea[:], ACT.Exp, scale=-1.0).then_inc(dte_s, 1)
                        act.wait_ge(dte_s, 2 * s + 1)
                        act.activation(ea[:], ea[:], ACT.Ln, bias=one[:]).then_inc(dte_s, 1)
                        act.wait_ge(dt_s, s + 1)
                        for n in range(NS):
                            if n >= 2:
                                act.wait_ge(scan_s, MB * (s * NS + n - 1))
                            for m in range(MB):
                                act.activation(dA[:, n % 2, m], dt[:, m], ACT.Exp, scale=a_neg[:, m, n:n + 1]).then_inc(dA_s, 1)
                        for f in range(FB):
                            act.wait_ge(up_s, FB * s + f + 1)
                            act.activation(g1[:, f], bank[:, f], ACT.Gelu, bias=b_1[:, f:f + 1]).then_inc(g1_s, 1)

            @block.vector
            def _(dve):
                dve.wait_ge(weights_in, 16 * n_loads)
                dve.wait_ge(consts, 8)
                dve.sem_inc(x1_s, 1)
                dve.sem_inc(tail_s, 1)
                with dve.Fori(0, TI) as i:
                    for b in range(B):
                        s = i * B + b
                        for k in range(2):
                            dve.wait_ge(mean[k], s + 1)
                            if k == 0:
                                dve.wait_ge(x_in_s, 16 * s + 16)
                            src = xt if k == 0 else v
                            dve.tensor_tensor(xc[:], src[:], bcast(bank[:, 0], KB), ALU.subtract).then_inc(cent[k], 1)
                            dve.wait_ge(rst[k], s + 1)
                            dve.tensor_tensor(v[:], xc[:], bcast(rstd[:], KB), ALU.mult).then_inc(nrm[k], 1)
                            if k == 0:
                                dve.wait_ge(nrm[0], s + 1)
                        for tap in range(4):
                            for m in range(MB):
                                if tap == 0:
                                    dve.wait_ge(xm_s, MB * s + m + 1)
                                    dve.tensor_scalar(cx[:, m], xm[:, b, m, 0:T], conv_w[:, m, 0:1], None, ALU.mult).then_inc(conv_s, 1)
                                else:
                                    dve.wait_ge(conv_s, 4 * MB * s + (tap - 1) * MB + m + 1)
                                    dve.scalar_tensor_tensor(out=cx[:, m], in0=xm[:, b, m, tap:tap + T], scalar=conv_w[:, m, tap:tap + 1],
                                                             in1=cx[:, m], op0=ALU.mult, op1=ALU.add).then_inc(conv_s, 1)
                        dve.wait_ge(conv_s, 4 * MB * (s + 1))
                        dve.tensor_copy(xm[:, b, :, 0:3], xm[:, b, :, T:T + 3]).then_inc(tail_s, 1)
                        dve.wait_ge(dtp_s, s + 1)
                        dve.wait_ge(u_s, MB * (s + 1))
                        for m in range(MB):
                            dve.wait_ge(abs_s, MB * s + m + 1)
                            dve.tensor_scalar(r_dt[:, m], bank[:, 4 + m], b_dt[:, m:m + 1], 0.0, ALU.add, ALU.max).then_inc(dta_s, 1)
                        dve.wait_ge(dte_s, 2 * s + 2)
                        dve.wait_ge(dta_s, MB * (s + 1))
                        dve.tensor_tensor(dt[:], r_dt[:], ea[:], ALU.add).then_inc(dt_s, 1)
                        dve.wait_ge(dt_s, s + 1)
                        dve.tensor_tensor(dtu[:], dt[:], u[:], ALU.mult).then_inc(dtu_s, 1)
                        dve.wait_ge(dtu_s, s + 1)
                        for n in range(NS):
                            g = s * NS + n
                            dve.wait_ge(bc_s, g + 1)
                            dve.tensor_tensor(dbu[:], dtu[:], bcast(bank[:, n % 2], MB), ALU.mult).then_inc(dbu_s, 1)
                            dve.wait_ge(dbu_s, g + 1)
                            for m in range(MB):
                                dve.wait_ge(dA_s, MB * g + m + 1)
                                dve.tensor_tensor_scan(out=hh[:, n % 2, m], data0=dA[:, n % 2, m], data1=dbu[:, m],
                                                       initial=state[:, b, n, m:m + 1], op0=ALU.mult, op1=ALU.add).then_inc(scan_s, 1)
                            dve.wait_ge(scan_s, MB * (g + 1))
                            dve.tensor_copy(state[:, b, n, :], hh[:, n % 2, :, T - 1]).then_inc(save_s, 1)
                            if n >= 2:
                                dve.wait_ge(yacc_s, s * (NS - 1) + max(n - 2, 1))
                            dve.tensor_tensor(hc[:, n % 2], hh[:, n % 2], bcast(bank[:, 2 + n % 2], MB), ALU.mult).then_inc(hc_s, 1)
                            dve.wait_ge(save_s, g + 1)
                        dve.wait_ge(yacc_s, (NS - 1) * (s + 1))
                        for m in range(MB):
                            dve.scalar_tensor_tensor(out=y[:, m], in0=u[:, m], scalar=d_skip[:, m:m + 1], in1=y[:, m],
                                                     op0=ALU.mult, op1=ALU.add).then_inc(yd_s, 1)
                        dve.wait_ge(yd_s, MB * (s + 1))
                        dve.wait_ge(zs_s, MB * (s + 1))
                        dve.tensor_tensor(y[:], y[:], zs[:], ALU.mult).then_inc(ym_s, 1)
                        dve.wait_ge(wo_s, s + 1)
                        dve.wait_ge(yn_s, KB * (s + 1))
                        dve.tensor_tensor(y2[:], bank[:, 4:4 + KB], yn[:], ALU.add).then_inc(y2_s, 1)
                        dve.wait_ge(dn_s, s + 1)
                        dve.wait_ge(y2_s, s + 1)
                        for ob in range(KB):
                            dve.scalar_tensor_tensor(out=xc[:, ob], in0=bank[:, ob], scalar=b_2[:, ob:ob + 1], in1=y2[:, ob],
                                                     op0=ALU.add, op1=ALU.add).then_inc(y3_s, 1)
                        dve.wait_ge(y3_s, KB * (s + 1))
                        dve.tensor_tensor(xo[:], xc[:], xt[:], ALU.add).then_inc(x1_s, 1)
NB = M // P
HEADS, EXPERTS = 4, 4
HC = HEADS * EXPERTS
TW = HC + HEADS
EDGES = 1048576
EC = EDGES // P
FE = 512
FEB = FE // P
SUB = T // P
KEY_CHUNK = 1024
ROUNDS = 7
SLOTS = 8 * ROUNDS
FAR_CHUNK = EC // 32
NEAR_CHUNK = EC // 4
FAR_COLS = EC // FAR_CHUNK * SLOTS
NEAR_COLS = EC // NEAR_CHUNK * SLOTS
GROUP = 16


class Graph:

    def __init__(self, nc, ctx, name):
        def sb(n, shape, dt=F32):
            return ctx.enter_context(nc.sbuf_tensor(f"{name}_{n}", shape, dt))
        self.h = sb("h", [P, NB, TW])
        self.a_dst = sb("a_dst", [P, NB, HEADS])
        self.top = sb("top", [P, HEADS])
        self.last = sb("last", [P, TW])
        self.count = sb("count", [P, NB])
        self.agg = sb("agg", [P, NB, TW])
        self.gate = sb("gate", [P, NB, EXPERTS])
        self.table = nc.dram_tensor(f"{name}_table", (M, TW), F32, kind="Internal").ap()
        self.dst_table = nc.dram_tensor(f"{name}_dst_table", (M, HEADS), F32, kind="Internal").ap()
        self.tn = nc.dram_tensor(f"{name}_tn", (B, C, L), F32, kind="Internal").ap()


def rows(ap, n=P):
    return ap.rearrange("(o n) -> o n", o=1).to_broadcast([n, ap.shape[0]])


def features_phase(nc, name, w, g, x_in):
    with Phase(nc, name) as ph:
        sb, ps, sem = ph.sb, ph.ps, ph.sem
        w_gat = sb("w_gat", [P, KB, HC])
        att = sb("att", [P, 2, HC])
        ones_mean, eps = sb("ones_mean", [P, P]), sb("eps", [P, 1])
        xt, xc, sq, tn = (sb(n, [P, KB, T]) for n in ("xt", "xc", "sq", "tn"))
        lnv, rstd = sb("lnv", [P, T]), sb("rstd", [P, T])
        prod, part_top = sb("prod", [P, 2, SUB, HC]), sb("part_top", [P, HEADS])
        bank = ps("bank", [P, 3, T])
        weights_in, consts, x_loaded, stored, free = (sem(n) for n in ("weights_in", "consts", "x_loaded", "stored", "free"))
        mean, cent, sqd, var, lns, rst, tn_s = (sem(n) for n in ("mean", "cent", "sqd", "var", "lns", "rst", "tn"))
        hp_s, h_s, prod_s, a_s, top_s, all_top, tabled, last_s = (sem(n) for n in ("hp", "h", "prod", "a", "top", "all_top", "tabled", "last"))

        with nc.Block() as block:
            @block.sync
            def _(sp):
                sp.dma_start(w_gat[:], w["W_gat"].rearrange("(k p) n -> p k n", p=P)).then_inc(weights_in, 16)
                for k, n in enumerate(("att_src", "att_dst")):
                    sp.dma_start(att[:, k], rows(w[n].rearrange("h e -> (h e)"))).then_inc(weights_in, 16)
                sp.sem_inc(free, 1)
                with sp.Fori(0, TI) as i:
                    for b in range(B):
                        s = i * B + b
                        sp.wait_ge(cent, s + 1)
                        sp.dma_start(xt[:], x_in[b].rearrange("(k p) t -> p k t", p=P)[:, :, bass.ds(i * T, T)]).then_inc(x_loaded, 16)
                        sp.wait_ge(tn_s, s + 1)
                        sp.dma_start(g.tn[b].rearrange("(k p) t -> p k t", p=P)[:, :, bass.ds(i * T, T)], tn[:]).then_inc(stored, 16)
                        sp.wait_ge(stored, 16 * s + 16)
                        sp.sem_inc(free, 1)
                sp.wait_ge(a_s, 2 * B * TI + 1)
                sp.wait_ge(h_s, B * TI)
                sp.dma_start(g.table.rearrange("(n p) c -> p n c", p=P), g.h[:]).then_inc(tabled, 16)
                sp.dma_start(g.dst_table.rearrange("(n p) c -> p n c", p=P), g.a_dst[:]).then_inc(tabled, 16)
                sp.wait_ge(tabled, 32)
                sp.dma_start(g.last[:], g.table[M - 1:M, :].to_broadcast([P, TW])).then_inc(last_s, 16)
                sp.wait_ge(last_s, 16)

            @block.gpsimd
            def _(pool):
                pool.memset(ones_mean[:], 1.0 / C).then_inc(consts, 1)
                pool.memset(eps[:], 1e-5).then_inc(consts, 1)
                pool.wait_ge(top_s, 1)
                pool.partition_all_reduce(g.top[:], part_top[:], P, bass.bass_isa.ReduceOp.max).then_inc(all_top, 1)
                pool.wait_ge(all_top, 1)

            @block.tensor
            def _(pe):
                pe.wait_ge(weights_in, 48)
                pe.wait_ge(consts, 2)
                with pe.Fori(0, TI) as i:
                    for b in range(B):
                        s = i * B + b
                        pe.wait_ge(x_loaded, 16 * s + 16)
                        for kb in range(KB):
                            mm = pe.matmul(bank[:, 0], ones_mean[:], xt[:, kb], start=kb == 0, stop=kb == KB - 1)
                        mm.then_inc(mean, 1)
                        pe.wait_ge(sqd, s + 1)
                        for kb in range(KB):
                            mm = pe.matmul(bank[:, 1], ones_mean[:], sq[:, kb], start=kb == 0, stop=kb == KB - 1)
                        mm.then_inc(var, 1)
                        pe.wait_ge(tn_s, s + 1)
                        pe.wait_ge(a_s, 2 * s + 1)
                        for sub in range(SUB):
                            for kb in range(KB):
                                mm = pe.matmul(bank[:, 2, sub * HC:(sub + 1) * HC], tn[:, kb, sub * P:(sub + 1) * P], w_gat[:, kb],
                                               start=kb == 0, stop=kb == KB - 1)
                        mm.then_inc(hp_s, 1)

            @block.scalar
            def _(act):
                act.wait_ge(consts, 2)
                with act.Fori(0, TI) as i:
                    for b in range(B):
                        s = i * B + b
                        act.wait_ge(cent, s + 2)
                        act.activation(sq[:], xc[:], ACT.Square).then_inc(sqd, 1)
                        act.wait_ge(var, s + 1)
                        act.activation(lnv[:], bank[:, 1], ACT.Ln, bias=eps[:]).then_inc(lns, 1)
                        act.wait_ge(lns, s + 1)
                        act.activation(rstd[:], lnv[:], ACT.Exp, scale=-0.5).then_inc(rst, 1)

            @block.vector
            def _(dve):
                dve.wait_ge(weights_in, 48)
                dve.sem_inc(cent, 1)
                dve.sem_inc(a_s, 1)
                with dve.Fori(0, TI) as i:
                    for b in range(B):
                        s = i * B + b
                        blocks = bass.ds(i * SUB + b * (NB // B), SUB)
                        dve.wait_ge(mean, s + 1)
                        dve.wait_ge(x_loaded, 16 * s + 16)
                        dve.tensor_tensor(xc[:], xt[:], bcast(bank[:, 0], KB), ALU.subtract).then_inc(cent, 1)
                        dve.wait_ge(rst, s + 1)
                        dve.wait_ge(free, s + 1)
                        dve.wait_ge(cent, s + 2)
                        dve.tensor_tensor(tn[:], xc[:], bcast(rstd[:], KB), ALU.mult).then_inc(tn_s, 1)
                        dve.wait_ge(hp_s, s + 1)
                        hp = bank[:, 2, 0:SUB * HC].rearrange("p (s c) -> p s c", s=SUB)
                        dve.tensor_copy(g.h[:, blocks, 0:HC], hp).then_inc(h_s, 1)
                        for k in range(2):
                            dve.tensor_tensor(prod[:, k], hp, bcast(att[:, k], SUB), ALU.mult).then_inc(prod_s, 1)
                        dve.wait_ge(prod_s, 2 * s + 2)
                        for k, dst in enumerate((g.h[:, blocks, HC:TW], g.a_dst[:, blocks, :])):
                            dve.tensor_reduce(dst, prod[:, k].rearrange("p s (h e) -> p s h e", h=HEADS), AX.X, ALU.add).then_inc(a_s, 1)
                dve.wait_ge(a_s, 2 * B * TI + 1)
                dve.tensor_reduce(part_top[:], g.h[:, :, HC:TW].rearrange("p n c -> p c n"), AX.X, ALU.max).then_inc(top_s, 1)


def keys_phase(nc, name, edge_index, near_key, far_key):
    src_d = edge_index[0].rearrange("(p n) -> p n", p=P)
    dst_d = edge_index[1].rearrange("(p n) -> p n", p=P)
    n_chunks = EC // KEY_CHUNK
    with Phase(nc, name) as ph:
        sb, sem = ph.sb, ph.sem
        src, dst = sb("src", [P, 2, KEY_CHUNK], I32), sb("dst", [P, 2, KEY_CHUNK], I32)
        packed, src_m, dst_1 = sb("packed", [P, KEY_CHUNK], I32), sb("src_m", [P, KEY_CHUNK]), sb("dst_1", [P, KEY_CHUNK])
        loaded = [sem("loaded0"), sem("loaded1")]
        packed_s, clamped_s, near_s, far_s = (sem(n) for n in ("packed", "clamped", "near", "far"))
        with nc.Block() as block:
            @block.sync
            def _(sp):
                sp.sem_inc(near_s, 2)
                with sp.Fori(0, n_chunks // 2) as i:
                    for k in range(2):
                        c = i * 2 + k
                        sp.wait_ge(near_s, c + 1)
                        sp.dma_start(src[:, k], src_d[:, bass.ds(c * KEY_CHUNK, KEY_CHUNK)]).then_inc(loaded[k], 16)
                        sp.dma_start(dst[:, k], dst_d[:, bass.ds(c * KEY_CHUNK, KEY_CHUNK)]).then_inc(loaded[k], 16)

            @block.vector
            def _(dve):
                dve.sem_inc(far_s, 1)
                with dve.Fori(0, n_chunks // 2) as i:
                    for k in range(2):
                        c = i * 2 + k
                        here = bass.ds(c * KEY_CHUNK, KEY_CHUNK)
                        dve.wait_ge(loaded[k], 32 * i + 32)
                        dve.wait_ge(near_s, c + 2)
                        dve.wait_ge(far_s, c + 1)
                        dve.tensor_scalar(packed[:], dst[:, k], 13, 0x40000000, ALU.logical_shift_left, ALU.bitwise_or).then_inc(packed_s, 1)
                        dve.tensor_scalar(src_m[:], src[:, k], float(M - 1), None, ALU.is_lt).then_inc(packed_s, 1)
                        dve.tensor_scalar(dst_1[:], dst[:, k], 1.0, None, ALU.add).then_inc(packed_s, 1)
                        dve.wait_ge(packed_s, 5 * c + 3)
                        dve.tensor_tensor(packed[:], packed[:], src[:, k], ALU.bitwise_or).then_inc(clamped_s, 1)
                        dve.scalar_tensor_tensor(out=src_m[:], in0=dst[:, k], scalar=float(M), in1=src_m[:],
                                                 op0=ALU.is_lt, op1=ALU.mult).then_inc(packed_s, 1)
                        dve.scalar_tensor_tensor(out=dst_1[:], in0=dst_1[:], scalar=float(M + 1), in1=dst_1[:],
                                                 op0=ALU.is_lt, op1=ALU.mult).then_inc(packed_s, 1)
                        dve.wait_ge(clamped_s, c + 1)
                        dve.wait_ge(packed_s, 5 * c + 5)
                        dve.scalar_tensor_tensor(out=far_key[:, here], in0=src[:, k], scalar=float(M - 1), in1=dst_1[:],
                                                 op0=ALU.is_ge, op1=ALU.mult).then_inc(far_s, 1)
                        dve.tensor_tensor(near_key[:, here], packed[:].bitcast(F32), src_m[:], ALU.mult).then_inc(near_s, 1)


def take_largest(dve, keys, taken, chunk, max_s, cleared_s):
    n = EC // chunk
    for r in range(ROUNDS):
        for c in range(n):
            if r > 0:
                dve.wait_ge(cleared_s, (r - 1) * n + c + 1)
            dve.max(taken[:, c, 8 * r:8 * r + 8], keys[:, c * chunk:(c + 1) * chunk]).then_inc(max_s, 1)
        for c in range(n):
            dve.wait_ge(max_s, r * n + c + 1)
            part = keys[:, c * chunk:(c + 1) * chunk]
            dve.match_replace(part, taken[:, c, 8 * r:8 * r + 8], part, 0.0).then_inc(cleared_s, 1)


def passes(nc, name, n_passes, sems, more, programs):
    with nc.Fori(0, n_passes):
        left = nc.values_load(more[0:1, 0:1], min_val=0, max_val=1)
        nc.all_engine_barrier()
        with nc.If(left != 0):
            for eng, program in programs:
                program(eng)
            nc.all_engine_barrier()
            for s in sems:
                nc.sync.sem_clear(s)
            nc.all_engine_barrier()
        with nc.Else():
            for eng in (nc.tensor, nc.vector, nc.scalar, nc.gpsimd, nc.sync):
                eng.nop()
        nc.all_engine_barrier()


def far_phase(nc, name, g, far_key):
    n_passes = -(-FAR_CHUNK // SLOTS)
    n_groups = FAR_COLS // GROUP
    with Phase(nc, name) as ph:
        sb, ps, sem = ph.sb, ph.ps, ph.sem
        taken = sb("taken", [P, EC // FAR_CHUNK, SLOTS])
        node = sb("node", [P, FAR_COLS], I32)
        field = sb("field", [P, 2, FAR_COLS], I32)
        field_b = sb("field_b", [P, 2, FAR_COLS], BF16)
        iota_i, iota_b = sb("iota_i", [P, P], I32), sb("iota_b", [P, P], BF16)
        lo, hi = sb("lo", [P, 2, GROUP, P], BF16), sb("hi", [P, 2, GROUP, NB], BF16)
        last_slot, any_last, more = sb("last_slot", [P, 1]), sb("any_last", [P, 1]), sb("more", [P, 1], I32)
        bank = ps("bank", [P, NB])
        setup = sem("setup")
        names = ("max", "cleared", "last_slot", "any_last", "more", "node", "field", "field_b", "lo", "hi", "summed", "count")
        max_s, cleared_s, last_s, any_s, more_s, node_s, field_s, fb_s, lo_s, hi_s, sum_s, count_s = in_pass = [sem(n) for n in names]

        with nc.Block() as block:
            @block.gpsimd
            def _(pool):
                pool.iota(iota_i[:], pattern=[[1, P]], base=0, channel_multiplier=0).then_inc(setup, 1)
                pool.memset(more[:], 1).then_inc(setup, 1)
                pool.memset(g.count[:], 0.0).then_inc(setup, 1)

            @block.vector
            def _(dve):
                dve.wait_ge(setup, 3)
                dve.tensor_copy(iota_b[:], iota_i[:]).then_inc(setup, 1)
                dve.wait_ge(setup, 4)

        def vector_program(dve):
            take_largest(dve, far_key, taken, FAR_CHUNK, max_s, cleared_s)
            dve.wait_ge(max_s, ROUNDS * EC // FAR_CHUNK)
            dve.wait_ge(cleared_s, ROUNDS * EC // FAR_CHUNK)
            dve.tensor_reduce(last_slot[:], taken[:, :, SLOTS - 1], AX.X, ALU.max).then_inc(last_s, 1)
            dve.tensor_scalar(node[:], taken[:, :, :].rearrange("p c s -> p (c s)"), -1.0, None, ALU.add).then_inc(node_s, 1)
            dve.wait_ge(node_s, 1)
            dve.tensor_scalar(field[:, 0], node[:], P - 1, None, ALU.bitwise_and).then_inc(field_s, 1)
            dve.tensor_scalar(field[:, 1], node[:], 7, None, ALU.arith_shift_right).then_inc(field_s, 1)
            dve.wait_ge(field_s, 2)
            dve.tensor_copy(field_b[:], field[:]).then_inc(fb_s, 1)
            dve.wait_ge(fb_s, 1)
            dve.sem_inc(sum_s, 2)
            with dve.Fori(0, n_groups // 2) as i:
                for k in range(2):
                    q = i * 2 + k
                    here = bass.ds(q * GROUP, GROUP)
                    dve.wait_ge(sum_s, q + 1)
                    dve.tensor_tensor(lo[:, k], bcast(iota_b[:], GROUP), spread(field_b[:, 0, here], P), ALU.is_equal).then_inc(lo_s, 1)
                    dve.tensor_tensor(hi[:, k], bcast(iota_b[:, 0:NB], GROUP), spread(field_b[:, 1, here], NB), ALU.is_equal).then_inc(hi_s, 1)
            dve.wait_ge(sum_s, n_groups + 3)
            dve.tensor_tensor(g.count[:], g.count[:], bank[:], ALU.add).then_inc(count_s, 1)
            dve.wait_ge(any_s, 1)
            dve.tensor_scalar(more[:], any_last[:], 0.0, None, ALU.is_gt).then_inc(more_s, 1)
            dve.wait_ge(more_s, 1)

        def tensor_program(pe):
            pe.matmul(bank[:], zero_b[:], zero_b[:, 0:NB], start=True, stop=False)
            with pe.Fori(0, n_groups // 2) as i:
                for k in range(2):
                    q = i * 2 + k
                    pe.wait_ge(lo_s, q + 1)
                    pe.wait_ge(hi_s, q + 1)
                    for c in range(GROUP):
                        mm = pe.matmul(bank[:], lo[:, k, c], hi[:, k, c], start=False, stop=False)
                    mm.then_inc(sum_s, 1)
            pe.matmul(bank[:], zero_b[:], zero_b[:, 0:NB], start=False, stop=True).then_inc(sum_s, 1)

        zero_b = sb("zero_b", [P, P], BF16)
        nc.vector.memset(zero_b[:], 0.0)
        nc.all_engine_barrier()

        def pool_program(pool):
            pool.wait_ge(last_s, 1)
            pool.partition_all_reduce(any_last[:], last_slot[:], P, bass.bass_isa.ReduceOp.max).then_inc(any_s, 1)

        passes(nc, name, n_passes, in_pass, more,
               [(nc.vector, vector_program), (nc.tensor, tensor_program), (nc.gpsimd, pool_program)])


def spread(ap, n):
    return ap.rearrange("p (g o) -> p g o", o=1).to_broadcast([ap.shape[0], ap.shape[1], n])


def near_phase(nc, name, g, near_key):
    n_passes = -(-NEAR_CHUNK // SLOTS)
    splits = [(0, 25), (25, 50), (50, NB)]
    with Phase(nc, name) as ph:
        sb, ps, sem = ph.sb, ph.ps, ph.sem
        taken = sb("taken", [P, EC // NEAR_CHUNK, SLOTS])
        keys = taken[:, :, :].rearrange("p c s -> p (c s)")
        bits = keys.bitcast(I32)
        src_i, dst_i = sb("src_i", [P, NEAR_COLS], I32), sb("dst_i", [P, NEAR_COLS], I32)
        lo_i, hi_i = sb("lo_i", [P, NEAR_COLS], I32), sb("hi_i", [P, NEAR_COLS], I32)
        lo_f, hi_f, there = sb("lo_f", [P, NEAR_COLS]), sb("hi_f", [P, NEAR_COLS]), sb("there", [P, NEAR_COLS])
        rows_g, dst_g = sb("rows_g", [P, NEAR_COLS, TW]), sb("dst_g", [P, NEAR_COLS, HEADS])
        logit, bound = sb("logit", [P, NEAR_COLS, HEADS]), sb("bound", [P, NEAR_COLS, HEADS])
        val = sb("val", [P, NEAR_COLS, TW])
        iota_i, iota_f = sb("iota_i", [P, P], I32), sb("iota_f", [P, P])
        lo, rhs = sb("lo", [P, 2, P]), sb("rhs", [P, 2, NB, TW])
        zero = sb("zero", [P, 512])
        last_slot, any_last, more = sb("last_slot", [P, 1]), sb("any_last", [P, 1]), sb("more", [P, 1], I32)
        bank = ps("bank", [P, 3, 512])
        setup = sem("setup")
        names = ("max", "cleared", "last_slot", "any_last", "more", "field", "field_f", "hi_m", "rows", "dsts",
                 "logit", "lrelu", "diff", "weight", "val", "lo", "rhs", "summed", "agg")
        (max_s, cleared_s, last_s, any_s, more_s, field_s, ff_s, him_s, rows_s, dsts_s, logit_s, lrelu_s, diff_s, weight_s,
         val_s, lo_s, rhs_s, sum_s, agg_s) = in_pass = [sem(n) for n in names]

        with nc.Block() as block:
            @block.gpsimd
            def _(pool):
                pool.iota(iota_i[:], pattern=[[1, P]], base=0, channel_multiplier=0).then_inc(setup, 1)
                pool.memset(more[:], 1).then_inc(setup, 1)
                pool.memset(g.agg[:], 0.0).then_inc(setup, 1)
                pool.memset(zero[:], 0.0).then_inc(setup, 1)

            @block.vector
            def _(dve):
                dve.wait_ge(setup, 4)
                dve.tensor_copy(iota_f[:], iota_i[:]).then_inc(setup, 1)
                dve.wait_ge(setup, 5)

        def vector_program(dve):
            take_largest(dve, near_key, taken, NEAR_CHUNK, max_s, cleared_s)
            dve.wait_ge(max_s, ROUNDS * EC // NEAR_CHUNK)
            dve.wait_ge(cleared_s, ROUNDS * EC // NEAR_CHUNK)
            dve.tensor_scalar(src_i[:], bits, M - 1, None, ALU.bitwise_and).then_inc(field_s, 1)
            dve.tensor_scalar(dst_i[:], bits, 13, M - 1, ALU.logical_shift_right, ALU.bitwise_and).then_inc(field_s, 1)
            dve.tensor_scalar(lo_i[:], bits, 13, P - 1, ALU.logical_shift_right, ALU.bitwise_and).then_inc(field_s, 1)
            dve.tensor_scalar(hi_i[:], bits, 20, NB - 1, ALU.logical_shift_right, ALU.bitwise_and).then_inc(field_s, 1)
            dve.tensor_reduce(last_slot[:], taken[:, :, SLOTS - 1], AX.X, ALU.max).then_inc(last_s, 1)
            dve.wait_ge(field_s, 4)
            dve.tensor_copy(lo_f[:], lo_i[:]).then_inc(ff_s, 1)
            dve.tensor_scalar(hi_f[:], hi_i[:], 1.0, None, ALU.add).then_inc(ff_s, 1)
            dve.wait_ge(ff_s, 2)
            dve.scalar_tensor_tensor(out=hi_f[:], in0=keys, scalar=0.0, in1=hi_f[:], op0=ALU.is_gt, op1=ALU.mult).then_inc(him_s, 1)
            dve.wait_ge(him_s, 1)
            dve.tensor_scalar(hi_f[:], hi_f[:], -1.0, None, ALU.add).then_inc(him_s, 1)
            dve.wait_ge(rows_s, 16 * NEAR_COLS)
            dve.wait_ge(dsts_s, 16 * NEAR_COLS)
            dve.tensor_tensor(logit[:], rows_g[:, :, HC:TW], dst_g[:], ALU.add).then_inc(logit_s, 1)
            dve.tensor_tensor(bound[:], dst_g[:], bcast(g.top[:], NEAR_COLS), ALU.add).then_inc(logit_s, 1)
            dve.wait_ge(logit_s, 2)
            for a in (logit, bound):
                dve.scalar_tensor_tensor(out=a[:], in0=a[:], scalar=0.2, in1=a[:], op0=ALU.mult, op1=ALU.max).then_inc(lrelu_s, 1)
            dve.wait_ge(lrelu_s, 2)
            dve.tensor_tensor(logit[:], logit[:], bound[:], ALU.subtract).then_inc(diff_s, 1)
            dve.wait_ge(weight_s, 1)
            for h in range(HEADS):
                dve.tensor_tensor(val[:, :, EXPERTS * h:EXPERTS * (h + 1)], rows_g[:, :, EXPERTS * h:EXPERTS * (h + 1)],
                                  val[:, :, HC + h:HC + h + 1].to_broadcast([P, NEAR_COLS, EXPERTS]), ALU.mult).then_inc(val_s, 1)
            dve.wait_ge(val_s, HEADS)
            dve.wait_ge(him_s, 2)
            dve.sem_inc(sum_s, 2)
            with dve.Fori(0, NEAR_COLS // 2) as i:
                for k in range(2):
                    q = i * 2 + k
                    dve.wait_ge(sum_s, q + 1)
                    dve.tensor_scalar(lo[:, k], iota_f[:], lo_f[:, bass.ds(q, 1)], None, ALU.is_equal).then_inc(lo_s, 1)
                    dve.scalar_tensor_tensor(out=rhs[:, k], in0=spread(iota_f[:, 0:NB], TW), scalar=hi_f[:, bass.ds(q, 1)],
                                             in1=val[:, bass.ds(q, 1), :].to_broadcast([P, NB, TW]),
                                             op0=ALU.is_equal, op1=ALU.mult).then_inc(rhs_s, 1)
            dve.wait_ge(sum_s, NEAR_COLS + 3)
            for k, (a, b) in enumerate(splits):
                dve.tensor_tensor(g.agg[:, a:b, :], g.agg[:, a:b, :], bank[:, k, 0:(b - a) * TW].rearrange("p (n c) -> p n c", c=TW),
                                  ALU.add).then_inc(agg_s, 1)
            dve.wait_ge(any_s, 1)
            dve.tensor_scalar(more[:], any_last[:], 0.0, None, ALU.is_gt).then_inc(more_s, 1)
            dve.wait_ge(more_s, 1)

        def tensor_program(pe):
            for n, (a, b) in enumerate(splits):
                pe.matmul(bank[:, n, 0:(b - a) * TW], zero[:, 0:P], zero[:, 0:(b - a) * TW], start=True, stop=False)
            with pe.Fori(0, NEAR_COLS // 2) as i:
                for k in range(2):
                    q = i * 2 + k
                    pe.wait_ge(lo_s, q + 1)
                    pe.wait_ge(rhs_s, q + 1)
                    for n, (a, b) in enumerate(splits):
                        mm = pe.matmul(bank[:, n, 0:(b - a) * TW], lo[:, k], rhs[:, k, a:b].rearrange("p n c -> p (n c)"),
                                       start=False, stop=False)
                    mm.then_inc(sum_s, 1)
            for n, (a, b) in enumerate(splits):
                mm = pe.matmul(bank[:, n, 0:(b - a) * TW], zero[:, 0:P], zero[:, 0:(b - a) * TW], start=False, stop=True)
            mm.then_inc(sum_s, 1)

        def scalar_program(act):
            act.wait_ge(diff_s, 1)
            act.activation(val[:, :, HC:TW], logit[:], ACT.Exp).then_inc(weight_s, 1)

        def pool_program(pool):
            pool.wait_ge(field_s, 4)
            pool.wait_ge(last_s, 1)
            pool.partition_all_reduce(any_last[:], last_slot[:], P, bass.bass_isa.ReduceOp.max).then_inc(any_s, 1)
            for q in range(NEAR_COLS):
                pool.indirect_dma_start(out=rows_g[:, q], out_offset=None, in_=g.table,
                                        in_offset=bass.IndirectOffsetOnAxis(ap=src_i[:, q:q + 1].bitcast(U32), axis=0)).then_inc(rows_s, 16)
                pool.indirect_dma_start(out=dst_g[:, q], out_offset=None, in_=g.dst_table,
                                        in_offset=bass.IndirectOffsetOnAxis(ap=dst_i[:, q:q + 1].bitcast(U32), axis=0)).then_inc(dsts_s, 16)
            pool.wait_ge(rows_s, 16 * NEAR_COLS)
            pool.wait_ge(dsts_s, 16 * NEAR_COLS)

        passes(nc, name, n_passes, in_pass, more,
               [(nc.vector, vector_program), (nc.tensor, tensor_program), (nc.scalar, scalar_program), (nc.gpsimd, pool_program)])


def gate_phase(nc, name, w, g):
    with Phase(nc, name) as ph:
        sb, sem = ph.sb, ph.sem
        b_gat, ln_g, ln_b = sb("b_gat", [P, HC]), sb("ln_g", [P, HC]), sb("ln_b", [P, HC])
        loop, far, bound = (sb(n, [P, NB, HEADS]) for n in ("loop", "far", "bound"))
        den, s4, e4, t4, rank = (sb(n, [P, NB, HEADS]) for n in ("den", "s4", "e4", "t4", "rank"))
        tmp, a = sb("tmp", [P, NB, HC]), sb("a", [P, NB, HC])
        mu, var, m1 = sb("mu", [P, NB]), sb("var", [P, NB]), sb("m1", [P, NB])
        eps = sb("eps", [P, 1])
        loaded, consts, step, exp_in, exp_out, var_in, lnv_s, rstd_s, sh_in, sh_out = (
            sem(n) for n in ("loaded", "consts", "step", "exp_in", "exp_out", "var_in", "lnv", "rstd", "sh_in", "sh_out"))
        h = g.h[:, :, 0:HC]

        def col(t):
            return t.rearrange("p (n o) -> p n o", o=1)

        def heads(t):
            return t

        with nc.Block() as block:
            @block.sync
            def _(sp):
                for t, n in ((b_gat, "b_gat"), (ln_g, "ln_gamma"), (ln_b, "ln_beta")):
                    sp.dma_start(t[:], rows(w[n])).then_inc(loaded, 16)

            @block.gpsimd
            def _(pool):
                pool.memset(eps[:], 1e-5).then_inc(consts, 1)

            @block.scalar
            def _(act):
                act.wait_ge(consts, 1)
                act.wait_ge(exp_in, 1)
                act.activation(loop[:], loop[:], ACT.Exp).then_inc(exp_out, 1)
                act.activation(far[:], far[:], ACT.Exp).then_inc(exp_out, 1)
                act.wait_ge(var_in, 1)
                act.activation(var[:], var[:], ACT.Ln, bias=eps[:], scale=1.0 / HC).then_inc(lnv_s, 1)
                act.wait_ge(lnv_s, 1)
                act.activation(var[:], var[:], ACT.Exp, scale=-0.5).then_inc(rstd_s, 1)
                act.wait_ge(sh_in, 1)
                act.activation(e4[:], e4[:], ACT.Exp).then_inc(sh_out, 1)

            @block.vector
            def _(dve):
                done = [0]

                def then(ins, s=step):
                    ins.then_inc(step, 1)
                    done[0] += 1
                    dve.wait_ge(step, done[0])

                dve.wait_ge(loaded, 48)
                then(dve.tensor_tensor(loop[:], g.h[:, :, HC:TW], g.a_dst[:], ALU.add))
                then(dve.tensor_tensor(far[:], g.a_dst[:], bcast(g.last[:, HC:TW], NB), ALU.add))
                then(dve.tensor_tensor(bound[:], g.a_dst[:], bcast(g.top[:], NB), ALU.add))
                for t in (loop, far, bound):
                    then(dve.scalar_tensor_tensor(out=t[:], in0=t[:], scalar=0.2, in1=t[:], op0=ALU.mult, op1=ALU.max))
                then(dve.tensor_tensor(loop[:], loop[:], bound[:], ALU.subtract))
                then(dve.tensor_tensor(far[:], far[:], bound[:], ALU.subtract))
                dve.sem_inc(exp_in, 1)
                dve.wait_ge(exp_out, 2)
                then(dve.tensor_tensor(far[:], far[:], col(g.count[:]).to_broadcast([P, NB, HEADS]), ALU.mult))
                then(dve.tensor_tensor(den[:], g.agg[:, :, HC:TW], loop[:], ALU.add))
                then(dve.scalar_tensor_tensor(out=den[:], in0=den[:], scalar=1e-16, in1=far[:], op0=ALU.add, op1=ALU.add))
                then(dve.reciprocal(den[:], den[:]))
                for k in range(HEADS):
                    e = slice(EXPERTS * k, EXPERTS * (k + 1))
                    wide = [P, NB, EXPERTS]
                    then(dve.tensor_tensor(tmp[:, :, e], h[:, :, e], loop[:, :, k:k + 1].to_broadcast(wide), ALU.mult))
                    then(dve.tensor_tensor(a[:, :, e], g.agg[:, :, e], tmp[:, :, e], ALU.add))
                    then(dve.tensor_tensor(tmp[:, :, e], bcast(g.last[:, e], NB), far[:, :, k:k + 1].to_broadcast(wide), ALU.mult))
                    then(dve.tensor_tensor(a[:, :, e], a[:, :, e], tmp[:, :, e], ALU.add))
                    then(dve.tensor_tensor(a[:, :, e], a[:, :, e], den[:, :, k:k + 1].to_broadcast(wide), ALU.mult))
                then(dve.tensor_tensor(a[:], a[:], bcast(b_gat[:], NB), ALU.add))
                then(dve.tensor_reduce(mu[:], a[:], AX.X, ALU.add))
                then(dve.tensor_scalar(mu[:], mu[:], 1.0 / HC, None, ALU.mult))
                then(dve.tensor_tensor(a[:], a[:], col(mu[:]).to_broadcast([P, NB, HC]), ALU.subtract))
                then(dve.tensor_tensor(tmp[:], a[:], a[:], ALU.mult))
                then(dve.tensor_reduce(var[:], tmp[:], AX.X, ALU.add))
                dve.sem_inc(var_in, 1)
                dve.wait_ge(rstd_s, 1)
                then(dve.tensor_tensor(a[:], a[:], col(var[:]).to_broadcast([P, NB, HC]), ALU.mult))
                then(dve.tensor_tensor(a[:], a[:], bcast(ln_g[:], NB), ALU.mult))
                then(dve.tensor_tensor(a[:], a[:], bcast(ln_b[:], NB), ALU.add))
                then(dve.tensor_reduce(s4[:], a[:, :, :].rearrange("p n (h e) -> p n e h", h=HEADS), AX.X, ALU.add))
                then(dve.tensor_scalar(s4[:], s4[:], 1.0 / HEADS, None, ALU.mult))
                then(dve.memset(rank[:], 0.0))
                for j in range(EXPERTS):
                    for k in range(EXPERTS):
                        if j != k:
                            op = ALU.is_ge if j < k else ALU.is_gt
                            then(dve.tensor_tensor(m1[:], s4[:, :, j], s4[:, :, k], op))
                            then(dve.tensor_tensor(rank[:, :, k], rank[:, :, k], m1[:], ALU.add))
                then(dve.tensor_reduce(m1[:], s4[:], AX.X, ALU.max))
                then(dve.tensor_tensor(e4[:], s4[:], col(m1[:]).to_broadcast([P, NB, EXPERTS]), ALU.subtract))
                dve.sem_inc(sh_in, 1)
                dve.wait_ge(sh_out, 1)
                then(dve.scalar_tensor_tensor(out=e4[:], in0=rank[:], scalar=1.5, in1=e4[:], op0=ALU.is_lt, op1=ALU.mult))
                then(dve.tensor_reduce(m1[:], e4[:], AX.X, ALU.add))
                then(dve.reciprocal(m1[:], m1[:]))
                then(dve.tensor_tensor(g.gate[:], e4[:], col(m1[:]).to_broadcast([P, NB, EXPERTS]), ALU.mult))


def experts_phase(nc, name, w, g, x_in, x_out):
    with Phase(nc, name) as ph:
        sb, ps, sem = ph.sb, ph.ps, ph.sem
        w_1, w_2 = sb("w_1", [P, EXPERTS, KB, FE]), sb("w_2", [P, EXPERTS, FEB, C])
        b_1, b_2 = sb("b_1", [P, EXPERTS, FEB]), sb("b_2", [1, EXPERTS, C])
        ident, ones = sb("ident", [P, P]), sb("ones", [1, P])
        tn, xt, xo = (sb(n, [P, 2, KB, T]) for n in ("tn", "xt", "xo"))
        gt = sb("gt", [P, 2, SUB, EXPERTS])
        hid = sb("hid", [P, 2, FEB, T])
        acc = sb("acc", [P, SUB, C])
        up = ps("up", [P, FEB, T])
        down = ps("down", [P, 2, 2, C])
        turned = ps("turned", [P, KB, T])
        weights_in, consts = sem("weights_in"), sem("consts")
        in_s, stored = [sem("in0"), sem("in1")], [sem("stored0"), sem("stored1")]
        free, gt_s, up_s, hid_s, down_s, acc_s, turn_s, out_s = (
            sem(n) for n in ("free", "gt", "up", "hid", "down", "acc", "turn", "out"))
        E_ = EXPERTS
        with nc.Block() as block:
            @block.sync
            def _(sp):
                for e in range(E_):
                    sp.dma_start(w_1[:, e], w["W1"][e].rearrange("(k p) n -> p k n", p=P)).then_inc(weights_in, 16)
                    sp.dma_start(w_2[:, e], w["W2"][e].rearrange("(k p) n -> p k n", p=P)).then_inc(weights_in, 16)
                with nc.allow_non_contiguous_dma(reason="short vectors"):
                    sp.dma_start(b_1[:], w["b1"].rearrange("e (k p) -> p e k", p=P)).then_inc(weights_in, 16)
                sp.dma_start(b_2[:], w["b2"].rearrange("(o e) n -> o e n", o=1)).then_inc(weights_in, 16)
                with sp.Fori(0, TI) as i:
                    for b in range(B):
                        s = i * B + b
                        at = bass.ds(i * T, T)
                        sp.wait_ge(out_s, s + 1)
                        sp.dma_start(tn[:, b], g.tn[b].rearrange("(k p) t -> p k t", p=P)[:, :, at]).then_inc(in_s[b], 16)
                        sp.dma_start(xt[:, b], x_in[b].rearrange("(k p) t -> p k t", p=P)[:, :, at]).then_inc(in_s[b], 16)

            @block.gpsimd
            def _(pool):
                pool.memset(ident[:], 0.0).then_inc(consts, 1)
                pool.memset(ones[:], 1.0).then_inc(consts, 1)
                pool.wait_ge(consts, 2)
                pool.affine_select(out=ident[:], in_=ident[:], compare_op=ALU.not_equal, fill=1.0, base=0,
                                   pattern=[[-1, P]], channel_multiplier=1).then_inc(consts, 1)
                with pool.Fori(0, TI) as i:
                    for b in range(B):
                        s = i * B + b
                        pool.wait_ge(out_s, s + 3)
                        pool.dma_start(x_out[b].rearrange("(k p) t -> p k t", p=P)[:, :, bass.ds(i * T, T)], xo[:, b]).then_inc(stored[b], 16)
                        pool.wait_ge(stored[b], 16 * i + 16)
                        pool.sem_inc(free, 1)

            @block.tensor
            def _(pe):
                pe.wait_ge(weights_in, 16 * (2 * E_ + 2))
                pe.wait_ge(consts, 3)
                with pe.Fori(0, TI) as i:
                    for b in range(B):
                        s = i * B + b
                        pe.wait_ge(in_s[b], 32 * i + 32)
                        for e in range(E_ + 1):
                            if e < E_:
                                for f in range(FEB):
                                    pe.wait_ge(hid_s, FEB * (E_ * s + e - 1) + f + 1 + FEB)
                                    for kb in range(KB):
                                        mm = pe.matmul(up[:, f], w_1[:, e, kb, f * P:(f + 1) * P], tn[:, b, kb], start=kb == 0, stop=kb == KB - 1)
                                    mm.then_inc(up_s, 1)
                            if e > 0:
                                pe.wait_ge(hid_s, FEB * (E_ * s + e) + FEB)
                                for sub in range(SUB):
                                    n = SUB * (E_ * s + e - 1) + sub
                                    pe.wait_ge(acc_s, n - 1 + SUB)
                                    half = down[:, sub % 2, 0]
                                    for f in range(FEB):
                                        pe.matmul(half, hid[:, (e - 1) % 2, f, sub * P:(sub + 1) * P], w_2[:, e - 1, f], start=f == 0, stop=False)
                                    mm = pe.matmul(half, ones[:], b_2[:, e - 1], start=False, stop=True)
                                    mm.then_inc(down_s, 1)
                        pe.wait_ge(acc_s, SUB * E_ * (s + 1) + SUB)
                        pe.wait_ge(out_s, s + 2)
                        for sub in range(SUB):
                            for kb in range(KB):
                                mm = pe.transpose(turned[:, kb, sub * P:(sub + 1) * P], acc[:, sub, kb * P:(kb + 1) * P], ident[:])
                        mm.then_inc(turn_s, 1)

            @block.scalar
            def _(act):
                act.wait_ge(weights_in, 16 * (2 * E_ + 2))
                act.sem_inc(hid_s, FEB)
                with act.Fori(0, TI) as i:
                    for b in range(B):
                        s = i * B + b
                        for e in range(E_):
                            act.wait_ge(down_s, SUB * (E_ * s + e - 2) + SUB + 2 * SUB)
                            for f in range(FEB):
                                act.wait_ge(up_s, FEB * (E_ * s + e) + f + 1)
                                act.activation(hid[:, e % 2, f], up[:, f], ACT.Gelu, bias=b_1[:, e, f:f + 1]).then_inc(hid_s, 1)

            @block.vector
            def _(dve):
                dve.sem_inc(out_s, 2)
                dve.sem_inc(acc_s, SUB)
                dve.sem_inc(free, 2)
                dve.sem_inc(down_s, 2 * SUB)
                with dve.Fori(0, TI) as i:
                    for b in range(B):
                        s = i * B + b
                        dve.tensor_copy(gt[:, b], g.gate[:, bass.ds(i * SUB + b * (NB // B), SUB), :]).then_inc(gt_s, 1)
                        dve.wait_ge(gt_s, s + 1)
                        for e in range(E_):
                            for sub in range(SUB):
                                n = SUB * (E_ * s + e) + sub
                                dve.wait_ge(down_s, n + 1 + 2 * SUB)
                                half = down[:, sub % 2, 0]
                                if e == 0:
                                    dve.tensor_scalar(acc[:, sub], half, gt[:, b, sub, e:e + 1], None, ALU.mult).then_inc(acc_s, 1)
                                else:
                                    dve.wait_ge(acc_s, n - SUB + 1 + SUB)
                                    dve.scalar_tensor_tensor(out=acc[:, sub], in0=half, scalar=gt[:, b, sub, e:e + 1], in1=acc[:, sub],
                                                             op0=ALU.mult, op1=ALU.add).then_inc(acc_s, 1)
                        dve.wait_ge(turn_s, s + 1)
                        dve.wait_ge(in_s[b], 32 * i + 32)
                        dve.wait_ge(free, s + 1)
                        dve.tensor_tensor(xo[:, b], turned[:], xt[:, b], ALU.add).then_inc(out_s, 1)
TILE_OUT, TILE_IN, KERNEL = 4, 6, 3
NT = HW // TILE_OUT
TP = TILE_IN * TILE_IN
HALF_T = NT // 2
HALF_R = HW // 2
N_T = HALF_T * NT
ROWS = HALF_R + 2
WIDE = HW + 2


def kernel_points_phase(nc, name, w, points):
    with Phase(nc, name) as ph:
        sb, sem = ph.sb, ph.sem
        k9 = sb("k9", [P, KB, KERNEL, KERNEL, C])
        half = sb("half", [P, TILE_IN, KERNEL, C])
        mask = sb("mask", [P, 2, TILE_IN, C])
        s0, s1 = sb("s0", [P, TILE_IN, C]), sb("s1", [P, TILE_IN, C])
        loaded, mask_in, step, masked = sem("loaded"), [sem("mask_in0"), sem("mask_in1")], sem("step"), sem("masked")
        mask_d = w["mask"].rearrange("(k p) t u o -> p k t u o", p=P)
        k_d = w["weight"].rearrange("(k p) i j o -> p k (i j o)", p=P)
        chunks = [(kb, t) for kb in range(KB) for t in range(TILE_IN)]

        with nc.Block() as block:
            @block.sync
            def _(sp):
                for kb in range(KB):
                    sp.dma_start(k9[:, kb].rearrange("p i j o -> p (i j o)"), k_d[:, kb]).then_inc(loaded, 16)
                for n, (kb, t) in enumerate(chunks):
                    if n >= 2:
                        sp.wait_ge(masked, n - 1)
                    sp.dma_start(mask[:, n % 2], mask_d[:, kb, t]).then_inc(mask_in[n % 2], 16)

            @block.vector
            def _(dve):
                done = [0]

                def then(ins):
                    ins.then_inc(step, 1)
                    done[0] += 1
                    dve.wait_ge(step, done[0])

                def expand(w0, w1, w2, out, n):
                    a, b = s0[:, 0:n], s1[:, 0:n]
                    then(dve.tensor_scalar(out(0), w0, 0.25, None, ALU.mult))
                    then(dve.tensor_copy(out(5), w2))
                    then(dve.tensor_tensor(a, w0, w2, ALU.add))
                    for k, op in ((1, ALU.add), (2, ALU.subtract)):
                        then(dve.tensor_tensor(b, a, w1, op))
                        then(dve.tensor_scalar(out(k), b, -1.0 / 6, None, ALU.mult))
                    then(dve.scalar_tensor_tensor(out=a, in0=w0, scalar=0.25, in1=w2, op0=ALU.mult, op1=ALU.add))
                    for k, f in ((3, 0.5), (4, -0.5)):
                        then(dve.scalar_tensor_tensor(out=b, in0=w1, scalar=f, in1=a, op0=ALU.mult, op1=ALU.add))
                        then(dve.tensor_scalar(out(k), b, 1.0 / 6, None, ALU.mult))

                dve.wait_ge(loaded, 16 * KB)
                for kb in range(KB):
                    expand(k9[:, kb, 0], k9[:, kb, 1], k9[:, kb, 2], lambda t: half[:, t], KERNEL)
                    expand(half[:, :, 0], half[:, :, 1], half[:, :, 2], lambda u: points[:, kb, u], TILE_IN)
                    for t in range(TILE_IN):
                        n = kb * TILE_IN + t
                        dve.wait_ge(mask_in[n % 2], 16 * (n // 2) + 16)
                        then(dve.tensor_scalar(mask[:, n % 2], mask[:, n % 2], -1.0, 1.0, ALU.mult, ALU.add))
                        dve.tensor_tensor(points[:, kb, :, t], points[:, kb, :, t], mask[:, n % 2], ALU.mult).then_inc(masked, 1)
                dve.wait_ge(masked, KB * TILE_IN)


def winograd_phase(nc, name, w, points, x_in, x_out):
    with Phase(nc, name) as ph:
        sb, ps, sem = ph.sb, ph.ps, ph.sem
        ones_mean, eps, bias = sb("ones_mean", [P, P]), sb("eps", [P, 1]), sb("bias", [P, KB])
        v = sb("v", [P, KB, ROWS, WIDE])
        xt, xc, sq = (sb(n, [P, KB, T]) for n in ("xt", "xc", "sq"))
        lnv, rstd = sb("lnv", [P, T]), sb("rstd", [P, T])
        r = sb("r", [P, TILE_IN, HALF_T, WIDE])
        pts = sb("pts", [P, KB, TILE_IN, TILE_IN, N_T])
        prod = sb("prod", [P, TILE_IN, TILE_IN, N_T])
        s1 = sb("s1", [P, TILE_OUT, TILE_IN, N_T])
        y = sb("y", [P, HALF_R, HW])
        res = sb("res", [P, HALF_R * HW])
        tmp = [sb(f"tmp{k}", [P, TILE_IN * N_T]) for k in range(2)]
        bank = ps("bank", [P, 8, T])
        G4 = 4
        n_g = TP // G4
        consts, weights_in, x_loaded, res_in, stored, free = (sem(n) for n in ("consts", "weights_in", "x_loaded", "res_in", "stored", "free"))
        mean, cent, sqd, var, lns, rst, v_s, clean = (sem(n) for n in ("mean", "cent", "sqd", "var", "lns", "rst", "v", "clean"))
        rows_s, pts_s, prod_s, copied, out_s, step = (sem(n) for n in ("rows", "pts", "prod", "copied", "out", "step"))
        pieces = [[(0, 8), (8, 8), (16, 8), (24, 8), (32, 1)], [(31, 1), (32, 8), (40, 8), (48, 8), (56, 8)]]
        NP_ = len(pieces[0])
        n_steps = 2 * B
        x_px = x_in.rearrange("b (k p) t -> b p k t", p=P)
        o_px = x_out.rearrange("b (k p) t -> b p k t", p=P)

        with nc.Block() as block:
            @block.sync
            def _(sp):
                with nc.allow_non_contiguous_dma(reason="a short vector"):
                    sp.dma_start(bias[:], w["bias"].rearrange("(k p) -> p k", p=P)).then_inc(weights_in, 16)
                for s in range(n_steps):
                    b, h = s // 2, s % 2
                    for k, (row, n) in enumerate(pieces[h]):
                        q = s * NP_ + k
                        if q:
                            sp.wait_ge(cent, q)
                        sp.dma_start(xt[:, :, 0:n * HW], x_px[b, :, :, row * HW:(row + n) * HW]).then_inc(x_loaded, 16)
                    for ob in range(KB):
                        if s or ob:
                            sp.wait_ge(out_s, KB * s + ob)
                        sp.dma_start(res[:], x_px[b, :, ob, h * HALF_R * HW:(h + 1) * HALF_R * HW]).then_inc(res_in, 16)

            @block.gpsimd
            def _(pool):
                pool.memset(ones_mean[:], 1.0 / C).then_inc(consts, 1)
                pool.memset(eps[:], 1e-6).then_inc(consts, 1)
                pool.memset(v[:], 0.0).then_inc(consts, 1)
                for s in range(n_steps):
                    b, h = s // 2, s % 2
                    for ob in range(KB):
                        pool.wait_ge(out_s, KB * s + ob + 1)
                        pool.dma_start(o_px[b, :, ob, h * HALF_R * HW:(h + 1) * HALF_R * HW],
                                       y[:].rearrange("p r c -> p (r c)")).then_inc(stored, 16)
                pool.wait_ge(stored, 16 * KB * n_steps)

            @block.tensor
            def _(pe):
                pe.wait_ge(consts, 3)
                for s in range(n_steps):
                    for k, (row, n) in enumerate(pieces[s % 2]):
                        q = s * NP_ + k
                        w_ = n * HW
                        pe.wait_ge(x_loaded, 16 * q + 16)
                        for kb in range(KB):
                            mm = pe.matmul(bank[:, 6, 0:w_], ones_mean[:], xt[:, kb, 0:w_], start=kb == 0, stop=kb == KB - 1)
                        mm.then_inc(mean, 1)
                        pe.wait_ge(sqd, q + 1)
                        for kb in range(KB):
                            mm = pe.matmul(bank[:, 7, 0:w_], ones_mean[:], sq[:, kb, 0:w_], start=kb == 0, stop=kb == KB - 1)
                        mm.then_inc(var, 1)
                    pe.wait_ge(pts_s, 12 * KB * (s + 1))
                    for ob in range(KB):
                        for gr in range(n_g):
                            c = (s * KB + ob) * n_g + gr
                            if c >= 6:
                                pe.wait_ge(copied, c - 5)
                            for j in range(G4):
                                u, t = divmod(gr * G4 + j, TILE_IN)
                                for kb in range(KB):
                                    mm = pe.matmul(bank[:, c % 6, j * N_T:(j + 1) * N_T], points[:, kb, u, t, ob * P:(ob + 1) * P],
                                                   pts[:, kb, u, t], start=kb == 0, stop=kb == KB - 1)
                            mm.then_inc(prod_s, 1)

            @block.scalar
            def _(act):
                act.wait_ge(consts, 3)
                for s in range(n_steps):
                    for k, (row, n) in enumerate(pieces[s % 2]):
                        q = s * NP_ + k
                        w_ = n * HW
                        act.wait_ge(cent, q + 1)
                        act.activation(sq[:, :, 0:w_], xc[:, :, 0:w_], ACT.Square).then_inc(sqd, 1)
                        act.wait_ge(var, q + 1)
                        act.activation(lnv[:, 0:w_], bank[:, 7, 0:w_], ACT.Ln, bias=eps[:]).then_inc(lns, 1)
                        act.wait_ge(lns, q + 1)
                        act.activation(rstd[:, 0:w_], lnv[:, 0:w_], ACT.Exp, scale=-0.5).then_inc(rst, 1)
                    flat = prod[:].rearrange("p u t n -> p (u t n)")
                    for ob in range(KB):
                        if s or ob:
                            act.wait_ge(out_s, KB * s + ob)
                        for gr in range(n_g):
                            c = (s * KB + ob) * n_g + gr
                            act.wait_ge(prod_s, c + 1)
                            act.copy(flat[:, gr * G4 * N_T:(gr + 1) * G4 * N_T], bank[:, c % 6]).then_inc(copied, 1)

            @block.vector
            def _(dve):
                dve.wait_ge(consts, 3)
                dve.wait_ge(weights_in, 16)
                done = [0]

                def then(ins):
                    ins.then_inc(step, 1)
                    done[0] += 1
                    dve.wait_ge(step, done[0])

                def input_points(d, out, a, b, last):
                    then(dve.scalar_tensor_tensor(out=a, in0=d(2), scalar=-4.0, in1=d(4), op0=ALU.mult, op1=ALU.add))
                    then(dve.scalar_tensor_tensor(out=b, in0=d(1), scalar=-4.0, in1=d(3), op0=ALU.mult, op1=ALU.add))
                    dve.tensor_tensor(out(1), a, b, ALU.add).then_inc(last, 1)
                    dve.tensor_tensor(out(2), a, b, ALU.subtract).then_inc(last, 1)
                    dve.wait_ge(last, marks[last] + 2)
                    then(dve.tensor_tensor(a, d(4), d(2), ALU.subtract))
                    then(dve.tensor_tensor(b, d(3), d(1), ALU.subtract))
                    dve.scalar_tensor_tensor(out=out(3), in0=b, scalar=2.0, in1=a, op0=ALU.mult, op1=ALU.add).then_inc(last, 1)
                    dve.scalar_tensor_tensor(out=out(4), in0=b, scalar=-2.0, in1=a, op0=ALU.mult, op1=ALU.add).then_inc(last, 1)
                    dve.wait_ge(last, marks[last] + 4)
                    then(dve.scalar_tensor_tensor(out=a, in0=d(2), scalar=-5.0, in1=d(4), op0=ALU.mult, op1=ALU.add))
                    then(dve.scalar_tensor_tensor(out=b, in0=d(3), scalar=-5.0, in1=d(5), op0=ALU.mult, op1=ALU.add))
                    dve.scalar_tensor_tensor(out=out(0), in0=d(0), scalar=4.0, in1=a, op0=ALU.mult, op1=ALU.add).then_inc(last, 1)
                    dve.scalar_tensor_tensor(out=out(5), in0=d(1), scalar=4.0, in1=b, op0=ALU.mult, op1=ALU.add).then_inc(last, 1)
                    marks[last] += 6
                    dve.wait_ge(last, marks[last])

                def output_rows(m, out, a, b):
                    then(dve.tensor_tensor(a, m(1), m(2), ALU.add))
                    then(dve.tensor_tensor(b, m(3), m(4), ALU.add))
                    then(dve.tensor_tensor(out(0), a, b, ALU.add))
                    then(dve.tensor_tensor(out(0), out(0), m(0), ALU.add))
                    then(dve.tensor_scalar(b, b, 4.0, None, ALU.mult))
                    then(dve.tensor_tensor(out(2), a, b, ALU.add))
                    then(dve.tensor_tensor(a, m(1), m(2), ALU.subtract))
                    then(dve.tensor_tensor(b, m(3), m(4), ALU.subtract))
                    then(dve.tensor_scalar(b, b, 2.0, None, ALU.mult))
                    then(dve.tensor_tensor(out(1), a, b, ALU.add))
                    then(dve.tensor_tensor(a, a, m(5), ALU.add))
                    then(dve.tensor_scalar(b, b, 4.0, None, ALU.mult))
                    then(dve.tensor_tensor(out(3), a, b, ALU.add))

                marks = {rows_s: 0, pts_s: 0}
                for s in range(n_steps):
                    h = s % 2
                    if s:
                        border = 0 if h == 0 else ROWS - 1
                        then(dve.memset(v[:, :, border, :], 0.0))
                    for k, (row, n) in enumerate(pieces[h]):
                        q = s * NP_ + k
                        w_ = n * HW
                        at = row + 1 - h * HALF_R
                        if q:
                            dve.wait_ge(v_s, KB * q)
                        dve.wait_ge(mean, q + 1)
                        dve.wait_ge(x_loaded, 16 * q + 16)
                        dve.tensor_tensor(xc[:, :, 0:w_], xt[:, :, 0:w_], bcast(bank[:, 6, 0:w_], KB), ALU.subtract).then_inc(cent, 1)
                        dve.wait_ge(rst, q + 1)
                        dve.wait_ge(cent, q + 1)
                        for kb in range(KB):
                            dve.tensor_tensor(v[:, kb, at:at + n, 1:1 + HW], xc[:, kb, 0:w_].rearrange("p (r c) -> p r c", c=HW),
                                              rstd[:, 0:w_].rearrange("p (r c) -> p r c", c=HW), ALU.mult).then_inc(v_s, 1)
                    dve.wait_ge(v_s, KB * NP_ * (s + 1))
                    for kb in range(KB):
                        shape = dict(p=P)
                        n1, n2 = HALF_T * WIDE, TILE_IN * N_T
                        ta, tb = (t[:, 0:n1].rearrange("p (r c) -> p r c", c=WIDE) for t in tmp)
                        input_points(lambda i: v[:, kb, i:i + TILE_OUT * (HALF_T - 1) + 1:TILE_OUT, :], lambda t: r[:, t], ta, tb, rows_s)
                        ta, tb = (t[:, 0:n2].rearrange("p (r c) -> p r c", c=NT) for t in tmp)
                        rr = r[:].rearrange("p t h c -> p (t h) c")
                        pp = pts[:, kb].rearrange("p u t (h c) -> p u (t h) c", c=NT)
                        input_points(lambda j: rr[:, :, j:j + TILE_OUT * (NT - 1) + 1:TILE_OUT], lambda u: pp[:, u], ta, tb, pts_s)
                        dve.sem_inc(pts_s, 6)
                        marks[pts_s] += 6
                    for ob in range(KB):
                        dve.wait_ge(copied, ((s * KB) + ob + 1) * n_g)
                        ta, tb = (t[:, 0:TILE_IN * N_T].rearrange("p (u n) -> p u n", n=N_T) for t in tmp)
                        output_rows(lambda t: prod[:, :, t], lambda p: s1[:, p], ta, tb)
                        if s or ob:
                            dve.wait_ge(stored, 16 * (KB * s + ob))
                        ta, tb = (t[:, 0:TILE_OUT * N_T].rearrange("p (q h c) -> p q h c", q=TILE_OUT, c=NT) for t in tmp)
                        yv = y[:].rearrange("p (h a) (c q) -> p a h c q", a=TILE_OUT, q=TILE_OUT)
                        output_rows(lambda u: s1[:, :, u].rearrange("p a (h c) -> p a h c", c=NT), lambda q: yv[:, :, :, :, q], ta, tb)
                        dve.wait_ge(res_in, 16 * (KB * s + ob) + 16)
                        dve.scalar_tensor_tensor(out=y[:].rearrange("p r c -> p (r c)"), in0=y[:].rearrange("p r c -> p (r c)"),
                                                 scalar=bias[:, ob:ob + 1], in1=res[:], op0=ALU.add, op1=ALU.add).then_inc(out_s, 1)


def graph_experts(nc, name, w, x_in, x_out):
    with ExitStack() as ctx:
        g = Graph(nc, ctx, name)
        features_phase(nc, f"{name}_features", w, g, x_in)
        with nc.sbuf_tensor(f"{name}_near_key", [P, EC], F32) as near_key:
            with nc.sbuf_tensor(f"{name}_far_key", [P, EC], F32) as far_key:
                keys_phase(nc, f"{name}_keys", w["edge_index"], near_key, far_key)
                far_phase(nc, f"{name}_far", g, far_key)
            near_phase(nc, f"{name}_near", g, near_key)
        gate_phase(nc, f"{name}_gate", w, g)
        experts_phase(nc, f"{name}_experts", w, g, x_in, x_out)


def build(nc, a, out):
    x1, x2, x3 = (nc.dram_tensor(n, (B, C, L), F32, kind="Internal").ap() for n in ("x1", "x2", "x3"))

    def layer(prefix):
        return {k[len(prefix):]: v for k, v in a.items() if k.startswith(prefix)}

    mamba_phase(nc, layer("L0_conv_"), a["x"], x1)
    graph_experts(nc, "g0", layer("L0_ffn_"), x1, x2)
    conv = layer("L1_conv_")
    with nc.sbuf_tensor("points", [P, KB, TILE_IN, TILE_IN, C], F32) as points:
        kernel_points_phase(nc, "kernels", conv, points)
        winograd_phase(nc, "winograd", conv, points, x2, x3)
    graph_experts(nc, "g1", layer("L1_ffn_"), x3, out)


TRANSPOSED = ("W_in", "W_xp", "W_dt", "W_out", "W1", "W2")


def kernel(**inputs):
    import concourse.bacc as _bacc
    from concourse.bass_utils import run_bass_kernel_spmd as _run

    laid = {}
    for name, value in inputs.items():
        v = np.asarray(value)
        if name == "x":
            v = v.reshape(B, C, L)
        elif name.startswith("L0_conv_") and name[8:] in TRANSPOSED:
            name, v = name + "T", v.T
        elif name in ("L1_conv_weight", "L1_conv_mask"):
            v = v.transpose(1, 2, 3, 0)
        laid[name] = np.ascontiguousarray(v)

    nc = _bacc.Bacc("TRN2", target_bir_lowering=False, num_devices=1)
    arrays, aps = {}, {}
    for name, v in laid.items():
        arrays[f"in_{name}"] = v
        aps[name] = nc.dram_tensor(f"in_{name}", v.shape, mybir.dt.from_np(v.dtype), kind="ExternalInput").ap()
    out = nc.dram_tensor("out", (B, C, L), F32, kind="ExternalOutput").ap()
    build(nc, aps, out)
    r = _run(nc, [arrays], core_ids=[0])
    return r.results[0]["out"].reshape(B, C, HW, HW)
```

```python
from contextlib import ExitStack

import numpy as np
import concourse.bass as bass
from concourse import mybir

F32 = mybir.dt.float32
BF16 = mybir.dt.bfloat16
I32 = mybir.dt.int32
U32 = mybir.dt.uint32
ALU = mybir.AluOpType
ACT = mybir.ActivationFunctionType
AX = mybir.AxisListType

P = 128
B, C, HW = 2, 256, 64
L = HW * HW
M = B * L
KB = C // P
T = 512
TI = L // T
DI, NS, R = 512, 16, 16
MB = DI // P
FF = 4 * C
FB = FF // P


class Phase:

    def __init__(self, nc, name):
        self.nc, self.name, self.ctx = nc, name, ExitStack()
        self.sems = []

    def __enter__(self):
        return self

    def sb(self, name, shape, dt=F32):
        return self.ctx.enter_context(self.nc.sbuf_tensor(f"{self.name}_{name}", shape, dt))

    def ps(self, name, shape, dt=F32):
        return self.ctx.enter_context(self.nc.psum_tensor(f"{self.name}_{name}", shape, dt))

    def sem(self, name):
        s = self.nc.alloc_semaphore(name=f"{self.name}_{name}")
        self.sems.append(s)
        return s

    def __exit__(self, *exc):
        if exc[0] is None:
            self.nc.all_engine_barrier()
            self.nc.gpsimd.dma_reset()
            self.nc.all_engine_barrier()
            self.nc.clear_and_free_semaphores(self.sems)
            self.nc.all_engine_barrier()
        self.ctx.close()


def bcast(ap, n):
    return ap.rearrange("p (o t) -> p o t", o=1).to_broadcast([ap.shape[0], n, ap.shape[1]])


def mamba_phase(nc, w, x_in, x_out):
    LAST = B * TI - 1
    HF = FB // 2
    RW = R + 2 * NS
    with Phase(nc, "mamba") as ph:
        sb, ps, sem = ph.sb, ph.ps, ph.sem
        w_in = sb("w_in", [P, KB, 2 * DI])
        w_xp = sb("w_xp", [P, MB, RW])
        w_dt = sb("w_dt", [R, DI])
        w_out = sb("w_out", [P, MB, C])
        w_1 = sb("w_1", [P, KB, FF])
        w_2 = sb("w_2", [P, FB, C])
        gamma, beta = sb("gamma", [P, KB]), sb("beta", [P, KB])
        conv_w, conv_b = sb("conv_w", [P, MB, 4]), sb("conv_b", [P, MB])
        b_dt, d_skip = sb("b_dt", [P, MB]), sb("d_skip", [P, MB])
        b_1, b_2 = sb("b_1", [P, FB]), sb("b_2", [P, KB])
        a_neg, a_log = sb("a_neg", [P, MB, NS]), sb("a_log", [P, MB, NS])
        ones_mean, ident = sb("ones_mean", [P, P]), sb("ident", [P, P])
        eps_c, eps_n, one = sb("eps_c", [P, 1]), sb("eps_n", [P, 1]), sb("one", [P, 1])
        xt, yn = (sb(n, [P, B, KB, T]) for n in ("xt", "yn"))
        lnb = sb("lnb", [P, 2 * KB, T])
        xc, v = lnb[:, 0:KB], lnb[:, KB:2 * KB]
        r_dt = lnb
        sq, y2, res = (sb(n, [P, KB, T]) for n in ("sq", "y2", "res"))
        rstd = sb("rstd", [P, T])
        xm = sb("xm", [P, MB, T + 3])
        tail = sb("tail", [P, B, MB, 3])
        zs, dt, dtu, y = (sb(n, [P, B, MB, T]) for n in ("zs", "dt", "dtu", "y"))
        cx, u = (sb(n, [P, MB, T]) for n in ("cx", "u"))
        ea = cx
        prj = sb("prj", [RW, B, T])
        dA, hb = (sb(n, [P, 2, MB, T]) for n in ("dA", "hb"))
        g1 = sb("g1", [P, HF, T])
        state = sb("state", [P, B, NS, MB])
        bank = ps("bank", [P, 8, T])
        B_BANK, C_BANK, LN_BANK, TURN, ACC = 0, 1, 3, 4, 6

        weights_in, a_exp, consts = sem("weights_in"), sem("a_exp"), sem("consts")
        x_in_s, x_stored, out_free = sem("x_in"), sem("x_stored"), sem("out_free")
        mean, cent, sqd, var, lns, rst, nrm = ([sem(f"{n}{k}") for k in range(2)] for n in ("mean", "cent", "sqd", "var", "lns", "rst", "nrm"))
        yn_s, xz_s, xm_s, tails_s, conv_s, tail_s, u_s = (sem(n) for n in ("yn", "xz", "xm", "tails", "conv", "tail", "u"))
        proj_s, prj_s, dtp_s, z_s, dte_s, dt_s, dtu_s, yi_s = (sem(n) for n in ("proj", "prj", "dtp", "z", "dte", "dt", "dtu", "yi"))
        bc_s, dA_s, dbu_s, scan_s, save_s, hc_s, yacc_s = (sem(n) for n in ("bc", "dA", "dbu", "scan", "save", "hc", "yacc"))
        ym_s, wo_s, y2_s, res_s, up_s, g1_s, dn_s, x1_s = (sem(n) for n in ("ym", "wo", "y2", "res", "up", "g1", "dn", "x1"))

        loads = [(w_in, w["W_inT"].rearrange("(k p) n -> p k n", p=P)), (w_xp, w["W_xpT"].rearrange("(k p) n -> p k n", p=P)),
                 (w_dt, w["W_dtT"]), (w_out, w["W_outT"].rearrange("(k p) n -> p k n", p=P)),
                 (w_1, w["W1T"].rearrange("(k p) n -> p k n", p=P)), (w_2, w["W2T"].rearrange("(k p) n -> p k n", p=P)),
                 (conv_w, w["conv_w"].rearrange("(k p) o n -> p k (o n)", p=P)),
                 (a_log, w["A_log"].rearrange("(k p) n -> p k n", p=P))]
        vectors = [(gamma, "gamma"), (beta, "beta"), (conv_b, "conv_b"), (b_dt, "b_dt"), (d_skip, "D"), (b_1, "b1"), (b_2, "b2")]
        n_loads = len(loads) + len(vectors)

        def tiles(eng, step):
            step(0, 0, 0, True, False)
            with eng.Fori(0, TI - 1) as i:
                step(i * 2 + 1, i, 1, False, False)
                step(i * 2 + 2, i + 1, 0, False, False)
            step(LAST, TI - 1, 1, False, True)

        def is_first(q):
            return isinstance(q, int) and q == 0

        def before(i, b):
            return (i, 1) if b == 0 else (i + 1, 0)

        with nc.Block() as block:
            @block.sync
            def _(sp):
                for tile, src in loads:
                    sp.dma_start(tile[:], src).then_inc(weights_in, 16)
                with nc.allow_non_contiguous_dma(reason="short vectors"):
                    for tile, name in vectors:
                        sp.dma_start(tile[:], w[name].rearrange("(k p) -> p k", p=P)).then_inc(weights_in, 16)
                sp.sem_inc(out_free, 1)

                def load(i, b):
                    sp.dma_start(xt[:, b], x_in[b].rearrange("(k p) t -> p k t", p=P)[:, :, bass.ds(i * T, T)]).then_inc(x_in_s, 16)

                def store(q, i, b):
                    sp.wait_ge(x1_s, KB * q + KB)
                    sp.dma_start(x_out[b].rearrange("(k p) t -> p k t", p=P)[:, :, bass.ds(i * T, T)], y2[:]).then_inc(x_stored, 16)
                    sp.wait_ge(x_stored, 16 * q + 16)
                    sp.sem_inc(out_free, 1)

                def step(s, i, b, first, last):
                    if not last:
                        if not first:
                            sp.wait_ge(res_s, s)
                        sp.wait_ge(x_in_s, 16 * s + 16)
                        load(*before(i, b))
                    if not first:
                        store(s - 1, i if b else i - 1, 1 - b)

                load(0, 0)
                tiles(sp, step)
                store(LAST, TI - 1, 1)

            @block.gpsimd
            def _(pool):
                for k, (t, value) in enumerate(((ident, 0.0), (ones_mean, 1.0 / C), (tail, 0.0), (state, 0.0), (eps_c, 1e-6), (eps_n, 1e-5),
                                                (one, 1.0))):
                    pool.memset(t[:], value).then_inc(consts, 1)
                pool.wait_ge(consts, 7)
                pool.affine_select(out=ident[:], in_=ident[:], compare_op=ALU.not_equal, fill=1.0, base=0,
                                   pattern=[[-1, P]], channel_multiplier=1).then_inc(consts, 1)
                pool.sem_inc(yacc_s, 1)

                def step(s, i, b, first, last):
                    pool.wait_ge(yi_s, MB * (s + 1))
                    for n in range(NS):
                        pool.wait_ge(hc_s, s * NS + n + 1)
                        pool.wait_ge(yacc_s, s * NS + n + 1)
                        pool.tensor_tensor(y[:, b], y[:, b], hb[:, n % 2], ALU.add).then_inc(yacc_s, 1)

                tiles(pool, step)

            @block.tensor
            def _(pe):
                pe.wait_ge(weights_in, 16 * n_loads)
                pe.wait_ge(consts, 8)
                pe.wait_ge(a_exp, 1)

                def mean_of(q, b, k):
                    if k == 0:
                        pe.wait_ge(x_in_s, 16 * q + 16)
                    else:
                        pe.wait_ge(nrm[0], q + 1)
                    for kb in range(KB):
                        mm = pe.matmul(bank[:, LN_BANK], ones_mean[:], xt[:, b, kb] if k == 0 else v[:, kb], start=kb == 0, stop=kb == KB - 1)
                    mm.then_inc(mean[k], 1)

                def var_of(q, k):
                    pe.wait_ge(sqd[k], q + 1)
                    for kb in range(KB):
                        mm = pe.matmul(bank[:, LN_BANK], ones_mean[:], sq[:, kb], start=kb == 0, stop=kb == KB - 1)
                    mm.then_inc(var[k], 1)

                def xz(q, b, m0):
                    pe.wait_ge(yn_s, KB * (q + 1))
                    for m in range(m0, m0 + MB):
                        if m0 == 0 and m < 2:
                            if not is_first(q):
                                pe.wait_ge(g1_s, FB * q)
                                pe.wait_ge(z_s, MB * q)
                        else:
                            pe.wait_ge(xm_s, 2 * MB * q + m - 1)
                        for kb in range(KB):
                            mm = pe.matmul(bank[:, TURN + m % 2], w_in[:, kb, m * P:(m + 1) * P], yn[:, b, kb], start=kb == 0, stop=kb == KB - 1)
                        mm.then_inc(xz_s, 1)

                def project(q, b):
                    pe.wait_ge(u_s, MB * (q + 1))
                    pe.wait_ge(xm_s, 2 * MB * (q + 1))
                    for m in range(MB):
                        mm = pe.matmul(bank[0:RW, TURN], w_xp[:, m, :], u[:, m], start=m == 0, stop=m == MB - 1)
                    mm.then_inc(proj_s, 1)

                def dt_blocks(q, b):
                    pe.wait_ge(prj_s, q + 1)
                    for m in range(MB):
                        if m >= 2:
                            pe.wait_ge(z_s, MB * q + m - 1)
                        mm = pe.matmul(bank[:, TURN + m % 2], w_dt[:, m * P:(m + 1) * P], prj[0:R, b], start=True, stop=True)
                        mm.then_inc(dtp_s, 1)

                def spread_bc(s, b, n):
                    g = s * NS + n
                    if n == 0:
                        pe.wait_ge(prj_s, s + 1)
                    pe.wait_ge(dbu_s, g + 1)
                    for c, at in ((0, B_BANK), (1, C_BANK + n % 2)):
                        k = R + c * NS + n
                        mm = pe.matmul(bank[:, at], ident[0:RW, k:k + 1].to_broadcast([RW, P]), prj[:, b], start=True, stop=True)
                    mm.then_inc(bc_s, 1)

                def out_blocks(q, b):
                    pe.wait_ge(ym_s, q + 1)
                    for ob in range(KB):
                        for m in range(MB):
                            mm = pe.matmul(bank[:, ACC + ob], w_out[:, m, ob * P:(ob + 1) * P], y[:, b, m], start=m == 0, stop=m == MB - 1)
                    mm.then_inc(wo_s, 1)

                def up_blocks(q, f0, dts):
                    pe.wait_ge(y2_s, q + 1)
                    for f in range(f0, f0 + 2):
                        if f >= 2:
                            pe.wait_ge(g1_s, FB * q + f - 1 + FB)
                        else:
                            pe.wait_ge(z_s, MB * dts)
                        for kb in range(KB):
                            mm = pe.matmul(bank[:, TURN + f % 2], w_1[:, kb, f * P:(f + 1) * P], y2[:, kb], start=kb == 0, stop=kb == KB - 1)
                        mm.then_inc(up_s, 1)

                def down_blocks(q, h):
                    pe.wait_ge(g1_s, FB * q + HF * (h + 1) + FB)
                    if h == 0:
                        pe.wait_ge(y2_s, q + 1)
                    for ob in range(KB):
                        for f in range(HF):
                            mm = pe.matmul(bank[:, ACC + ob], w_2[:, h * HF + f, ob * P:(ob + 1) * P], g1[:, f],
                                           start=h == 0 and f == 0, stop=h == 1 and f == HF - 1)
                    mm.then_inc(dn_s, 1)

                def step(s, i, b, first, last):
                    o = 1 - b
                    for n in range(NS):
                        if n < NS - 1:
                            spread_bc(s, b, n + 1)
                        elif not last:
                            spread_bc(s + 1, o, 0)
                        if not first:
                            if n == 0:
                                out_blocks(s - 1, o)
                            if n in (3, 4):
                                up_blocks(s - 1, 2 * (n - 3), s + 1)
                            if n == 5:
                                down_blocks(s - 1, 0)
                            if n in (6, 7):
                                up_blocks(s - 1, 2 * (n - 4), s + 1)
                        if not last:
                            if n in (3, 6):
                                mean_of(s + 1, o, (n - 3) // 3)
                            if n in (4, 7):
                                var_of(s + 1, (n - 4) // 3)
                            if n in (8, 9):
                                xz(s + 1, o, MB * (n - 8))
                        if n == 10 and not first:
                            down_blocks(s - 1, 1)
                        if n == 11 and not last:
                            project(s + 1, o)
                        if n == 12 and not last:
                            dt_blocks(s + 1, o)

                for k in range(2):
                    mean_of(0, 0, k)
                    var_of(0, k)
                xz(0, 0, 0)
                xz(0, 0, MB)
                project(0, 0)
                dt_blocks(0, 0)
                spread_bc(0, 0, 0)
                tiles(pe, step)
                out_blocks(LAST, 1)
                for h in range(2):
                    up_blocks(LAST, 4 * h, LAST + 1)
                    up_blocks(LAST, 4 * h + 2, LAST + 1)
                    down_blocks(LAST, h)

            @block.scalar
            def _(act):
                act.sem_inc(g1_s, FB)
                act.wait_ge(weights_in, 16 * n_loads)
                act.wait_ge(consts, 8)
                act.activation(a_neg[:], a_log[:], ACT.Exp).then_inc(a_exp, 1)
                act.wait_ge(a_exp, 1)
                act.mul(a_neg[:], a_neg[:], -1.0).then_inc(a_exp, 1)
                act.wait_ge(a_exp, 2)

                def square(q, k):
                    act.wait_ge(cent[k], q + 1)
                    act.activation(sq[:], xc[:], ACT.Square).then_inc(sqd[k], 1)

                def root(q, k):
                    act.wait_ge(var[k], q + 1)
                    act.wait_ge(nrm[1 - k], q + 1)
                    act.activation(rstd[:], bank[:, LN_BANK], ACT.Ln, bias=(eps_c if k == 0 else eps_n)[:]).then_inc(lns[k], 1)
                    act.wait_ge(lns[k], q + 1)
                    act.activation(rstd[:], rstd[:], ACT.Exp, scale=-0.5).then_inc(rst[k], 1)

                def affine(q, b):
                    act.wait_ge(nrm[1], q + 2)
                    for kb in range(KB):
                        act.activation(yn[:, b, kb], v[:, kb], ACT.Identity, scale=gamma[:, kb:kb + 1], bias=beta[:, kb:kb + 1]).then_inc(yn_s, 1)

                def take_xm(q, b):
                    act.wait_ge(tail_s, q + 1)
                    act.copy(xm[:, :, 0:3], tail[:, b]).then_inc(tails_s, 1)
                    for m in range(MB):
                        act.wait_ge(xz_s, 2 * MB * q + m + 1)
                        act.copy(xm[:, m, 3:3 + T], bank[:, TURN + m % 2]).then_inc(xm_s, 1)

                def take_z(q, b):
                    for m in range(MB):
                        act.wait_ge(xz_s, 2 * MB * q + MB + m + 1)
                        act.activation(zs[:, b, m], bank[:, TURN + m % 2], ACT.Silu).then_inc(xm_s, 1)

                def take_u(q):
                    for m in range(MB):
                        act.wait_ge(conv_s, 4 * MB * q + 3 * MB + m + 1)
                        act.activation(u[:, m], cx[:, m], ACT.Silu, bias=conv_b[:, m:m + 1]).then_inc(u_s, 1)

                def take_prj(q, b):
                    act.wait_ge(proj_s, q + 1)
                    act.copy(prj[:, b], bank[0:RW, TURN]).then_inc(prj_s, 1)
                    act.wait_ge(u_s, MB * (q + 1))
                    for m in range(MB):
                        act.activation(y[:, b, m], u[:, m], ACT.Copy, scale=d_skip[:, m:m + 1]).then_inc(yi_s, 1)

                def softplus(q):
                    for m in range(MB):
                        act.wait_ge(dtp_s, MB * q + m + 1)
                        act.activation(r_dt[:, m], bank[:, TURN + m % 2], ACT.Identity, bias=b_dt[:, m:m + 1]).then_inc(z_s, 1)
                    act.wait_ge(z_s, MB * (q + 1))
                    act.activation(ea[:], r_dt[:], ACT.Abs).then_inc(dte_s, 1)
                    act.wait_ge(dte_s, 3 * q + 1)
                    act.activation(ea[:], ea[:], ACT.Exp, scale=-1.0).then_inc(dte_s, 1)
                    act.wait_ge(dte_s, 3 * q + 2)
                    act.activation(ea[:], ea[:], ACT.Ln, bias=one[:]).then_inc(dte_s, 1)

                def decay(s, b, n):
                    if n == 0:
                        act.wait_ge(dt_s, s + 1)
                    act.wait_ge(scan_s, MB * (s * NS + n - 1) + 2 * MB)
                    for m in range(MB):
                        act.activation(dA[:, n % 2, m], dt[:, b, m], ACT.Exp, scale=a_neg[:, m, n:n + 1]).then_inc(dA_s, 1)

                def gelus(q, f0):
                    for f in range(f0, f0 + 2):
                        if f % HF == 0:
                            act.wait_ge(dn_s, 2 * q + f // HF + 1)
                        act.wait_ge(up_s, FB * q + f + 1)
                        act.activation(g1[:, f % HF], bank[:, TURN + f % 2], ACT.Gelu, bias=b_1[:, f:f + 1]).then_inc(g1_s, 1)

                def step(s, i, b, first, last):
                    o = 1 - b
                    for n in range(NS):
                        if n < NS - 1:
                            decay(s, b, n + 1)
                        elif not last:
                            decay(s + 1, o, 0)
                        if not first and n in (3, 4, 6, 7):
                            gelus(s - 1, {3: 0, 4: 2, 6: 4, 7: 6}[n])
                        if not last:
                            if n in (4, 6):
                                square(s + 1, (n - 4) // 2)
                            if n in (5, 7):
                                root(s + 1, (n - 5) // 2)
                            if n == 8:
                                affine(s + 1, o)
                                take_xm(s + 1, o)
                            if n == 9:
                                take_z(s + 1, o)
                            if n == 10:
                                take_u(s + 1)
                            if n == 11:
                                take_prj(s + 1, o)
                            if n == 12:
                                softplus(s + 1)

                for k in range(2):
                    square(0, k)
                    root(0, k)
                affine(0, 0)
                take_xm(0, 0)
                take_z(0, 0)
                take_u(0)
                take_prj(0, 0)
                softplus(0)
                decay(0, 0, 0)
                tiles(act, step)
                for f0 in range(0, FB, 2):
                    gelus(LAST, f0)

            @block.vector
            def _(dve):
                dve.wait_ge(weights_in, 16 * n_loads)
                dve.wait_ge(consts, 8)
                dve.sem_inc(tail_s, 1)
                dve.sem_inc(dbu_s, 1)
                dve.sem_inc(nrm[1], 1)
                dve.sem_inc(scan_s, 2 * MB)
                dve.sem_inc(dn_s, 1)

                def centre(q, b, k):
                    dve.wait_ge(mean[k], q + 1)
                    dve.tensor_tensor(xc[:], xt[:, b] if k == 0 else v[:], bcast(bank[:, LN_BANK], KB), ALU.subtract).then_inc(cent[k], 1)

                def scale(q, k):
                    dve.wait_ge(rst[k], q + 1)
                    dve.tensor_tensor(v[:], xc[:], bcast(rstd[:], KB), ALU.mult).then_inc(nrm[k], 1)

                def convolve(q, b, taps):
                    for tap in taps:
                        for m in range(MB):
                            if tap == 0:
                                dve.wait_ge(xm_s, 2 * MB * q + m + 1)
                                dve.wait_ge(tails_s, q + 1)
                                dve.tensor_scalar(cx[:, m], xm[:, m, 0:T], conv_w[:, m, 0:1], None, ALU.mult).then_inc(conv_s, 1)
                            else:
                                dve.wait_ge(conv_s, 4 * MB * q + (tap - 1) * MB + m + 1)
                                dve.scalar_tensor_tensor(out=cx[:, m], in0=xm[:, m, tap:tap + T], scalar=conv_w[:, m, tap:tap + 1],
                                                         in1=cx[:, m], op0=ALU.mult, op1=ALU.add).then_inc(conv_s, 1)
                    if 3 in taps:
                        dve.wait_ge(conv_s, 4 * MB * (q + 1))
                        dve.tensor_copy(tail[:, b], xm[:, :, T:T + 3]).then_inc(tail_s, 1)

                def make_dt(q, b):
                    dve.wait_ge(dte_s, 3 * q + 3)
                    dve.scalar_tensor_tensor(out=dt[:, b], in0=r_dt[:], scalar=0.0, in1=ea[:], op0=ALU.max, op1=ALU.add).then_inc(dt_s, 1)
                    dve.wait_ge(dt_s, q + 1)
                    dve.tensor_tensor(dtu[:, b], dt[:, b], u[:], ALU.mult).then_inc(dtu_s, 1)

                def scan(s, b, n):
                    g = s * NS + n
                    h = hb[:, n % 2]
                    dve.wait_ge(bc_s, g + 1)
                    if n == 0:
                        dve.wait_ge(dtu_s, s + 1)
                    if not (is_first(s) and n == 0):
                        dve.wait_ge(yacc_s, g)
                    dve.tensor_tensor(h, dtu[:, b], bcast(bank[:, B_BANK], MB), ALU.mult).then_inc(dbu_s, 1)
                    dve.wait_ge(dbu_s, g + 2)
                    for m in range(MB):
                        dve.wait_ge(dA_s, MB * g + m + 1)
                        dve.tensor_tensor_scan(out=h[:, m], data0=dA[:, n % 2, m], data1=h[:, m],
                                               initial=state[:, b, n, m:m + 1], op0=ALU.mult, op1=ALU.add).then_inc(scan_s, 1)
                    dve.wait_ge(scan_s, MB * (g + 1) + 2 * MB)
                    dve.tensor_copy(state[:, b, n, :], h[:, :, T - 1]).then_inc(save_s, 1)
                    dve.wait_ge(save_s, g + 1)
                    dve.tensor_tensor(h, h, bcast(bank[:, C_BANK + n % 2], MB), ALU.mult).then_inc(hc_s, 1)

                def gate(q, b):
                    dve.wait_ge(yacc_s, NS * (q + 1) + 1)
                    dve.wait_ge(xm_s, 2 * MB * (q + 1))
                    dve.tensor_tensor(y[:, b], y[:, b], zs[:, b], ALU.mult).then_inc(ym_s, 1)

                def join(q, b):
                    dve.wait_ge(wo_s, q + 1)
                    dve.wait_ge(out_free, q + 1)
                    dve.tensor_tensor(y2[:], bank[:, ACC:ACC + KB], yn[:, b], ALU.add).then_inc(y2_s, 1)
                    dve.wait_ge(y2_s, q + 1)
                    dve.tensor_tensor(res[:], y2[:], xt[:, b], ALU.add).then_inc(res_s, 1)

                def finish(q):
                    dve.wait_ge(dn_s, 2 * q + 3)
                    dve.wait_ge(res_s, q + 1)
                    for ob in range(KB):
                        dve.scalar_tensor_tensor(out=y2[:, ob], in0=bank[:, ACC + ob], scalar=b_2[:, ob:ob + 1], in1=res[:, ob],
                                                 op0=ALU.add, op1=ALU.add).then_inc(x1_s, 1)

                def step(s, i, b, first, last):
                    o = 1 - b
                    for n in range(NS):
                        scan(s, b, n)
                        if not first:
                            if n == 0:
                                gate(s - 1, o)
                            if n == 2:
                                join(s - 1, o)
                            if n == 12:
                                finish(s - 1)
                        if not last:
                            if n in (4, 6):
                                centre(s + 1, o, (n - 4) // 2)
                            if n in (5, 7):
                                scale(s + 1, (n - 5) // 2)
                            if n == 9:
                                convolve(s + 1, o, (0, 1))
                            if n == 10:
                                convolve(s + 1, o, (2, 3))
                            if n == 14:
                                make_dt(s + 1, o)

                for k in range(2):
                    centre(0, 0, k)
                    scale(0, k)
                convolve(0, 0, (0, 1, 2, 3))
                make_dt(0, 0)
                tiles(dve, step)
                gate(LAST, 1)
                join(LAST, 1)
                finish(LAST)
NB = M // P
HEADS, EXPERTS = 4, 4
HC = HEADS * EXPERTS
TW = HC + HEADS
EDGES = 1048576
EC = EDGES // P
FE = 512
FEB = FE // P
SUB = T // P
KEY_CHUNK = 1024
FAR_CHUNK, FAR_ROUNDS = EC // 32, 7
FAR_COLS = EC // FAR_CHUNK * 8 * FAR_ROUNDS
FAR_SUB = 16
PICK_CHUNK, PICK_ROUNDS = EC // 32, 2
PICKS = EC // PICK_CHUNK * 8 * PICK_ROUNDS
NEAR_ROUNDS = 22
NEAR_COLS = 8 * NEAR_ROUNDS
GROUPS = 16
NEAR_GROUP, FAR_GROUP = NEAR_COLS // GROUPS, FAR_COLS // GROUPS
FAR_SUBS = FAR_GROUP // FAR_SUB
REST_CHUNK, REST_ROUNDS = (EC + PICKS) // 4, 7
REST_COLS = 4 * 8 * REST_ROUNDS


class Graph:

    def __init__(self, nc, ctx, name):
        def sb(n, shape, dt=F32):
            return ctx.enter_context(nc.sbuf_tensor(f"{name}_{n}", shape, dt))
        self.h = sb("h", [P, NB, TW])
        self.a_dst = sb("a_dst", [P, NB, HEADS])
        self.top = sb("top", [P, HEADS])
        self.last = sb("last", [P, TW])
        self.count = sb("count", [P, NB])
        self.agg = sb("agg", [P, NB, TW])
        self.near_more = sb("near_more", [1, 1], I32)
        self.far_more = sb("far_more", [1, 1], I32)
        self.gate = sb("gate", [P, NB, EXPERTS])
        self.table = nc.dram_tensor(f"{name}_table", (M, TW), F32, kind="Internal").ap()
        self.dst_table = nc.dram_tensor(f"{name}_dst_table", (M, HEADS), F32, kind="Internal").ap()
        self.tn = nc.dram_tensor(f"{name}_tn", (B, C, L), F32, kind="Internal").ap()


def rows(ap, n=P):
    return ap.rearrange("(o n) -> o n", o=1).to_broadcast([n, ap.shape[0]])


def tiles(eng, step):
    step(0, 0, 0, True, False)
    with eng.Fori(0, TI - 1) as i:
        step(i * 2 + 1, i, 1, False, False)
        step(i * 2 + 2, i + 1, 0, False, False)
    step(B * TI - 1, TI - 1, 1, False, True)


def after(i, b):
    return (i, 1) if b == 0 else (i + 1, 0)


def ahead_of(i, b):
    return (i, 0) if b == 1 else (i - 1, 1)


def features_phase(nc, name, w, g, x_in):
    LAST = B * TI - 1
    with Phase(nc, name) as ph:
        sb, ps, sem = ph.sb, ph.ps, ph.sem
        w_gat = sb("w_gat", [P, KB, HC])
        att = sb("att", [P, 2, HC])
        ones_mean, eps = sb("ones_mean", [P, P]), sb("eps", [P, 1])
        xt, xc, sq, tn = (sb(n, [P, B, KB, T]) for n in ("xt", "xc", "sq", "tn"))
        lnv, rstd = sb("lnv", [P, T]), sb("rstd", [P, B, T])
        prod, part_top = sb("prod", [P, 2, SUB, HC]), sb("part_top", [P, HEADS])
        mean_b, var_b, h_b = (ps(n, [P, B, T]) for n in ("mean_b", "var_b", "h_b"))
        weights_in, consts, free = (sem(n) for n in ("weights_in", "consts", "free"))
        x_loaded, stored = [sem("x_loaded0"), sem("x_loaded1")], [sem("stored0"), sem("stored1")]
        mean, cent, sqd, var, lns, rst, tn_s = (sem(n) for n in ("mean", "cent", "sqd", "var", "lns", "rst", "tn"))
        hp_s, h_s, prod_s, a_s, top_s, all_top, tabled, last_s = (sem(n) for n in ("hp", "h", "prod", "a", "top", "all_top", "tabled", "last"))

        with nc.Block() as block:
            @block.sync
            def _(sp):
                sp.dma_start(w_gat[:], w["W_gat"].rearrange("(k p) n -> p k n", p=P)).then_inc(weights_in, 16)
                for k, n in enumerate(("att_src", "att_dst")):
                    sp.dma_start(att[:, k], rows(w[n].rearrange("h e -> (h e)"))).then_inc(weights_in, 16)
                with sp.Fori(0, TI) as i:
                    for b in range(B):
                        sp.wait_ge(cent, i * B + b + 1)
                        sp.wait_ge(sqd, i * B + b + 1)
                        sp.dma_start(xt[:, b], x_in[b].rearrange("(k p) t -> p k t", p=P)[:, :, bass.ds(i * T, T)]).then_inc(x_loaded[b], 16)
                sp.wait_ge(a_s, 2 * B * TI + 2)
                sp.wait_ge(h_s, B * TI + 2)
                sp.dma_start(g.table.rearrange("(n p) c -> p n c", p=P), g.h[:]).then_inc(tabled, 16)
                sp.dma_start(g.dst_table.rearrange("(n p) c -> p n c", p=P), g.a_dst[:]).then_inc(tabled, 16)
                sp.wait_ge(tabled, 32)
                sp.dma_start(g.last[:], g.table[M - 1:M, :].to_broadcast([P, TW])).then_inc(last_s, 16)
                sp.wait_ge(last_s, 16)

            @block.gpsimd
            def _(pool):
                pool.memset(ones_mean[:], 1.0 / C).then_inc(consts, 1)
                pool.memset(eps[:], 1e-5).then_inc(consts, 1)
                with pool.Fori(0, TI) as i:
                    for b in range(B):
                        pool.wait_ge(tn_s, i * B + b + 3)
                        pool.dma_start(g.tn[b].rearrange("(k p) t -> p k t", p=P)[:, :, bass.ds(i * T, T)], tn[:, b]).then_inc(stored[b], 16)
                        pool.wait_ge(stored[b], 16 * i + 16)
                        pool.sem_inc(free, 1)
                pool.wait_ge(top_s, 1)
                pool.partition_all_reduce(g.top[:], part_top[:], P, bass.bass_isa.ReduceOp.max).then_inc(all_top, 1)
                pool.wait_ge(all_top, 1)

            @block.tensor
            def _(pe):
                def mean_of(s, i, b):
                    pe.wait_ge(x_loaded[b], 16 * i + 16)
                    pe.wait_ge(cent, s + 1)
                    for kb in range(KB):
                        mm = pe.matmul(mean_b[:, b], ones_mean[:], xt[:, b, kb], start=kb == 0, stop=kb == KB - 1)
                    mm.then_inc(mean, 1)

                def features_of(s, b):
                    pe.wait_ge(tn_s, s + 3)
                    pe.wait_ge(prod_s, 2 * s + 2)
                    pe.wait_ge(h_s, s + 1)
                    for sub in range(SUB):
                        for kb in range(KB):
                            mm = pe.matmul(h_b[:, b, sub * HC:(sub + 1) * HC], tn[:, b, kb, sub * P:(sub + 1) * P], w_gat[:, kb],
                                           start=kb == 0, stop=kb == KB - 1)
                    mm.then_inc(hp_s, 1)

                def step(s, i, b, first, last):
                    if not last:
                        mean_of(s + 1, *after(i, b))
                    pe.wait_ge(sqd, s + 3)
                    pe.wait_ge(lns, s + 1)
                    for kb in range(KB):
                        mm = pe.matmul(var_b[:, b], ones_mean[:], sq[:, b, kb], start=kb == 0, stop=kb == KB - 1)
                    mm.then_inc(var, 1)
                    if not first:
                        features_of(s - 1, 1 - b)

                pe.wait_ge(weights_in, 48)
                pe.wait_ge(consts, 2)
                mean_of(0, 0, 0)
                tiles(pe, step)
                features_of(LAST, 1)

            @block.scalar
            def _(act):
                def square(s, b):
                    act.wait_ge(cent, s + 3)
                    act.wait_ge(var, s + 1)
                    act.activation(sq[:, b], xc[:, b], ACT.Square).then_inc(sqd, 1)

                def step(s, i, b, first, last):
                    act.wait_ge(var, s + 3)
                    act.wait_ge(rst, s + 2)
                    act.activation(lnv[:], var_b[:, b], ACT.Ln, bias=eps[:]).then_inc(lns, 1)
                    act.wait_ge(lns, s + 3)
                    act.wait_ge(tn_s, s + 1)
                    act.activation(rstd[:, b], lnv[:], ACT.Exp, scale=-0.5).then_inc(rst, 1)
                    if not last:
                        square(s + 1, 1 - b)

                act.wait_ge(consts, 2)
                act.sem_inc(sqd, 2)
                act.sem_inc(lns, 2)
                act.sem_inc(rst, 2)
                act.sem_inc(var, 2)
                square(0, 0)
                tiles(act, step)

            @block.vector
            def _(dve):
                def centre(s, b):
                    dve.wait_ge(mean, s + 1)
                    dve.wait_ge(tn_s, s + 1)
                    dve.wait_ge(sqd, s + 1)
                    dve.tensor_tensor(xc[:, b], xt[:, b], bcast(mean_b[:, b], KB), ALU.subtract).then_inc(cent, 1)

                def logits(s, i, b):
                    blocks = bass.ds(i * SUB + b * (NB // B), SUB)
                    dve.wait_ge(hp_s, s + 3)
                    dve.wait_ge(a_s, 2 * s + 2)
                    hp = h_b[:, b, 0:SUB * HC].rearrange("p (s c) -> p s c", s=SUB)
                    dve.tensor_copy(g.h[:, blocks, 0:HC], hp).then_inc(h_s, 1)
                    for k in range(2):
                        dve.tensor_tensor(prod[:, k], hp, bcast(att[:, k], SUB), ALU.mult).then_inc(prod_s, 1)
                    dve.wait_ge(prod_s, 2 * s + 6)
                    for k, dst in enumerate((g.h[:, blocks, HC:TW], g.a_dst[:, blocks, :])):
                        dve.tensor_reduce(dst, prod[:, k].rearrange("p s (h e) -> p s h e", h=HEADS), AX.X, ALU.add).then_inc(a_s, 1)

                def step(s, i, b, first, last):
                    if not last:
                        centre(s + 1, 1 - b)
                    if not first:
                        logits(s - 1, *ahead_of(i, b))
                    dve.wait_ge(rst, s + 3)
                    dve.wait_ge(free, s + 1)
                    dve.wait_ge(hp_s, s + 1)
                    dve.wait_ge(cent, s + 3)
                    dve.tensor_tensor(tn[:, b], xc[:, b], bcast(rstd[:, b], KB), ALU.mult).then_inc(tn_s, 1)

                dve.wait_ge(weights_in, 48)
                dve.sem_inc(cent, 2)
                dve.sem_inc(tn_s, 2)
                dve.sem_inc(hp_s, 2)
                dve.sem_inc(a_s, 2)
                dve.sem_inc(free, 2)
                dve.sem_inc(h_s, 2)
                dve.sem_inc(prod_s, 4)
                centre(0, 0)
                tiles(dve, step)
                logits(LAST, TI - 1, 1)
                dve.wait_ge(a_s, 2 * B * TI + 2)
                dve.tensor_reduce(part_top[:], g.h[:, :, HC:TW].rearrange("p n c -> p c n"), AX.X, ALU.max).then_inc(top_s, 1)


def keys_phase(nc, name, edge_index, near_key, far_key):
    src_d = edge_index[0].rearrange("(p n) -> p n", p=P)
    dst_d = edge_index[1].rearrange("(p n) -> p n", p=P)
    n_chunks = EC // KEY_CHUNK
    with Phase(nc, name) as ph:
        sb, sem = ph.sb, ph.sem
        src, dst = sb("src", [P, 2, KEY_CHUNK], I32), sb("dst", [P, 2, KEY_CHUNK], I32)
        packed, src_m, dst_1 = sb("packed", [P, KEY_CHUNK], I32), sb("src_m", [P, KEY_CHUNK]), sb("dst_1", [P, KEY_CHUNK])
        loaded = [sem("loaded0"), sem("loaded1")]
        packed_s, clamped_s, near_s, far_s = (sem(n) for n in ("packed", "clamped", "near", "far"))
        with nc.Block() as block:
            @block.sync
            def _(sp):
                sp.sem_inc(near_s, 2)
                with sp.Fori(0, n_chunks // 2) as i:
                    for k in range(2):
                        c = i * 2 + k
                        sp.wait_ge(near_s, c + 1)
                        sp.dma_start(src[:, k], src_d[:, bass.ds(c * KEY_CHUNK, KEY_CHUNK)]).then_inc(loaded[k], 16)
                        sp.dma_start(dst[:, k], dst_d[:, bass.ds(c * KEY_CHUNK, KEY_CHUNK)]).then_inc(loaded[k], 16)

            @block.vector
            def _(dve):
                dve.sem_inc(far_s, 1)
                with dve.Fori(0, n_chunks // 2) as i:
                    for k in range(2):
                        c = i * 2 + k
                        here = bass.ds(c * KEY_CHUNK, KEY_CHUNK)
                        dve.wait_ge(loaded[k], 32 * i + 32)
                        dve.wait_ge(near_s, c + 2)
                        dve.wait_ge(far_s, c + 1)
                        dve.tensor_scalar(packed[:], dst[:, k], 13, 0x40000000, ALU.logical_shift_left, ALU.bitwise_or).then_inc(packed_s, 1)
                        dve.tensor_scalar(src_m[:], src[:, k], float(M - 1), None, ALU.is_lt).then_inc(packed_s, 1)
                        dve.tensor_scalar(dst_1[:], dst[:, k], 1.0, None, ALU.add).then_inc(packed_s, 1)
                        dve.wait_ge(packed_s, 5 * c + 3)
                        dve.tensor_tensor(packed[:], packed[:], src[:, k], ALU.bitwise_or).then_inc(clamped_s, 1)
                        dve.scalar_tensor_tensor(out=src_m[:], in0=dst[:, k], scalar=float(M), in1=src_m[:],
                                                 op0=ALU.is_lt, op1=ALU.mult).then_inc(packed_s, 1)
                        dve.scalar_tensor_tensor(out=dst_1[:], in0=dst_1[:], scalar=float(M + 1), in1=dst_1[:],
                                                 op0=ALU.is_lt, op1=ALU.mult).then_inc(packed_s, 1)
                        dve.wait_ge(clamped_s, c + 1)
                        dve.wait_ge(packed_s, 5 * c + 5)
                        dve.scalar_tensor_tensor(out=far_key[:, here], in0=src[:, k], scalar=float(M - 1), in1=dst_1[:],
                                                 op0=ALU.is_ge, op1=ALU.mult).then_inc(far_s, 1)
                        dve.tensor_tensor(near_key[:, here], packed[:].bitcast(F32), src_m[:], ALU.mult).then_inc(near_s, 1)


def take_largest(dve, keys, taken, chunk, rounds, max_s, cleared_s):
    n = keys.shape[1] // chunk
    for r in range(rounds):
        for c in range(n):
            if r > 0:
                dve.wait_ge(cleared_s, (r - 1) * n + c + 1)
            dve.max(taken[:, c, 8 * r:8 * r + 8], keys[:, c * chunk:(c + 1) * chunk]).then_inc(max_s, 1)
        for c in range(n):
            dve.wait_ge(max_s, r * n + c + 1)
            part = keys[:, c * chunk:(c + 1) * chunk]
            dve.match_replace(part, taken[:, c, 8 * r:8 * r + 8], part, 0.0).then_inc(cleared_s, 1)
    dve.wait_ge(max_s, rounds * n)
    dve.wait_ge(cleared_s, rounds * n)


def passes(nc, n_passes, sems, more, programs):
    engines = (nc.tensor, nc.vector, nc.scalar, nc.gpsimd, nc.sync)
    left = nc.values_load(more, min_val=0, max_val=1)
    nc.all_engine_barrier()
    with nc.If(left != 0):
        with nc.Fori(0, n_passes):
            left_now = nc.values_load(more, min_val=0, max_val=1)
            nc.all_engine_barrier()
            with nc.If(left_now != 0):
                for eng, program in programs:
                    program(eng)
                nc.all_engine_barrier()
                for s in sems:
                    nc.sync.sem_clear(s)
                nc.all_engine_barrier()
            with nc.Else():
                for eng in engines:
                    eng.nop()
            nc.all_engine_barrier()
        nc.all_engine_barrier()
    with nc.Else():
        for eng in engines:
            eng.nop()
    nc.all_engine_barrier()


def far_rest_phase(nc, name, g, far_key):
    slots = 8 * FAR_ROUNDS
    n_passes = -(-FAR_CHUNK // slots)
    n_groups = FAR_COLS // FAR_SUB
    with Phase(nc, name) as ph:
        sb, ps, sem = ph.sb, ph.ps, ph.sem
        taken = sb("taken", [P, EC // FAR_CHUNK, slots])
        node = sb("node", [P, FAR_COLS], I32)
        field = sb("field", [P, 2, FAR_COLS], I32)
        field_b = sb("field_b", [P, 2, FAR_COLS], BF16)
        iota_i, iota_b = sb("iota_i", [P, P], I32), sb("iota_b", [P, P], BF16)
        lo, hi = sb("lo", [P, 2, FAR_SUB, P], BF16), sb("hi", [P, 2, FAR_SUB, NB], BF16)
        last_slot, any_last = sb("last_slot", [P, 1]), sb("any_last", [P, 1])
        bank = ps("bank", [P, NB])
        setup = sem("setup")
        names = ("max", "cleared", "last_slot", "any_last", "more", "node", "field", "field_b", "lo", "hi", "summed", "count")
        max_s, cleared_s, last_s, any_s, more_s, node_s, field_s, fb_s, lo_s, hi_s, sum_s, count_s = in_pass = [sem(n) for n in names]

        with nc.Block() as block:
            @block.gpsimd
            def _(pool):
                pool.iota(iota_i[:], pattern=[[1, P]], base=0, channel_multiplier=0).then_inc(setup, 1)

            @block.vector
            def _(dve):
                dve.wait_ge(setup, 1)
                dve.tensor_copy(iota_b[:], iota_i[:]).then_inc(setup, 1)
                dve.wait_ge(setup, 2)

        def vector_program(dve):
            take_largest(dve, far_key, taken, FAR_CHUNK, FAR_ROUNDS, max_s, cleared_s)
            dve.tensor_reduce(last_slot[:], taken[:, :, slots - 1], AX.X, ALU.max).then_inc(last_s, 1)
            dve.tensor_scalar(node[:], taken[:, :, :].rearrange("p c s -> p (c s)"), -1.0, None, ALU.add).then_inc(node_s, 1)
            dve.wait_ge(node_s, 1)
            dve.tensor_scalar(field[:, 0], node[:], P - 1, None, ALU.bitwise_and).then_inc(field_s, 1)
            dve.tensor_scalar(field[:, 1], node[:], 7, None, ALU.arith_shift_right).then_inc(field_s, 1)
            dve.wait_ge(field_s, 2)
            dve.tensor_copy(field_b[:], field[:]).then_inc(fb_s, 1)
            dve.wait_ge(fb_s, 1)
            dve.sem_inc(sum_s, 2)
            with dve.Fori(0, n_groups // 2) as i:
                for k in range(2):
                    q = i * 2 + k
                    here = bass.ds(q * FAR_SUB, FAR_SUB)
                    dve.wait_ge(sum_s, q + 1)
                    dve.tensor_tensor(lo[:, k], bcast(iota_b[:], FAR_SUB), spread(field_b[:, 0, here], P), ALU.is_equal).then_inc(lo_s, 1)
                    dve.tensor_tensor(hi[:, k], bcast(iota_b[:, 0:NB], FAR_SUB), spread(field_b[:, 1, here], NB), ALU.is_equal).then_inc(hi_s, 1)
            dve.wait_ge(sum_s, n_groups + 3)
            dve.tensor_tensor(g.count[:], g.count[:], bank[:], ALU.add).then_inc(count_s, 1)
            dve.wait_ge(any_s, 1)
            dve.tensor_scalar(g.far_more[:], any_last[0:1], 0.0, None, ALU.is_gt).then_inc(more_s, 1)
            dve.wait_ge(more_s, 1)

        def tensor_program(pe):
            pe.matmul(bank[:], zero_b[:], zero_b[:, 0:NB], start=True, stop=False)
            with pe.Fori(0, n_groups // 2) as i:
                for k in range(2):
                    q = i * 2 + k
                    pe.wait_ge(lo_s, q + 1)
                    pe.wait_ge(hi_s, q + 1)
                    for c in range(FAR_SUB):
                        mm = pe.matmul(bank[:], lo[:, k, c], hi[:, k, c], start=False, stop=False)
                    mm.then_inc(sum_s, 1)
            pe.matmul(bank[:], zero_b[:], zero_b[:, 0:NB], start=False, stop=True).then_inc(sum_s, 1)

        zero_b = sb("zero_b", [P, P], BF16)
        nc.vector.memset(zero_b[:], 0.0)
        nc.all_engine_barrier()

        def pool_program(pool):
            pool.wait_ge(last_s, 1)
            pool.partition_all_reduce(any_last[:], last_slot[:], P, bass.bass_isa.ReduceOp.max).then_inc(any_s, 1)

        passes(nc, n_passes, in_pass, g.far_more[0:1, 0:1],
               [(nc.vector, vector_program), (nc.tensor, tensor_program), (nc.gpsimd, pool_program)])


def spread(ap, n):
    return ap.rearrange("p (g o) -> p g o", o=1).to_broadcast([ap.shape[0], ap.shape[1], n])


def near_rest_phase(nc, name, g, near_key):
    slots = 8 * REST_ROUNDS
    n_passes = -(-REST_CHUNK // slots)
    with Phase(nc, name) as ph:
        sb, ps, sem = ph.sb, ph.ps, ph.sem
        taken = sb("taken", [P, 4, slots])
        keys = taken[:, :, :].rearrange("p c s -> p (c s)")
        bits = keys.bitcast(I32)
        src_i, dst_i = sb("src_i", [P, REST_COLS], I32), sb("dst_i", [P, REST_COLS], I32)
        lo_i, hi_i = sb("lo_i", [P, REST_COLS], I32), sb("hi_i", [P, REST_COLS], I32)
        lo_f, hi_f, there = sb("lo_f", [P, REST_COLS]), sb("hi_f", [P, REST_COLS]), sb("there", [P, REST_COLS])
        rows_g, dst_g = sb("rows_g", [P, REST_COLS, TW]), sb("dst_g", [P, REST_COLS, HEADS])
        logit, bound = sb("logit", [P, REST_COLS, HEADS]), sb("bound", [P, REST_COLS, HEADS])
        val = sb("val", [P, REST_COLS, TW])
        iota_i, iota_f = sb("iota_i", [P, P], I32), sb("iota_f", [P, P])
        lo, rhs = sb("lo", [P, 2, P]), sb("rhs", [P, 2, NB, TW])
        zero = sb("zero", [P, 512])
        last_slot, any_last = sb("last_slot", [P, 1]), sb("any_last", [P, 1])
        bank = ps("bank", [P, 3, 512])
        setup = sem("setup")
        names = ("max", "cleared", "last_slot", "any_last", "more", "field", "field_f", "hi_m", "rows", "dsts",
                 "logit", "lrelu", "diff", "weight", "val", "lo", "rhs", "summed", "agg")
        (max_s, cleared_s, last_s, any_s, more_s, field_s, ff_s, him_s, rows_s, dsts_s, logit_s, lrelu_s, diff_s, weight_s,
         val_s, lo_s, rhs_s, sum_s, agg_s) = in_pass = [sem(n) for n in names]

        with nc.Block() as block:
            @block.gpsimd
            def _(pool):
                pool.iota(iota_i[:], pattern=[[1, P]], base=0, channel_multiplier=0).then_inc(setup, 1)
                pool.memset(zero[:], 0.0).then_inc(setup, 1)

            @block.vector
            def _(dve):
                dve.wait_ge(setup, 2)
                dve.tensor_copy(iota_f[:], iota_i[:]).then_inc(setup, 1)
                dve.wait_ge(setup, 3)

        def vector_program(dve):
            take_largest(dve, near_key, taken, REST_CHUNK, REST_ROUNDS, max_s, cleared_s)
            dve.tensor_scalar(src_i[:], bits, M - 1, None, ALU.bitwise_and).then_inc(field_s, 1)
            dve.tensor_scalar(dst_i[:], bits, 13, M - 1, ALU.logical_shift_right, ALU.bitwise_and).then_inc(field_s, 1)
            dve.tensor_scalar(lo_i[:], bits, 13, P - 1, ALU.logical_shift_right, ALU.bitwise_and).then_inc(field_s, 1)
            dve.tensor_scalar(hi_i[:], bits, 20, NB - 1, ALU.logical_shift_right, ALU.bitwise_and).then_inc(field_s, 1)
            dve.tensor_reduce(last_slot[:], taken[:, :, slots - 1], AX.X, ALU.max).then_inc(last_s, 1)
            dve.wait_ge(field_s, 4)
            dve.tensor_copy(lo_f[:], lo_i[:]).then_inc(ff_s, 1)
            dve.tensor_scalar(hi_f[:], hi_i[:], 1.0, None, ALU.add).then_inc(ff_s, 1)
            dve.wait_ge(ff_s, 2)
            dve.scalar_tensor_tensor(out=hi_f[:], in0=keys, scalar=0.0, in1=hi_f[:], op0=ALU.is_gt, op1=ALU.mult).then_inc(him_s, 1)
            dve.wait_ge(him_s, 1)
            dve.tensor_scalar(hi_f[:], hi_f[:], -1.0, None, ALU.add).then_inc(him_s, 1)
            dve.wait_ge(rows_s, 16 * REST_COLS)
            dve.wait_ge(dsts_s, 16 * REST_COLS)
            dve.tensor_tensor(logit[:], rows_g[:, :, HC:TW], dst_g[:], ALU.add).then_inc(logit_s, 1)
            dve.tensor_tensor(bound[:], dst_g[:], bcast(g.top[:], REST_COLS), ALU.add).then_inc(logit_s, 1)
            dve.wait_ge(logit_s, 2)
            for a in (logit, bound):
                dve.scalar_tensor_tensor(out=a[:], in0=a[:], scalar=0.2, in1=a[:], op0=ALU.mult, op1=ALU.max).then_inc(lrelu_s, 1)
            dve.wait_ge(lrelu_s, 2)
            dve.tensor_tensor(logit[:], logit[:], bound[:], ALU.subtract).then_inc(diff_s, 1)
            dve.wait_ge(weight_s, 1)
            for h in range(HEADS):
                dve.tensor_tensor(val[:, :, EXPERTS * h:EXPERTS * (h + 1)], rows_g[:, :, EXPERTS * h:EXPERTS * (h + 1)],
                                  val[:, :, HC + h:HC + h + 1].to_broadcast([P, REST_COLS, EXPERTS]), ALU.mult).then_inc(val_s, 1)
            dve.wait_ge(val_s, HEADS)
            dve.wait_ge(him_s, 2)
            dve.sem_inc(sum_s, 2)
            with dve.Fori(0, REST_COLS // 2) as i:
                for k in range(2):
                    q = i * 2 + k
                    dve.wait_ge(sum_s, q + 1)
                    dve.tensor_scalar(lo[:, k], iota_f[:], lo_f[:, bass.ds(q, 1)], None, ALU.is_equal).then_inc(lo_s, 1)
                    dve.scalar_tensor_tensor(out=rhs[:, k], in0=spread(iota_f[:, 0:NB], TW), scalar=hi_f[:, bass.ds(q, 1)],
                                             in1=val[:, bass.ds(q, 1), :].to_broadcast([P, NB, TW]),
                                             op0=ALU.is_equal, op1=ALU.mult).then_inc(rhs_s, 1)
            dve.wait_ge(sum_s, REST_COLS + 3)
            for k, (a, b) in enumerate(SPLITS):
                dve.tensor_tensor(g.agg[:, a:b, :], g.agg[:, a:b, :], bank[:, k, 0:(b - a) * TW].rearrange("p (n c) -> p n c", c=TW),
                                  ALU.add).then_inc(agg_s, 1)
            dve.wait_ge(any_s, 1)
            dve.tensor_scalar(g.near_more[:], any_last[0:1], 0.0, None, ALU.is_gt).then_inc(more_s, 1)
            dve.wait_ge(more_s, 1)

        def tensor_program(pe):
            for n, (a, b) in enumerate(SPLITS):
                pe.matmul(bank[:, n, 0:(b - a) * TW], zero[:, 0:P], zero[:, 0:(b - a) * TW], start=True, stop=False)
            with pe.Fori(0, REST_COLS // 2) as i:
                for k in range(2):
                    q = i * 2 + k
                    pe.wait_ge(lo_s, q + 1)
                    pe.wait_ge(rhs_s, q + 1)
                    for n, (a, b) in enumerate(SPLITS):
                        mm = pe.matmul(bank[:, n, 0:(b - a) * TW], lo[:, k], rhs[:, k, a:b].rearrange("p n c -> p (n c)"),
                                       start=False, stop=False)
                    mm.then_inc(sum_s, 1)
            for n, (a, b) in enumerate(SPLITS):
                mm = pe.matmul(bank[:, n, 0:(b - a) * TW], zero[:, 0:P], zero[:, 0:(b - a) * TW], start=False, stop=True)
            mm.then_inc(sum_s, 1)

        def scalar_program(act):
            act.wait_ge(diff_s, 1)
            act.activation(val[:, :, HC:TW], logit[:], ACT.Exp).then_inc(weight_s, 1)

        def pool_program(pool):
            pool.wait_ge(field_s, 4)
            pool.wait_ge(last_s, 1)
            pool.partition_all_reduce(any_last[:], last_slot[:], P, bass.bass_isa.ReduceOp.max).then_inc(any_s, 1)
            for q in range(REST_COLS):
                pool.indirect_dma_start(out=rows_g[:, q], out_offset=None, in_=g.table,
                                        in_offset=bass.IndirectOffsetOnAxis(ap=src_i[:, q:q + 1].bitcast(U32), axis=0)).then_inc(rows_s, 16)
                pool.indirect_dma_start(out=dst_g[:, q], out_offset=None, in_=g.dst_table,
                                        in_offset=bass.IndirectOffsetOnAxis(ap=dst_i[:, q:q + 1].bitcast(U32), axis=0)).then_inc(dsts_s, 16)
            pool.wait_ge(rows_s, 16 * REST_COLS)
            pool.wait_ge(dsts_s, 16 * REST_COLS)
            pool.dma_reset()

        passes(nc, n_passes, in_pass, g.near_more[0:1, 0:1],
               [(nc.vector, vector_program), (nc.tensor, tensor_program), (nc.scalar, scalar_program), (nc.gpsimd, pool_program)])


SPLITS = [(0, 25), (25, 50), (50, NB)]


def edges_phase(nc, name, g, near_key, far_key):
    NG = NEAR_GROUP
    with Phase(nc, name) as ph:
        sb, ps, sem = ph.sb, ph.ps, ph.sem
        near_taken, far_taken = sb("near_taken", [P, 1, NEAR_COLS]), sb("far_taken", [P, EC // FAR_CHUNK, 8 * FAR_ROUNDS])
        picks = near_key[:, EC:EC + PICKS].rearrange("p (c s) -> p c s", c=EC // PICK_CHUNK)
        near_keys = near_taken[:, 0]
        bits = near_keys.bitcast(I32)
        ends = sb("ends", [P, 2, NEAR_COLS], I32)
        lo_i, hi_i = sb("lo_i", [P, NEAR_COLS], I32), sb("hi_i", [P, NEAR_COLS], I32)
        lo_f, hi_f = sb("lo_f", [P, NEAR_COLS]), sb("hi_f", [P, NEAR_COLS])
        far_node, far_field = sb("far_node", [P, FAR_COLS], I32), sb("far_field", [P, 2, FAR_COLS], I32)
        far_field_b = sb("far_field_b", [P, 2, FAR_COLS], BF16)
        iota_i, iota_f, iota_b = sb("iota_i", [P, P], I32), sb("iota_f", [P, P]), sb("iota_b", [P, P], BF16)
        zero, zero_b = sb("zero", [P, 512]), sb("zero_b", [P, P], BF16)
        index = sb("index", [P, 2, 2, NG], I32)
        rows_g, dst_g = sb("rows_g", [P, 2, NG, TW]), sb("dst_g", [P, 2, NG, HEADS])
        logit, bound = sb("logit", [P, 2, NG, HEADS]), sb("bound", [P, 2, NG, HEADS])
        val = sb("val", [P, 2, NG, TW])
        lo, rhs = sb("lo", [P, 2, P]), sb("rhs", [P, 2, NB, TW])
        far_lo, far_hi = sb("far_lo", [P, 2, FAR_SUB, P], BF16), sb("far_hi", [P, 2, FAR_SUB, NB], BF16)
        full, any_full = sb("full", [P, 3]), sb("any_full", [P, 3])
        near_sum, far_sum = ps("near_sum", [P, 3, 512]), ps("far_sum", [P, NB])
        setup, pick_max, pick_cleared, near_max, near_cleared, far_max, far_cleared = (
            sem(n) for n in ("setup", "pick_max", "pick_cleared", "near_max", "near_cleared", "far_max", "far_cleared"))
        full_s, any_s, more_s, field_s, ff_s, him_s, node_s, far_field_s, fb_s = (
            sem(n) for n in ("full", "any", "more", "field", "ff", "him", "node", "far_field", "fb"))
        rows_s = [sem("rows0"), sem("rows1")]
        index_s, go_s, logit_s, lrelu_s, diff_s, weight_s, val_s = (sem(n) for n in ("index", "go", "logit", "lrelu", "diff", "weight", "val"))
        lo_s, rhs_s, near_sum_s, far_lo_s, far_hi_s, far_sum_s, done_s = (
            sem(n) for n in ("lo", "rhs", "near_sum", "far_lo", "far_hi", "far_sum", "done"))

        def groups(eng, step):
            with eng.Fori(0, GROUPS // 2 - 1) as i:
                step(i, 0, False)
                step(i, 1, False)
            step(GROUPS // 2 - 1, 0, False)
            step(GROUPS // 2 - 1, 1, True)

        order = []
        for c in range(NG):
            order.append(("near", c))
            if c < FAR_SUBS:
                order.append(("far", c))

        with nc.Block() as block:
            @block.gpsimd
            def _(pool):
                pool.iota(iota_i[:], pattern=[[1, P]], base=0, channel_multiplier=0).then_inc(setup, 1)
                pool.memset(zero[:], 0.0).then_inc(setup, 1)
                pool.memset(zero_b[:], 0.0).then_inc(setup, 1)

                def gather(i, k):
                    g_ = 2 * i + k
                    pool.wait_ge(index_s, g_ + 1)
                    if not (isinstance(i, int) and i == 0):
                        pool.wait_ge(val_s, HEADS * (g_ - 1))
                    pool.sem_inc(go_s, 1)
                    for q in range(NG):
                        for e, (out, table) in enumerate(((rows_g, g.table), (dst_g, g.dst_table))):
                            pool.indirect_dma_start(out=out[:, k, q], out_offset=None, in_=table,
                                                    in_offset=bass.IndirectOffsetOnAxis(ap=index[:, k, e, q:q + 1].bitcast(U32), axis=0)
                                                    ).then_inc(rows_s[k], 16)

                def values(i, k):
                    for h in range(HEADS):
                        pool.wait_ge(weight_s, 2 * i + k + 1)
                        pool.tensor_tensor(val[:, k, :, EXPERTS * h:EXPERTS * (h + 1)], rows_g[:, k, :, EXPERTS * h:EXPERTS * (h + 1)],
                                           val[:, k, :, HC + h:HC + h + 1].to_broadcast([P, NG, EXPERTS]), ALU.mult).then_inc(val_s, 1)

                def step(i, k, last):
                    if not last:
                        gather(i + k, 1 - k)
                    values(i, k)

                gather(0, 0)
                groups(pool, step)
                pool.wait_ge(full_s, 3)
                pool.partition_all_reduce(any_full[:], full[:], P, bass.bass_isa.ReduceOp.max).then_inc(any_s, 1)

            @block.scalar
            def _(act):
                def copy_index(i, k):
                    act.copy(index[:, k], ends[:, :, bass.ds((2 * i + k) * NG, NG)]).then_inc(index_s, 1)

                def step(i, k, last):
                    act.wait_ge(diff_s, 2 * i + k + 1)
                    act.wait_ge(near_sum_s, NG * (2 * i + k + 1))
                    act.activation(val[:, k, :, HC:TW], logit[:, k], ACT.Exp).then_inc(weight_s, 1)
                    if not (isinstance(i, int) and i == GROUPS // 2 - 1):
                        act.wait_ge(rows_s[k], 16 * 2 * NG * (i + 1))
                        copy_index(i + 1, k)

                act.wait_ge(field_s, 4)
                act.sem_inc(near_sum_s, 2 * NG)
                copy_index(0, 0)
                copy_index(0, 1)
                groups(act, step)

            @block.vector
            def _(dve):
                dve.wait_ge(setup, 3)
                dve.tensor_copy(iota_f[:], iota_i[:]).then_inc(setup, 1)
                dve.tensor_copy(iota_b[:], iota_i[:]).then_inc(setup, 1)
                dve.wait_ge(setup, 5)
                take_largest(dve, near_key[:, 0:EC], picks, PICK_CHUNK, PICK_ROUNDS, pick_max, pick_cleared)
                dve.tensor_reduce(full[:, 0:1], picks[:, :, 8 * PICK_ROUNDS - 1], AX.X, ALU.max).then_inc(full_s, 1)
                dve.wait_ge(full_s, 1)
                take_largest(dve, near_key[:, EC:EC + PICKS], near_taken, PICKS, NEAR_ROUNDS, near_max, near_cleared)
                dve.tensor_copy(full[:, 1:2], near_taken[:, 0, NEAR_COLS - 1:NEAR_COLS]).then_inc(full_s, 1)
                dve.tensor_scalar(ends[:, 0], bits, M - 1, None, ALU.bitwise_and).then_inc(field_s, 1)
                dve.tensor_scalar(ends[:, 1], bits, 13, M - 1, ALU.logical_shift_right, ALU.bitwise_and).then_inc(field_s, 1)
                dve.tensor_scalar(lo_i[:], bits, 13, P - 1, ALU.logical_shift_right, ALU.bitwise_and).then_inc(field_s, 1)
                dve.tensor_scalar(hi_i[:], bits, 20, NB - 1, ALU.logical_shift_right, ALU.bitwise_and).then_inc(field_s, 1)
                dve.wait_ge(field_s, 4)
                dve.tensor_copy(lo_f[:], lo_i[:]).then_inc(ff_s, 1)
                dve.tensor_scalar(hi_f[:], hi_i[:], 1.0, None, ALU.add).then_inc(ff_s, 1)
                dve.wait_ge(ff_s, 2)
                dve.scalar_tensor_tensor(out=hi_f[:], in0=near_keys, scalar=0.0, in1=hi_f[:], op0=ALU.is_gt, op1=ALU.mult).then_inc(him_s, 1)
                dve.wait_ge(him_s, 1)
                dve.tensor_scalar(hi_f[:], hi_f[:], -1.0, None, ALU.add).then_inc(him_s, 1)
                take_largest(dve, far_key[:, :], far_taken, FAR_CHUNK, FAR_ROUNDS, far_max, far_cleared)
                dve.tensor_reduce(full[:, 2:3], far_taken[:, :, 8 * FAR_ROUNDS - 1], AX.X, ALU.max).then_inc(full_s, 1)
                dve.tensor_scalar(far_node[:], far_taken[:, :, :].rearrange("p c s -> p (c s)"), -1.0, None, ALU.add).then_inc(node_s, 1)
                dve.wait_ge(node_s, 1)
                dve.tensor_scalar(far_field[:, 0], far_node[:], P - 1, None, ALU.bitwise_and).then_inc(far_field_s, 1)
                dve.tensor_scalar(far_field[:, 1], far_node[:], 7, None, ALU.arith_shift_right).then_inc(far_field_s, 1)
                dve.wait_ge(far_field_s, 2)
                dve.tensor_copy(far_field_b[:], far_field[:]).then_inc(fb_s, 1)
                dve.wait_ge(fb_s, 1)
                dve.wait_ge(him_s, 2)
                dve.sem_inc(far_sum_s, 2)

                def exponents(i, k):
                    dve.wait_ge(rows_s[k], 16 * 2 * NG * (i + 1))
                    if not (isinstance(i, int) and i == 0 and k == 0):
                        dve.wait_ge(weight_s, 2 * i + k)
                    dve.tensor_tensor(logit[:, k], rows_g[:, k, :, HC:TW], dst_g[:, k], ALU.add).then_inc(logit_s, 1)
                    dve.tensor_tensor(bound[:, k], dst_g[:, k], bcast(g.top[:], NG), ALU.add).then_inc(logit_s, 1)
                    dve.wait_ge(logit_s, 2 * (2 * i + k + 1))
                    for a in (logit, bound):
                        dve.scalar_tensor_tensor(out=a[:, k], in0=a[:, k], scalar=0.2, in1=a[:, k], op0=ALU.mult, op1=ALU.max).then_inc(lrelu_s, 1)
                    dve.wait_ge(lrelu_s, 2 * (2 * i + k + 1))
                    dve.tensor_tensor(logit[:, k], logit[:, k], bound[:, k], ALU.subtract).then_inc(diff_s, 1)

                def step(i, k, last):
                    g_ = 2 * i + k
                    dve.wait_ge(val_s, HEADS * (g_ + 1))
                    for kind, c in order:
                        if kind == "near":
                            q, turn = g_ * NG + c, (k * NG + c) % 2
                            dve.wait_ge(near_sum_s, q + 2 * NG - 1)
                            dve.tensor_scalar(lo[:, turn], iota_f[:], lo_f[:, bass.ds(q, 1)], None, ALU.is_equal).then_inc(lo_s, 1)
                            dve.scalar_tensor_tensor(out=rhs[:, turn], in0=spread(iota_f[:, 0:NB], TW), scalar=hi_f[:, bass.ds(q, 1)],
                                                     in1=val[:, k, c:c + 1, :].to_broadcast([P, NB, TW]),
                                                     op0=ALU.is_equal, op1=ALU.mult).then_inc(rhs_s, 1)
                        else:
                            q, turn = g_ * FAR_SUBS + c, (k * FAR_SUBS + c) % 2
                            here = bass.ds(q * FAR_SUB, FAR_SUB)
                            dve.wait_ge(far_sum_s, q + 1)
                            dve.tensor_tensor(far_lo[:, turn], bcast(iota_b[:], FAR_SUB), spread(far_field_b[:, 0, here], P), ALU.is_equal).then_inc(far_lo_s, 1)
                            dve.tensor_tensor(far_hi[:, turn], bcast(iota_b[:, 0:NB], FAR_SUB), spread(far_field_b[:, 1, here], NB),
                                              ALU.is_equal).then_inc(far_hi_s, 1)
                        if kind == "near" and c == NG - 4 and not last:
                            exponents(i + k, 1 - k)

                exponents(0, 0)
                groups(dve, step)
                dve.wait_ge(near_sum_s, NEAR_COLS + 2 * NG + 1)
                for k, (a, b) in enumerate(SPLITS):
                    dve.tensor_copy(g.agg[:, a:b, :], near_sum[:, k, 0:(b - a) * TW].rearrange("p (n c) -> p n c", c=TW)).then_inc(done_s, 1)
                dve.wait_ge(far_sum_s, FAR_COLS // FAR_SUB + 3)
                dve.tensor_copy(g.count[:], far_sum[:]).then_inc(done_s, 1)
                dve.wait_ge(any_s, 1)
                dve.tensor_scalar(g.far_more[:], any_full[0:1, 2:3], 0.0, None, ALU.is_gt).then_inc(more_s, 1)
                dve.tensor_tensor(full[0:1, 0:1], any_full[0:1, 0:1], any_full[0:1, 1:2], ALU.max).then_inc(more_s, 1)
                dve.wait_ge(more_s, 2)
                dve.tensor_scalar(g.near_more[:], full[0:1, 0:1], 0.0, None, ALU.is_gt).then_inc(more_s, 1)
                dve.wait_ge(more_s, 3)
                dve.wait_ge(done_s, 4)

            @block.tensor
            def _(pe):
                pe.wait_ge(setup, 3)
                for n, (a, b) in enumerate(SPLITS):
                    pe.matmul(near_sum[:, n, 0:(b - a) * TW], zero[:, 0:P], zero[:, 0:(b - a) * TW], start=True, stop=False)
                pe.matmul(far_sum[:], zero_b[:], zero_b[:, 0:NB], start=True, stop=False)

                def step(i, k, last):
                    g_ = 2 * i + k
                    for kind, c in order:
                        if kind == "near":
                            q, turn = g_ * NG + c, (k * NG + c) % 2
                            pe.wait_ge(lo_s, q + 1)
                            pe.wait_ge(rhs_s, q + 1)
                            for n, (a, b) in enumerate(SPLITS):
                                mm = pe.matmul(near_sum[:, n, 0:(b - a) * TW], lo[:, turn], rhs[:, turn, a:b].rearrange("p n c -> p (n c)"),
                                               start=False, stop=False)
                            mm.then_inc(near_sum_s, 1)
                        else:
                            q, turn = g_ * FAR_SUBS + c, (k * FAR_SUBS + c) % 2
                            pe.wait_ge(far_lo_s, q + 1)
                            pe.wait_ge(far_hi_s, q + 1)
                            for e in range(FAR_SUB):
                                mm = pe.matmul(far_sum[:], far_lo[:, turn, e], far_hi[:, turn, e], start=False, stop=False)
                            mm.then_inc(far_sum_s, 1)

                groups(pe, step)
                for n, (a, b) in enumerate(SPLITS):
                    mm = pe.matmul(near_sum[:, n, 0:(b - a) * TW], zero[:, 0:P], zero[:, 0:(b - a) * TW], start=False, stop=True)
                mm.then_inc(near_sum_s, 1)
                pe.matmul(far_sum[:], zero_b[:], zero_b[:, 0:NB], start=False, stop=True).then_inc(far_sum_s, 1)


def gate_phase(nc, name, w, g):
    with Phase(nc, name) as ph:
        sb, sem = ph.sb, ph.sem
        b_gat, ln_g, ln_b = sb("b_gat", [P, HC]), sb("ln_g", [P, HC]), sb("ln_b", [P, HC])
        loop, far, bound = (sb(n, [P, NB, HEADS]) for n in ("loop", "far", "bound"))
        den, s4, e4, t4, rank = (sb(n, [P, NB, HEADS]) for n in ("den", "s4", "e4", "t4", "rank"))
        tmp, a = sb("tmp", [P, NB, HC]), sb("a", [P, NB, HC])
        mu, var, m1 = sb("mu", [P, NB]), sb("var", [P, NB]), sb("m1", [P, NB])
        eps = sb("eps", [P, 1])
        loaded, consts, step, exp_in, exp_out, var_in, lnv_s, rstd_s, sh_in, sh_out = (
            sem(n) for n in ("loaded", "consts", "step", "exp_in", "exp_out", "var_in", "lnv", "rstd", "sh_in", "sh_out"))
        h = g.h[:, :, 0:HC]

        def col(t):
            return t.rearrange("p (n o) -> p n o", o=1)

        def heads(t):
            return t

        with nc.Block() as block:
            @block.sync
            def _(sp):
                for t, n in ((b_gat, "b_gat"), (ln_g, "ln_gamma"), (ln_b, "ln_beta")):
                    sp.dma_start(t[:], rows(w[n])).then_inc(loaded, 16)

            @block.gpsimd
            def _(pool):
                pool.memset(eps[:], 1e-5).then_inc(consts, 1)

            @block.scalar
            def _(act):
                act.wait_ge(consts, 1)
                act.wait_ge(exp_in, 1)
                act.activation(loop[:], loop[:], ACT.Exp).then_inc(exp_out, 1)
                act.activation(far[:], far[:], ACT.Exp).then_inc(exp_out, 1)
                act.wait_ge(var_in, 1)
                act.activation(var[:], var[:], ACT.Ln, bias=eps[:], scale=1.0 / HC).then_inc(lnv_s, 1)
                act.wait_ge(lnv_s, 1)
                act.activation(var[:], var[:], ACT.Exp, scale=-0.5).then_inc(rstd_s, 1)
                act.wait_ge(sh_in, 1)
                act.activation(e4[:], e4[:], ACT.Exp).then_inc(sh_out, 1)

            @block.vector
            def _(dve):
                done = [0]

                def then(ins, s=step):
                    ins.then_inc(step, 1)
                    done[0] += 1
                    dve.wait_ge(step, done[0])

                dve.wait_ge(loaded, 48)
                then(dve.tensor_tensor(loop[:], g.h[:, :, HC:TW], g.a_dst[:], ALU.add))
                then(dve.tensor_tensor(far[:], g.a_dst[:], bcast(g.last[:, HC:TW], NB), ALU.add))
                then(dve.tensor_tensor(bound[:], g.a_dst[:], bcast(g.top[:], NB), ALU.add))
                for t in (loop, far, bound):
                    then(dve.scalar_tensor_tensor(out=t[:], in0=t[:], scalar=0.2, in1=t[:], op0=ALU.mult, op1=ALU.max))
                then(dve.tensor_tensor(loop[:], loop[:], bound[:], ALU.subtract))
                then(dve.tensor_tensor(far[:], far[:], bound[:], ALU.subtract))
                dve.sem_inc(exp_in, 1)
                dve.wait_ge(exp_out, 2)
                then(dve.tensor_tensor(far[:], far[:], col(g.count[:]).to_broadcast([P, NB, HEADS]), ALU.mult))
                then(dve.tensor_tensor(den[:], g.agg[:, :, HC:TW], loop[:], ALU.add))
                then(dve.scalar_tensor_tensor(out=den[:], in0=den[:], scalar=1e-16, in1=far[:], op0=ALU.add, op1=ALU.add))
                then(dve.reciprocal(den[:], den[:]))
                for k in range(HEADS):
                    e = slice(EXPERTS * k, EXPERTS * (k + 1))
                    wide = [P, NB, EXPERTS]
                    then(dve.tensor_tensor(tmp[:, :, e], h[:, :, e], loop[:, :, k:k + 1].to_broadcast(wide), ALU.mult))
                    then(dve.tensor_tensor(a[:, :, e], g.agg[:, :, e], tmp[:, :, e], ALU.add))
                    then(dve.tensor_tensor(tmp[:, :, e], bcast(g.last[:, e], NB), far[:, :, k:k + 1].to_broadcast(wide), ALU.mult))
                    then(dve.tensor_tensor(a[:, :, e], a[:, :, e], tmp[:, :, e], ALU.add))
                    then(dve.tensor_tensor(a[:, :, e], a[:, :, e], den[:, :, k:k + 1].to_broadcast(wide), ALU.mult))
                then(dve.tensor_tensor(a[:], a[:], bcast(b_gat[:], NB), ALU.add))
                then(dve.tensor_reduce(mu[:], a[:], AX.X, ALU.add))
                then(dve.tensor_scalar(mu[:], mu[:], 1.0 / HC, None, ALU.mult))
                then(dve.tensor_tensor(a[:], a[:], col(mu[:]).to_broadcast([P, NB, HC]), ALU.subtract))
                then(dve.tensor_tensor(tmp[:], a[:], a[:], ALU.mult))
                then(dve.tensor_reduce(var[:], tmp[:], AX.X, ALU.add))
                dve.sem_inc(var_in, 1)
                dve.wait_ge(rstd_s, 1)
                then(dve.tensor_tensor(a[:], a[:], col(var[:]).to_broadcast([P, NB, HC]), ALU.mult))
                then(dve.tensor_tensor(a[:], a[:], bcast(ln_g[:], NB), ALU.mult))
                then(dve.tensor_tensor(a[:], a[:], bcast(ln_b[:], NB), ALU.add))
                then(dve.tensor_reduce(s4[:], a[:, :, :].rearrange("p n (h e) -> p n e h", h=HEADS), AX.X, ALU.add))
                then(dve.tensor_scalar(s4[:], s4[:], 1.0 / HEADS, None, ALU.mult))
                then(dve.memset(rank[:], 0.0))
                for j in range(EXPERTS):
                    for k in range(EXPERTS):
                        if j != k:
                            op = ALU.is_ge if j < k else ALU.is_gt
                            then(dve.tensor_tensor(m1[:], s4[:, :, j], s4[:, :, k], op))
                            then(dve.tensor_tensor(rank[:, :, k], rank[:, :, k], m1[:], ALU.add))
                then(dve.tensor_reduce(m1[:], s4[:], AX.X, ALU.max))
                then(dve.tensor_tensor(e4[:], s4[:], col(m1[:]).to_broadcast([P, NB, EXPERTS]), ALU.subtract))
                dve.sem_inc(sh_in, 1)
                dve.wait_ge(sh_out, 1)
                then(dve.scalar_tensor_tensor(out=e4[:], in0=rank[:], scalar=1.5, in1=e4[:], op0=ALU.is_lt, op1=ALU.mult))
                then(dve.tensor_reduce(m1[:], e4[:], AX.X, ALU.add))
                then(dve.reciprocal(m1[:], m1[:]))
                then(dve.tensor_tensor(g.gate[:], e4[:], col(m1[:]).to_broadcast([P, NB, EXPERTS]), ALU.mult))


def experts_phase(nc, name, w, g, x_in, x_out):
    with Phase(nc, name) as ph:
        sb, ps, sem = ph.sb, ph.ps, ph.sem
        w_1, w_2 = sb("w_1", [P, EXPERTS, KB, FE]), sb("w_2", [P, EXPERTS, FEB, C])
        b_1, b_2 = sb("b_1", [P, EXPERTS, FEB]), sb("b_2", [P, EXPERTS, C])
        ident = sb("ident", [P, P])
        tn, xt, xo = (sb(n, [P, 2, KB, T]) for n in ("tn", "xt", "xo"))
        gt = sb("gt", [P, 2, SUB, EXPERTS])
        hid = sb("hid", [P, 2, FEB, T])
        acc = sb("acc", [P, SUB, C])
        up = ps("up", [P, FEB, T])
        down = ps("down", [P, 2, 2, C])
        turned = ps("turned", [P, KB, T])
        weights_in, consts = sem("weights_in"), sem("consts")
        in_s, stored = [sem("in0"), sem("in1")], [sem("stored0"), sem("stored1")]
        free, gt_s, up_s, hid_s, down_s, bias_s, acc_s, turn_s, out_s = (
            sem(n) for n in ("free", "gt", "up", "hid", "down", "bias", "acc", "turn", "out"))
        E_ = EXPERTS
        with nc.Block() as block:
            @block.sync
            def _(sp):
                for e in range(E_):
                    sp.dma_start(w_1[:, e], w["W1"][e].rearrange("(k p) n -> p k n", p=P)).then_inc(weights_in, 16)
                    sp.dma_start(w_2[:, e], w["W2"][e].rearrange("(k p) n -> p k n", p=P)).then_inc(weights_in, 16)
                with nc.allow_non_contiguous_dma(reason="short vectors"):
                    sp.dma_start(b_1[:], w["b1"].rearrange("e (k p) -> p e k", p=P)).then_inc(weights_in, 16)
                sp.dma_start(b_2[:].rearrange("p e n -> p (e n)"), rows(w["b2"].rearrange("e n -> (e n)"))).then_inc(weights_in, 16)
                with sp.Fori(0, TI) as i:
                    for b in range(B):
                        s = i * B + b
                        at = bass.ds(i * T, T)
                        sp.wait_ge(out_s, s + 1)
                        sp.dma_start(tn[:, b], g.tn[b].rearrange("(k p) t -> p k t", p=P)[:, :, at]).then_inc(in_s[b], 16)
                        sp.dma_start(xt[:, b], x_in[b].rearrange("(k p) t -> p k t", p=P)[:, :, at]).then_inc(in_s[b], 16)

            @block.gpsimd
            def _(pool):
                pool.memset(ident[:], 0.0).then_inc(consts, 1)
                pool.wait_ge(consts, 1)
                pool.affine_select(out=ident[:], in_=ident[:], compare_op=ALU.not_equal, fill=1.0, base=0,
                                   pattern=[[-1, P]], channel_multiplier=1).then_inc(consts, 1)
                with pool.Fori(0, TI) as i:
                    for b in range(B):
                        s = i * B + b
                        pool.wait_ge(out_s, s + 3)
                        pool.dma_start(x_out[b].rearrange("(k p) t -> p k t", p=P)[:, :, bass.ds(i * T, T)], xo[:, b]).then_inc(stored[b], 16)
                        pool.wait_ge(stored[b], 16 * i + 16)
                        pool.sem_inc(free, 1)

            @block.tensor
            def _(pe):
                pe.wait_ge(weights_in, 16 * (2 * E_ + 2))
                pe.wait_ge(consts, 2)
                with pe.Fori(0, TI) as i:
                    for b in range(B):
                        s = i * B + b
                        pe.wait_ge(in_s[b], 32 * i + 32)
                        for e in range(E_ + 1):
                            if e < E_:
                                for f in range(FEB):
                                    pe.wait_ge(hid_s, FEB * (E_ * s + e - 1) + f + 1 + FEB)
                                    for kb in range(KB):
                                        mm = pe.matmul(up[:, f], w_1[:, e, kb, f * P:(f + 1) * P], tn[:, b, kb], start=kb == 0, stop=kb == KB - 1)
                                    mm.then_inc(up_s, 1)
                            if e > 0:
                                pe.wait_ge(hid_s, FEB * (E_ * s + e) + FEB)
                                for sub in range(SUB):
                                    n = SUB * (E_ * s + e - 1) + sub
                                    pe.wait_ge(acc_s, n - 1 + SUB)
                                    half = down[:, sub % 2, 0]
                                    for f in range(FEB):
                                        mm = pe.matmul(half, hid[:, (e - 1) % 2, f, sub * P:(sub + 1) * P], w_2[:, e - 1, f], start=f == 0, stop=f == FEB - 1)
                                    mm.then_inc(down_s, 1)
                        pe.wait_ge(acc_s, SUB * E_ * (s + 1) + SUB)
                        pe.wait_ge(out_s, s + 2)
                        for sub in range(SUB):
                            for kb in range(KB):
                                mm = pe.transpose(turned[:, kb, sub * P:(sub + 1) * P], acc[:, sub, kb * P:(kb + 1) * P], ident[:])
                        mm.then_inc(turn_s, 1)

            @block.scalar
            def _(act):
                act.wait_ge(weights_in, 16 * (2 * E_ + 2))
                act.sem_inc(hid_s, FEB)
                with act.Fori(0, TI) as i:
                    for b in range(B):
                        s = i * B + b
                        for e in range(E_):
                            act.wait_ge(down_s, SUB * (E_ * s + e - 2) + SUB + 2 * SUB)
                            for f in range(FEB):
                                act.wait_ge(up_s, FEB * (E_ * s + e) + f + 1)
                                act.activation(hid[:, e % 2, f], up[:, f], ACT.Gelu, bias=b_1[:, e, f:f + 1]).then_inc(hid_s, 1)

            @block.vector
            def _(dve):
                dve.wait_ge(weights_in, 16 * (2 * E_ + 2))
                dve.sem_inc(out_s, 2)
                dve.sem_inc(acc_s, SUB)
                dve.sem_inc(free, 2)
                dve.sem_inc(down_s, 2 * SUB)
                with dve.Fori(0, TI) as i:
                    for b in range(B):
                        s = i * B + b
                        dve.tensor_copy(gt[:, b], g.gate[:, bass.ds(i * SUB + b * (NB // B), SUB), :]).then_inc(gt_s, 1)
                        dve.wait_ge(gt_s, s + 1)
                        for sub in range(SUB):
                            for e in range(E_):
                                if e == 0:
                                    dve.tensor_scalar(acc[:, sub], b_2[:, e], gt[:, b, sub, e:e + 1], None, ALU.mult).then_inc(bias_s, 1)
                                else:
                                    dve.wait_ge(bias_s, E_ * (SUB * s + sub) + e)
                                    dve.scalar_tensor_tensor(out=acc[:, sub], in0=b_2[:, e], scalar=gt[:, b, sub, e:e + 1], in1=acc[:, sub],
                                                             op0=ALU.mult, op1=ALU.add).then_inc(bias_s, 1)
                        dve.wait_ge(bias_s, E_ * SUB * (s + 1))
                        for e in range(E_):
                            for sub in range(SUB):
                                n = SUB * (E_ * s + e) + sub
                                dve.wait_ge(down_s, n + 1 + 2 * SUB)
                                if e > 0:
                                    dve.wait_ge(acc_s, n - SUB + 1 + SUB)
                                dve.scalar_tensor_tensor(out=acc[:, sub], in0=down[:, sub % 2, 0], scalar=gt[:, b, sub, e:e + 1], in1=acc[:, sub],
                                                         op0=ALU.mult, op1=ALU.add).then_inc(acc_s, 1)
                        dve.wait_ge(turn_s, s + 1)
                        dve.wait_ge(in_s[b], 32 * i + 32)
                        dve.wait_ge(free, s + 1)
                        dve.tensor_tensor(xo[:, b], turned[:], xt[:, b], ALU.add).then_inc(out_s, 1)
TILE_OUT, TILE_IN, KERNEL = 4, 6, 3
NT = HW // TILE_OUT
TP = TILE_IN * TILE_IN
HALF_T = NT // 2
HALF_R = HW // 2
N_T = HALF_T * NT
ROWS = HALF_R + 2
WIDE = HW + 2


def kernel_points_phase(nc, name, w, points):
    with Phase(nc, name) as ph:
        sb, sem = ph.sb, ph.sem
        k9 = sb("k9", [P, KB, KERNEL, KERNEL, C])
        half = sb("half", [P, TILE_IN, KERNEL, C])
        mask = sb("mask", [P, 2, TILE_IN, C])
        s0, s1 = sb("s0", [P, TILE_IN, C]), sb("s1", [P, TILE_IN, C])
        loaded, mask_in, step, masked = sem("loaded"), [sem("mask_in0"), sem("mask_in1")], sem("step"), sem("masked")
        mask_d = w["mask"].rearrange("(k p) t u o -> p k t u o", p=P)
        k_d = w["weight"].rearrange("(k p) i j o -> p k (i j o)", p=P)
        chunks = [(kb, t) for kb in range(KB) for t in range(TILE_IN)]

        with nc.Block() as block:
            @block.sync
            def _(sp):
                for kb in range(KB):
                    sp.dma_start(k9[:, kb].rearrange("p i j o -> p (i j o)"), k_d[:, kb]).then_inc(loaded, 16)
                for n, (kb, t) in enumerate(chunks):
                    if n >= 2:
                        sp.wait_ge(masked, n - 1)
                    sp.dma_start(mask[:, n % 2], mask_d[:, kb, t]).then_inc(mask_in[n % 2], 16)

            @block.vector
            def _(dve):
                done = [0]

                def then(ins):
                    ins.then_inc(step, 1)
                    done[0] += 1
                    dve.wait_ge(step, done[0])

                def expand(w0, w1, w2, out, n):
                    a, b = s0[:, 0:n], s1[:, 0:n]
                    then(dve.tensor_scalar(out(0), w0, 0.25, None, ALU.mult))
                    then(dve.tensor_copy(out(5), w2))
                    then(dve.tensor_tensor(a, w0, w2, ALU.add))
                    for k, op in ((1, ALU.add), (2, ALU.subtract)):
                        then(dve.tensor_tensor(b, a, w1, op))
                        then(dve.tensor_scalar(out(k), b, -1.0 / 6, None, ALU.mult))
                    then(dve.scalar_tensor_tensor(out=a, in0=w0, scalar=0.25, in1=w2, op0=ALU.mult, op1=ALU.add))
                    for k, f in ((3, 0.5), (4, -0.5)):
                        then(dve.scalar_tensor_tensor(out=b, in0=w1, scalar=f, in1=a, op0=ALU.mult, op1=ALU.add))
                        then(dve.tensor_scalar(out(k), b, 1.0 / 6, None, ALU.mult))

                dve.wait_ge(loaded, 16 * KB)
                for kb in range(KB):
                    expand(k9[:, kb, 0], k9[:, kb, 1], k9[:, kb, 2], lambda t: half[:, t], KERNEL)
                    expand(half[:, :, 0], half[:, :, 1], half[:, :, 2], lambda u: points[:, kb, u], TILE_IN)
                    for t in range(TILE_IN):
                        n = kb * TILE_IN + t
                        dve.wait_ge(mask_in[n % 2], 16 * (n // 2) + 16)
                        then(dve.tensor_scalar(mask[:, n % 2], mask[:, n % 2], -1.0, 1.0, ALU.mult, ALU.add))
                        dve.tensor_tensor(points[:, kb, :, t], points[:, kb, :, t], mask[:, n % 2], ALU.mult).then_inc(masked, 1)
                dve.wait_ge(masked, KB * TILE_IN)


def winograd_phase(nc, name, w, points, x_in, x_out):
    with Phase(nc, name) as ph:
        sb, ps, sem = ph.sb, ph.ps, ph.sem
        ones_mean, eps, bias = sb("ones_mean", [P, P]), sb("eps", [P, 1]), sb("bias", [P, KB])
        v = sb("v", [P, KB, ROWS, WIDE])
        xt, xc, sq = (sb(n, [P, KB, T]) for n in ("xt", "xc", "sq"))
        lnv, rstd = sb("lnv", [P, T]), sb("rstd", [P, T])
        r = sb("r", [P, TILE_IN, HALF_T, WIDE])
        pts = sb("pts", [P, KB, TILE_IN, TILE_IN, N_T])
        prod = sb("prod", [P, TILE_IN, TILE_IN, N_T])
        s1 = sb("s1", [P, TILE_OUT, TILE_IN, N_T])
        y = sb("y", [P, HALF_R, HW])
        res = sb("res", [P, HALF_R * HW])
        tmp = [sb(f"tmp{k}", [P, TILE_IN * N_T]) for k in range(2)]
        bank = ps("bank", [P, 8, T])
        G4 = 4
        n_g = TP // G4
        consts, weights_in, x_loaded, res_in, stored, free = (sem(n) for n in ("consts", "weights_in", "x_loaded", "res_in", "stored", "free"))
        mean, cent, sqd, var, lns, rst, v_s, clean = (sem(n) for n in ("mean", "cent", "sqd", "var", "lns", "rst", "v", "clean"))
        rows_s, pts_s, prod_s, copied, out_s, step = (sem(n) for n in ("rows", "pts", "prod", "copied", "out", "step"))
        pieces = [[(0, 8), (8, 8), (16, 8), (24, 8), (32, 1)], [(31, 1), (32, 8), (40, 8), (48, 8), (56, 8)]]
        NP_ = len(pieces[0])
        n_steps = 2 * B
        x_px = x_in.rearrange("b (k p) t -> b p k t", p=P)
        o_px = x_out.rearrange("b (k p) t -> b p k t", p=P)

        with nc.Block() as block:
            @block.sync
            def _(sp):
                with nc.allow_non_contiguous_dma(reason="a short vector"):
                    sp.dma_start(bias[:], w["bias"].rearrange("(k p) -> p k", p=P)).then_inc(weights_in, 16)
                for s in range(n_steps):
                    b, h = s // 2, s % 2
                    for k, (row, n) in enumerate(pieces[h]):
                        q = s * NP_ + k
                        if q:
                            sp.wait_ge(cent, q)
                        sp.dma_start(xt[:, :, 0:n * HW], x_px[b, :, :, row * HW:(row + n) * HW]).then_inc(x_loaded, 16)
                    for ob in range(KB):
                        if s or ob:
                            sp.wait_ge(out_s, KB * s + ob)
                        sp.dma_start(res[:], x_px[b, :, ob, h * HALF_R * HW:(h + 1) * HALF_R * HW]).then_inc(res_in, 16)

            @block.gpsimd
            def _(pool):
                pool.memset(ones_mean[:], 1.0 / C).then_inc(consts, 1)
                pool.memset(eps[:], 1e-6).then_inc(consts, 1)
                pool.memset(v[:], 0.0).then_inc(consts, 1)
                for s in range(n_steps):
                    b, h = s // 2, s % 2
                    for ob in range(KB):
                        pool.wait_ge(out_s, KB * s + ob + 1)
                        pool.dma_start(o_px[b, :, ob, h * HALF_R * HW:(h + 1) * HALF_R * HW],
                                       y[:].rearrange("p r c -> p (r c)")).then_inc(stored, 16)
                pool.wait_ge(stored, 16 * KB * n_steps)

            @block.tensor
            def _(pe):
                pe.wait_ge(consts, 3)
                for s in range(n_steps):
                    for k, (row, n) in enumerate(pieces[s % 2]):
                        q = s * NP_ + k
                        w_ = n * HW
                        pe.wait_ge(x_loaded, 16 * q + 16)
                        for kb in range(KB):
                            mm = pe.matmul(bank[:, 6, 0:w_], ones_mean[:], xt[:, kb, 0:w_], start=kb == 0, stop=kb == KB - 1)
                        mm.then_inc(mean, 1)
                        pe.wait_ge(sqd, q + 1)
                        for kb in range(KB):
                            mm = pe.matmul(bank[:, 7, 0:w_], ones_mean[:], sq[:, kb, 0:w_], start=kb == 0, stop=kb == KB - 1)
                        mm.then_inc(var, 1)
                    pe.wait_ge(pts_s, 12 * KB * (s + 1))
                    for ob in range(KB):
                        for gr in range(n_g):
                            c = (s * KB + ob) * n_g + gr
                            if c >= 6:
                                pe.wait_ge(copied, c - 5)
                            for j in range(G4):
                                u, t = divmod(gr * G4 + j, TILE_IN)
                                for kb in range(KB):
                                    mm = pe.matmul(bank[:, c % 6, j * N_T:(j + 1) * N_T], points[:, kb, u, t, ob * P:(ob + 1) * P],
                                                   pts[:, kb, u, t], start=kb == 0, stop=kb == KB - 1)
                            mm.then_inc(prod_s, 1)

            @block.scalar
            def _(act):
                act.wait_ge(consts, 3)
                for s in range(n_steps):
                    for k, (row, n) in enumerate(pieces[s % 2]):
                        q = s * NP_ + k
                        w_ = n * HW
                        act.wait_ge(cent, q + 1)
                        act.activation(sq[:, :, 0:w_], xc[:, :, 0:w_], ACT.Square).then_inc(sqd, 1)
                        act.wait_ge(var, q + 1)
                        act.activation(lnv[:, 0:w_], bank[:, 7, 0:w_], ACT.Ln, bias=eps[:]).then_inc(lns, 1)
                        act.wait_ge(lns, q + 1)
                        act.activation(rstd[:, 0:w_], lnv[:, 0:w_], ACT.Exp, scale=-0.5).then_inc(rst, 1)
                    flat = prod[:].rearrange("p u t n -> p (u t n)")
                    for ob in range(KB):
                        if s or ob:
                            act.wait_ge(out_s, KB * s + ob)
                        for gr in range(n_g):
                            c = (s * KB + ob) * n_g + gr
                            act.wait_ge(prod_s, c + 1)
                            act.copy(flat[:, gr * G4 * N_T:(gr + 1) * G4 * N_T], bank[:, c % 6]).then_inc(copied, 1)

            @block.vector
            def _(dve):
                dve.wait_ge(consts, 3)
                dve.wait_ge(weights_in, 16)
                done = [0]

                def then(ins):
                    ins.then_inc(step, 1)
                    done[0] += 1
                    dve.wait_ge(step, done[0])

                def input_points(d, out, a, b, last):
                    then(dve.scalar_tensor_tensor(out=a, in0=d(2), scalar=-4.0, in1=d(4), op0=ALU.mult, op1=ALU.add))
                    then(dve.scalar_tensor_tensor(out=b, in0=d(1), scalar=-4.0, in1=d(3), op0=ALU.mult, op1=ALU.add))
                    dve.tensor_tensor(out(1), a, b, ALU.add).then_inc(last, 1)
                    dve.tensor_tensor(out(2), a, b, ALU.subtract).then_inc(last, 1)
                    dve.wait_ge(last, marks[last] + 2)
                    then(dve.tensor_tensor(a, d(4), d(2), ALU.subtract))
                    then(dve.tensor_tensor(b, d(3), d(1), ALU.subtract))
                    dve.scalar_tensor_tensor(out=out(3), in0=b, scalar=2.0, in1=a, op0=ALU.mult, op1=ALU.add).then_inc(last, 1)
                    dve.scalar_tensor_tensor(out=out(4), in0=b, scalar=-2.0, in1=a, op0=ALU.mult, op1=ALU.add).then_inc(last, 1)
                    dve.wait_ge(last, marks[last] + 4)
                    then(dve.scalar_tensor_tensor(out=a, in0=d(2), scalar=-5.0, in1=d(4), op0=ALU.mult, op1=ALU.add))
                    then(dve.scalar_tensor_tensor(out=b, in0=d(3), scalar=-5.0, in1=d(5), op0=ALU.mult, op1=ALU.add))
                    dve.scalar_tensor_tensor(out=out(0), in0=d(0), scalar=4.0, in1=a, op0=ALU.mult, op1=ALU.add).then_inc(last, 1)
                    dve.scalar_tensor_tensor(out=out(5), in0=d(1), scalar=4.0, in1=b, op0=ALU.mult, op1=ALU.add).then_inc(last, 1)
                    marks[last] += 6
                    dve.wait_ge(last, marks[last])

                def output_rows(m, out, a, b):
                    then(dve.tensor_tensor(a, m(1), m(2), ALU.add))
                    then(dve.tensor_tensor(b, m(3), m(4), ALU.add))
                    then(dve.tensor_tensor(out(0), a, b, ALU.add))
                    then(dve.tensor_tensor(out(0), out(0), m(0), ALU.add))
                    then(dve.tensor_scalar(b, b, 4.0, None, ALU.mult))
                    then(dve.tensor_tensor(out(2), a, b, ALU.add))
                    then(dve.tensor_tensor(a, m(1), m(2), ALU.subtract))
                    then(dve.tensor_tensor(b, m(3), m(4), ALU.subtract))
                    then(dve.tensor_scalar(b, b, 2.0, None, ALU.mult))
                    then(dve.tensor_tensor(out(1), a, b, ALU.add))
                    then(dve.tensor_tensor(a, a, m(5), ALU.add))
                    then(dve.tensor_scalar(b, b, 4.0, None, ALU.mult))
                    then(dve.tensor_tensor(out(3), a, b, ALU.add))

                marks = {rows_s: 0, pts_s: 0}
                for s in range(n_steps):
                    h = s % 2
                    if s:
                        border = 0 if h == 0 else ROWS - 1
                        then(dve.memset(v[:, :, border, :], 0.0))
                    for k, (row, n) in enumerate(pieces[h]):
                        q = s * NP_ + k
                        w_ = n * HW
                        at = row + 1 - h * HALF_R
                        if q:
                            dve.wait_ge(v_s, KB * q)
                        dve.wait_ge(mean, q + 1)
                        dve.wait_ge(x_loaded, 16 * q + 16)
                        dve.tensor_tensor(xc[:, :, 0:w_], xt[:, :, 0:w_], bcast(bank[:, 6, 0:w_], KB), ALU.subtract).then_inc(cent, 1)
                        dve.wait_ge(rst, q + 1)
                        dve.wait_ge(cent, q + 1)
                        for kb in range(KB):
                            dve.tensor_tensor(v[:, kb, at:at + n, 1:1 + HW], xc[:, kb, 0:w_].rearrange("p (r c) -> p r c", c=HW),
                                              rstd[:, 0:w_].rearrange("p (r c) -> p r c", c=HW), ALU.mult).then_inc(v_s, 1)
                    dve.wait_ge(v_s, KB * NP_ * (s + 1))
                    for kb in range(KB):
                        shape = dict(p=P)
                        n1, n2 = HALF_T * WIDE, TILE_IN * N_T
                        ta, tb = (t[:, 0:n1].rearrange("p (r c) -> p r c", c=WIDE) for t in tmp)
                        input_points(lambda i: v[:, kb, i:i + TILE_OUT * (HALF_T - 1) + 1:TILE_OUT, :], lambda t: r[:, t], ta, tb, rows_s)
                        ta, tb = (t[:, 0:n2].rearrange("p (r c) -> p r c", c=NT) for t in tmp)
                        rr = r[:].rearrange("p t h c -> p (t h) c")
                        pp = pts[:, kb].rearrange("p u t (h c) -> p u (t h) c", c=NT)
                        input_points(lambda j: rr[:, :, j:j + TILE_OUT * (NT - 1) + 1:TILE_OUT], lambda u: pp[:, u], ta, tb, pts_s)
                        dve.sem_inc(pts_s, 6)
                        marks[pts_s] += 6
                    for ob in range(KB):
                        dve.wait_ge(copied, ((s * KB) + ob + 1) * n_g)
                        ta, tb = (t[:, 0:TILE_IN * N_T].rearrange("p (u n) -> p u n", n=N_T) for t in tmp)
                        output_rows(lambda t: prod[:, :, t], lambda p: s1[:, p], ta, tb)
                        if s or ob:
                            dve.wait_ge(stored, 16 * (KB * s + ob))
                        ta, tb = (t[:, 0:TILE_OUT * N_T].rearrange("p (q h c) -> p q h c", q=TILE_OUT, c=NT) for t in tmp)
                        yv = y[:].rearrange("p (h a) (c q) -> p a h c q", a=TILE_OUT, q=TILE_OUT)
                        output_rows(lambda u: s1[:, :, u].rearrange("p a (h c) -> p a h c", c=NT), lambda q: yv[:, :, :, :, q], ta, tb)
                        dve.wait_ge(res_in, 16 * (KB * s + ob) + 16)
                        dve.scalar_tensor_tensor(out=y[:].rearrange("p r c -> p (r c)"), in0=y[:].rearrange("p r c -> p (r c)"),
                                                 scalar=bias[:, ob:ob + 1], in1=res[:], op0=ALU.add, op1=ALU.add).then_inc(out_s, 1)


def graph_experts(nc, name, w, x_in, x_out):
    with ExitStack() as ctx:
        g = Graph(nc, ctx, name)
        features_phase(nc, f"{name}_features", w, g, x_in)
        with nc.sbuf_tensor(f"{name}_near_key", [P, EC + PICKS], F32) as near_key, nc.sbuf_tensor(f"{name}_far_key", [P, EC], F32) as far_key:
            keys_phase(nc, f"{name}_keys", w["edge_index"], near_key, far_key)
            edges_phase(nc, f"{name}_edges", g, near_key, far_key)
            far_rest_phase(nc, f"{name}_far_rest", g, far_key)
            near_rest_phase(nc, f"{name}_near_rest", g, near_key)
        gate_phase(nc, f"{name}_gate", w, g)
        experts_phase(nc, f"{name}_experts", w, g, x_in, x_out)


def build(nc, a, out):
    x1, x2, x3 = (nc.dram_tensor(n, (B, C, L), F32, kind="Internal").ap() for n in ("x1", "x2", "x3"))

    def layer(prefix):
        return {k[len(prefix):]: v for k, v in a.items() if k.startswith(prefix)}

    mamba_phase(nc, layer("L0_conv_"), a["x"], x1)
    graph_experts(nc, "g0", layer("L0_ffn_"), x1, x2)
    conv = layer("L1_conv_")
    with nc.sbuf_tensor("points", [P, KB, TILE_IN, TILE_IN, C], F32) as points:
        kernel_points_phase(nc, "kernels", conv, points)
        winograd_phase(nc, "winograd", conv, points, x2, x3)
    graph_experts(nc, "g1", layer("L1_ffn_"), x3, out)


TRANSPOSED = ("W_in", "W_xp", "W_dt", "W_out", "W1", "W2")


def kernel(**inputs):
    import concourse.bacc as _bacc
    from concourse.bass_utils import run_bass_kernel_spmd as _run

    laid = {}
    for name, value in inputs.items():
        v = np.asarray(value)
        if name == "x":
            v = v.reshape(B, C, L)
        elif name.startswith("L0_conv_") and name[8:] in TRANSPOSED:
            name, v = name + "T", v.T
        elif name in ("L1_conv_weight", "L1_conv_mask"):
            v = v.transpose(1, 2, 3, 0)
        laid[name] = np.ascontiguousarray(v)

    nc = _bacc.Bacc("TRN2", target_bir_lowering=False, num_devices=1)
    arrays, aps = {}, {}
    for name, v in laid.items():
        arrays[f"in_{name}"] = v
        aps[name] = nc.dram_tensor(f"in_{name}", v.shape, mybir.dt.from_np(v.dtype), kind="ExternalInput").ap()
    out = nc.dram_tensor("out", (B, C, L), F32, kind="ExternalOutput").ap()
    build(nc, aps, out)
    r = _run(nc, [arrays], core_ids=[0])
    return r.results[0]["out"].reshape(B, C, HW, HW)
```

```python
from contextlib import ExitStack

import numpy as np
import concourse.bass as bass
from concourse import mybir

F32 = mybir.dt.float32
BF16 = mybir.dt.bfloat16
I32 = mybir.dt.int32
U32 = mybir.dt.uint32
ALU = mybir.AluOpType
ACT = mybir.ActivationFunctionType
AX = mybir.AxisListType

P = 128
B, C, HW = 2, 256, 64
L = HW * HW
M = B * L
KB = C // P
T = 512
TI = L // T
DI, NS, R = 512, 16, 16
MB = DI // P
FF = 4 * C
FB = FF // P


class Phase:

    def __init__(self, nc, name):
        self.nc, self.name, self.ctx = nc, name, ExitStack()
        self.sems = []

    def __enter__(self):
        return self

    def sb(self, name, shape, dt=F32):
        return self.ctx.enter_context(self.nc.sbuf_tensor(f"{self.name}_{name}", shape, dt))

    def ps(self, name, shape, dt=F32):
        return self.ctx.enter_context(self.nc.psum_tensor(f"{self.name}_{name}", shape, dt))

    def sem(self, name):
        s = self.nc.alloc_semaphore(name=f"{self.name}_{name}")
        self.sems.append(s)
        return s

    def __exit__(self, *exc):
        if exc[0] is None:
            self.nc.all_engine_barrier()
            self.nc.gpsimd.dma_reset()
            self.nc.all_engine_barrier()
            self.nc.clear_and_free_semaphores(self.sems)
            self.nc.all_engine_barrier()
        self.ctx.close()


def bcast(ap, n):
    return ap.rearrange("p (o t) -> p o t", o=1).to_broadcast([ap.shape[0], n, ap.shape[1]])


def tiles(eng, step):
    step(0, 0, 0, True, False)
    with eng.Fori(0, TI - 1) as i:
        step(i * 2 + 1, i, 1, False, False)
        step(i * 2 + 2, i + 1, 0, False, False)
    step(B * TI - 1, TI - 1, 1, False, True)


def after(i, b):
    return (i, 1) if b == 0 else (i + 1, 0)


def ahead_of(i, b):
    return (i, 0) if b == 1 else (i - 1, 1)


def mamba_phase(nc, w, x_in, x_out):
    LAST = B * TI - 1
    HF = FB // 2
    RW = R + 2 * NS
    with Phase(nc, "mamba") as ph:
        sb, ps, sem = ph.sb, ph.ps, ph.sem
        w_in = sb("w_in", [P, KB, 2 * DI])
        w_xp = sb("w_xp", [P, MB, RW])
        w_dt = sb("w_dt", [R, DI])
        w_out = sb("w_out", [P, MB, C])
        w_1 = sb("w_1", [P, KB, FF])
        w_2 = sb("w_2", [P, FB, C])
        gamma, beta = sb("gamma", [P, KB]), sb("beta", [P, KB])
        conv_w, conv_b = sb("conv_w", [P, MB, 4]), sb("conv_b", [P, MB])
        b_dt, d_skip = sb("b_dt", [P, MB]), sb("d_skip", [P, MB])
        b_1, b_2 = sb("b_1", [P, FB]), sb("b_2", [P, KB])
        a_neg, a_log = sb("a_neg", [P, MB, NS]), sb("a_log", [P, MB, NS])
        ones_mean, ident = sb("ones_mean", [P, P]), sb("ident", [P, P])
        eps_c, eps_n, one = sb("eps_c", [P, 1]), sb("eps_n", [P, 1]), sb("one", [P, 1])
        xt, yn = (sb(n, [P, B, KB, T]) for n in ("xt", "yn"))
        lnb = sb("lnb", [P, 2 * KB, T])
        xc, v = lnb[:, 0:KB], lnb[:, KB:2 * KB]
        r_dt = lnb
        sq, y2, res = (sb(n, [P, KB, T]) for n in ("sq", "y2", "res"))
        rstd = sb("rstd", [P, T])
        xm = sb("xm", [P, MB, T + 3])
        tail = sb("tail", [P, B, MB, 3])
        zs, dt, dtu, y = (sb(n, [P, B, MB, T]) for n in ("zs", "dt", "dtu", "y"))
        cx, u = (sb(n, [P, MB, T]) for n in ("cx", "u"))
        ea = cx
        prj = sb("prj", [RW, B, T])
        dA, hb = (sb(n, [P, 2, MB, T]) for n in ("dA", "hb"))
        g1 = sb("g1", [P, HF, T])
        state = sb("state", [P, B, NS, MB])
        bank = ps("bank", [P, 8, T])
        B_BANK, C_BANK, LN_BANK, TURN, ACC = 0, 1, 3, 4, 6

        DT_BANKS = (TURN, TURN + 1, LN_BANK, TURN)

        weights_in, a_exp, consts = sem("weights_in"), sem("a_exp"), sem("consts")
        x_in_s, res_in, x_stored, out_free = [sem("x_in0"), sem("x_in1")], sem("res_in"), sem("x_stored"), sem("out_free")
        mean, cent, sqd, var, lns, rst, nrm = ([sem(f"{n}{k}") for k in range(2)] for n in ("mean", "cent", "sqd", "var", "lns", "rst", "nrm"))
        yn_s, xz_s, xm_s, tails_s, conv_s, tail_s, u_s = (sem(n) for n in ("yn", "xz", "xm", "tails", "conv", "tail", "u"))
        proj_s, prj_s, dtp_s, z_s, dte_s, dt_s, dtu_s, yi_s = (sem(n) for n in ("proj", "prj", "dtp", "z", "dte", "dt", "dtu", "yi"))
        bc_s, dA_s, dbu_s, scan_s, save_s, hc_s, yacc_s = (sem(n) for n in ("bc", "dA", "dbu", "scan", "save", "hc", "yacc"))
        ym_s, wo_s, y2_s, res_s, up_s, g1_s, dn_s, x1_s = (sem(n) for n in ("ym", "wo", "y2", "res", "up", "g1", "dn", "x1"))

        loads = [(w_in, w["W_inT"].rearrange("(k p) n -> p k n", p=P)), (w_xp, w["W_xpT"].rearrange("(k p) n -> p k n", p=P)),
                 (w_dt, w["W_dtT"]), (w_out, w["W_outT"].rearrange("(k p) n -> p k n", p=P)),
                 (w_1, w["W1T"].rearrange("(k p) n -> p k n", p=P)), (w_2, w["W2T"].rearrange("(k p) n -> p k n", p=P)),
                 (conv_w, w["conv_w"].rearrange("(k p) o n -> p k (o n)", p=P)),
                 (a_log, w["A_log"].rearrange("(k p) n -> p k n", p=P))]
        vectors = [(gamma, "gamma"), (beta, "beta"), (conv_b, "conv_b"), (b_dt, "b_dt"), (d_skip, "D"), (b_1, "b1"), (b_2, "b2")]
        n_loads = len(loads) + len(vectors)

        def is_first(q):
            return isinstance(q, int) and q == 0

        with nc.Block() as block:
            @block.sync
            def _(sp):
                def load(i, b):
                    sp.dma_start(xt[:, b], x_in[b].rearrange("(k p) t -> p k t", p=P)[:, :, bass.ds(i * T, T)]).then_inc(x_in_s[b], 16)

                load(0, 0)
                for tile, src in loads:
                    sp.dma_start(tile[:], src).then_inc(weights_in, 16)
                with nc.allow_non_contiguous_dma(reason="short vectors"):
                    for tile, name in vectors:
                        sp.dma_start(tile[:], w[name].rearrange("(k p) -> p k", p=P)).then_inc(weights_in, 16)
                sp.sem_inc(out_free, 1)

                def load_residual(i, b):
                    sp.dma_start(res[:], x_in[b].rearrange("(k p) t -> p k t", p=P)[:, :, bass.ds(i * T, T)]).then_inc(res_in, 16)

                def store(q, i, b):
                    sp.wait_ge(x1_s, KB * q + 2 * KB)
                    sp.dma_start(x_out[b].rearrange("(k p) t -> p k t", p=P)[:, :, bass.ds(i * T, T)], y2[:]).then_inc(x_stored, 16)
                    sp.wait_ge(x_stored, 16 * q + 16)
                    sp.sem_inc(out_free, 1)

                def step(s, i, b, first, last):
                    if not last:
                        if not first:
                            sp.wait_ge(cent[0], s)
                        load(*after(i, b))
                    if not first:
                        load_residual(*ahead_of(i, b))
                        store(s - 1, *ahead_of(i, b))

                tiles(sp, step)
                load_residual(TI - 1, 1)
                store(LAST, TI - 1, 1)

            @block.gpsimd
            def _(pool):
                for k, (t, value) in enumerate(((ident, 0.0), (ones_mean, 1.0 / C), (tail, 0.0), (state, 0.0), (eps_c, 1e-6), (eps_n, 1e-5),
                                                (one, 1.0))):
                    pool.memset(t[:], value).then_inc(consts, 1)
                pool.wait_ge(consts, 7)
                pool.affine_select(out=ident[:], in_=ident[:], compare_op=ALU.not_equal, fill=1.0, base=0,
                                   pattern=[[-1, P]], channel_multiplier=1).then_inc(consts, 1)
                pool.sem_inc(yacc_s, 1)

                def times_u(q, b):
                    pool.wait_ge(dt_s, q + 1)
                    pool.tensor_tensor(dtu[:, b], dt[:, b], u[:], ALU.mult).then_inc(dtu_s, 1)

                def gate(q, b):
                    pool.wait_ge(yacc_s, NS * (q + 1) + 1)
                    pool.wait_ge(xm_s, 2 * MB * (q + 1))
                    pool.tensor_tensor(y[:, b], y[:, b], zs[:, b], ALU.mult).then_inc(ym_s, 1)

                def add_residual(q):
                    pool.wait_ge(y2_s, q + 1)
                    pool.wait_ge(res_in, 16 * q + 16)
                    pool.tensor_tensor(res[:], y2[:], res[:], ALU.add).then_inc(res_s, 1)

                def step(s, i, b, first, last):
                    if not first:
                        gate(s - 1, 1 - b)
                    pool.wait_ge(yi_s, MB * (s + 1))
                    for n in range(NS):
                        pool.wait_ge(hc_s, s * NS + n + 1)
                        pool.wait_ge(yacc_s, s * NS + n + 1)
                        pool.tensor_tensor(y[:, b], y[:, b], hb[:, n % 2], ALU.add).then_inc(yacc_s, 1)
                        if n == 3 and not first:
                            add_residual(s - 1)
                        if n == 14 and not last:
                            times_u(s + 1, 1 - b)

                times_u(0, 0)
                tiles(pool, step)
                gate(LAST, 1)
                add_residual(LAST)

            @block.tensor
            def _(pe):
                pe.wait_ge(consts, 8)

                def mean_of(q, i, b, k):
                    if k == 0:
                        pe.wait_ge(x_in_s[b], 16 * i + 16)
                    else:
                        pe.wait_ge(nrm[0], q + 1)
                    for kb in range(KB):
                        mm = pe.matmul(bank[:, LN_BANK], ones_mean[:], xt[:, b, kb] if k == 0 else v[:, kb], start=kb == 0, stop=kb == KB - 1)
                    mm.then_inc(mean[k], 1)

                def var_of(q, k):
                    pe.wait_ge(sqd[k], q + 1)
                    for kb in range(KB):
                        mm = pe.matmul(bank[:, LN_BANK], ones_mean[:], sq[:, kb], start=kb == 0, stop=kb == KB - 1)
                    mm.then_inc(var[k], 1)

                def xz(q, b, m0):
                    pe.wait_ge(yn_s, KB * (q + 1))
                    for m in range(m0, m0 + MB):
                        if m0 == 0 and m < 2:
                            if not is_first(q):
                                pe.wait_ge(g1_s, FB * (q - 1) + HF)
                                pe.wait_ge(z_s, MB * q)
                        else:
                            pe.wait_ge(xm_s, 2 * MB * q + m - 1)
                        for kb in range(KB):
                            mm = pe.matmul(bank[:, TURN + m % 2], w_in[:, kb, m * P:(m + 1) * P], yn[:, b, kb], start=kb == 0, stop=kb == KB - 1)
                        mm.then_inc(xz_s, 1)

                def project(q, b):
                    pe.wait_ge(u_s, MB * (q + 1))
                    pe.wait_ge(xm_s, 2 * MB * (q + 1))
                    if not is_first(q):
                        pe.wait_ge(g1_s, FB * q)
                    for m in range(MB):
                        mm = pe.matmul(bank[0:RW, TURN], w_xp[:, m, :], u[:, m], start=m == 0, stop=m == MB - 1)
                    mm.then_inc(proj_s, 1)

                def dt_blocks(q, b):
                    pe.wait_ge(prj_s, q + 1)
                    for m in range(MB):
                        if m == 3:
                            pe.wait_ge(z_s, MB * q + 1)
                        mm = pe.matmul(bank[:, DT_BANKS[m]], w_dt[:, m * P:(m + 1) * P], prj[0:R, b], start=True, stop=True)
                        mm.then_inc(dtp_s, 1)

                def spread_bc(s, b, n):
                    g = s * NS + n
                    if n == 0:
                        pe.wait_ge(prj_s, s + 1)
                    pe.wait_ge(dbu_s, g + 1)
                    for c, at in ((0, B_BANK), (1, C_BANK + n % 2)):
                        k = R + c * NS + n
                        mm = pe.matmul(bank[:, at], ident[0:RW, k:k + 1].to_broadcast([RW, P]), prj[:, b], start=True, stop=True)
                    mm.then_inc(bc_s, 1)

                def out_block(q, b, ob):
                    pe.wait_ge(ym_s, q + 1)
                    pe.wait_ge(x1_s, KB * (q + 1))
                    for m in range(MB):
                        mm = pe.matmul(bank[:, ACC + ob], w_out[:, m, ob * P:(ob + 1) * P], y[:, b, m], start=m == 0, stop=m == MB - 1)
                    mm.then_inc(wo_s, 1)

                def up_blocks(q, f0, dts, xzs):
                    pe.wait_ge(y2_s, q + 1)
                    for f in range(f0, f0 + 2):
                        if f < 2:
                            pe.wait_ge(z_s, MB * dts)
                        elif f // 2 == 2 and xzs is not None:
                            pe.wait_ge(xm_s, 2 * MB * xzs)
                        else:
                            pe.wait_ge(g1_s, FB * q + f - 1 + FB)
                        for kb in range(KB):
                            mm = pe.matmul(bank[:, TURN + f % 2], w_1[:, kb, f * P:(f + 1) * P], y2[:, kb], start=kb == 0, stop=kb == KB - 1)
                        mm.then_inc(up_s, 1)

                def down_block(q, h, ob):
                    pe.wait_ge(g1_s, FB * q + HF * (h + 1) + FB)
                    for f in range(HF):
                        mm = pe.matmul(bank[:, ACC + ob], w_2[:, h * HF + f, ob * P:(ob + 1) * P], g1[:, f],
                                       start=h == 0 and f == 0, stop=h == 1 and f == HF - 1)
                    if ob == KB - 1:
                        mm.then_inc(dn_s, 1)

                def step(s, i, b, first, last):
                    o = 1 - b
                    for n in range(NS):
                        if n < NS - 1:
                            spread_bc(s, b, n + 1)
                        elif not last:
                            spread_bc(s + 1, o, 0)
                        if not last:
                            if n in (0, 3):
                                mean_of(s + 1, *after(i, b), n // 3)
                            if n in (1, 4):
                                var_of(s + 1, n // 3)
                            if n in (6, 7):
                                xz(s + 1, o, MB * (n - 6))
                        if not first:
                            if n in (0, 1):
                                out_block(s - 1, o, n)
                            if n in (3, 4, 8, 9):
                                up_blocks(s - 1, {3: 0, 4: 2, 8: 4, 9: 6}[n], s + 1, None if last else s + 2)
                            if n == 5:
                                down_block(s - 1, 0, 0)
                                down_block(s - 1, 0, 1)
                            if n in (13, 14):
                                down_block(s - 1, 1, n - 13)
                        if n == 10 and not last:
                            project(s + 1, o)
                        if n == 11 and not last:
                            dt_blocks(s + 1, o)

                for k in range(2):
                    mean_of(0, 0, 0, k)
                    var_of(0, k)
                pe.wait_ge(weights_in, 16 * n_loads)
                xz(0, 0, 0)
                xz(0, 0, MB)
                project(0, 0)
                dt_blocks(0, 0)
                spread_bc(0, 0, 0)
                tiles(pe, step)
                for ob in range(KB):
                    out_block(LAST, 1, ob)
                for h in range(2):
                    for f0 in (HF * h, HF * h + 2):
                        up_blocks(LAST, f0, LAST + 1, None)
                    for ob in range(KB):
                        down_block(LAST, h, ob)

            @block.scalar
            def _(act):
                act.sem_inc(g1_s, FB)
                act.wait_ge(consts, 8)

                def square(q, k):
                    act.wait_ge(cent[k], q + 1)
                    act.activation(sq[:], xc[:], ACT.Square).then_inc(sqd[k], 1)

                def root(q, k):
                    act.wait_ge(var[k], q + 1)
                    act.wait_ge(nrm[1 - k], q + 1)
                    act.activation(rstd[:], bank[:, LN_BANK], ACT.Ln, bias=(eps_c if k == 0 else eps_n)[:]).then_inc(lns[k], 1)
                    act.wait_ge(lns[k], q + 1)
                    act.activation(rstd[:], rstd[:], ACT.Exp, scale=-0.5).then_inc(rst[k], 1)

                def affine(q, b):
                    act.wait_ge(nrm[1], q + 2)
                    for kb in range(KB):
                        act.activation(yn[:, b, kb], v[:, kb], ACT.Identity, scale=gamma[:, kb:kb + 1], bias=beta[:, kb:kb + 1]).then_inc(yn_s, 1)

                def take_xm(q, b):
                    act.wait_ge(tail_s, q + 1)
                    act.copy(xm[:, :, 0:3], tail[:, b]).then_inc(tails_s, 1)
                    for m in range(MB):
                        act.wait_ge(xz_s, 2 * MB * q + m + 1)
                        act.copy(xm[:, m, 3:3 + T], bank[:, TURN + m % 2]).then_inc(xm_s, 1)

                def take_z(q, b):
                    for m in range(MB):
                        act.wait_ge(xz_s, 2 * MB * q + MB + m + 1)
                        act.activation(zs[:, b, m], bank[:, TURN + m % 2], ACT.Silu).then_inc(xm_s, 1)

                def take_u(q):
                    for m in range(MB):
                        act.wait_ge(conv_s, 4 * MB * q + 3 * MB + m + 1)
                        act.activation(u[:, m], cx[:, m], ACT.Silu, bias=conv_b[:, m:m + 1]).then_inc(u_s, 1)

                def take_prj(q, b):
                    act.wait_ge(proj_s, q + 1)
                    act.copy(prj[:, b], bank[0:RW, TURN]).then_inc(prj_s, 1)
                    act.wait_ge(u_s, MB * (q + 1))
                    for m in range(MB):
                        act.activation(y[:, b, m], u[:, m], ACT.Copy, scale=d_skip[:, m:m + 1]).then_inc(yi_s, 1)

                def softplus(q, part):
                    if part == 0:
                        for m in range(MB):
                            act.wait_ge(dtp_s, MB * q + m + 1)
                            act.activation(r_dt[:, m], bank[:, DT_BANKS[m]], ACT.Identity, bias=b_dt[:, m:m + 1]).then_inc(z_s, 1)
                        act.wait_ge(z_s, MB * (q + 1))
                        act.activation(ea[:], r_dt[:], ACT.Abs).then_inc(dte_s, 1)
                    if part == 1:
                        act.wait_ge(dte_s, 3 * q + 1)
                        act.activation(ea[:], ea[:], ACT.Exp, scale=-1.0).then_inc(dte_s, 1)
                    if part == 2:
                        act.wait_ge(dte_s, 3 * q + 2)
                        act.activation(ea[:], ea[:], ACT.Ln, bias=one[:]).then_inc(dte_s, 1)

                def decay(s, b, n):
                    if n == 0:
                        act.wait_ge(dt_s, s + 1)
                    act.wait_ge(scan_s, MB * (s * NS + n - 1) + 2 * MB)
                    for m in range(MB):
                        act.activation(dA[:, n % 2, m], dt[:, b, m], ACT.Exp, scale=a_neg[:, m, n:n + 1]).then_inc(dA_s, 1)

                def gelus(q, f0):
                    for f in range(f0, f0 + 2):
                        if f % HF == 0:
                            act.wait_ge(dn_s, 2 * q + f // HF + 1)
                        act.wait_ge(up_s, FB * q + f + 1)
                        act.activation(g1[:, f % HF], bank[:, TURN + f % 2], ACT.Gelu, bias=b_1[:, f:f + 1]).then_inc(g1_s, 1)

                def step(s, i, b, first, last):
                    o = 1 - b
                    for n in range(NS):
                        if n < NS - 1:
                            decay(s, b, n + 1)
                        elif not last:
                            decay(s + 1, o, 0)
                        if not first and n in (4, 5, 9, 10):
                            gelus(s - 1, {4: 0, 5: 2, 9: 4, 10: 6}[n])
                        if not last:
                            if n in (1, 4):
                                square(s + 1, n // 3)
                            if n in (2, 5):
                                root(s + 1, n // 3)
                            if n == 6:
                                affine(s + 1, o)
                                take_xm(s + 1, o)
                            if n == 7:
                                take_z(s + 1, o)
                            if n == 9:
                                take_u(s + 1)
                            if n == 10:
                                take_prj(s + 1, o)
                            if n in (11, 12, 13):
                                softplus(s + 1, n - 11)

                for k in range(2):
                    square(0, k)
                    root(0, k)
                act.wait_ge(weights_in, 16 * n_loads)
                act.activation(a_neg[:], a_log[:], ACT.Exp).then_inc(a_exp, 1)
                act.wait_ge(a_exp, 1)
                act.mul(a_neg[:], a_neg[:], -1.0).then_inc(a_exp, 1)
                act.wait_ge(a_exp, 2)
                affine(0, 0)
                take_xm(0, 0)
                take_z(0, 0)
                take_u(0)
                take_prj(0, 0)
                for part in range(3):
                    softplus(0, part)
                decay(0, 0, 0)
                tiles(act, step)
                for f0 in range(0, FB, 2):
                    gelus(LAST, f0)

            @block.vector
            def _(dve):
                dve.wait_ge(consts, 8)
                dve.sem_inc(tail_s, 1)
                dve.sem_inc(x1_s, KB)
                dve.sem_inc(dbu_s, 1)
                dve.sem_inc(nrm[1], 1)
                dve.sem_inc(scan_s, 2 * MB)
                dve.sem_inc(dn_s, 1)

                def centre(q, b, k):
                    dve.wait_ge(mean[k], q + 1)
                    dve.tensor_tensor(xc[:], xt[:, b] if k == 0 else v[:], bcast(bank[:, LN_BANK], KB), ALU.subtract).then_inc(cent[k], 1)

                def scale(q, k):
                    dve.wait_ge(rst[k], q + 1)
                    dve.tensor_tensor(v[:], xc[:], bcast(rstd[:], KB), ALU.mult).then_inc(nrm[k], 1)

                def convolve(q, b, taps):
                    for tap in taps:
                        for m in range(MB):
                            if tap == 0:
                                dve.wait_ge(xm_s, 2 * MB * q + m + 1)
                                dve.wait_ge(tails_s, q + 1)
                                dve.tensor_scalar(cx[:, m], xm[:, m, 0:T], conv_w[:, m, 0:1], None, ALU.mult).then_inc(conv_s, 1)
                            else:
                                dve.wait_ge(conv_s, 4 * MB * q + (tap - 1) * MB + m + 1)
                                dve.scalar_tensor_tensor(out=cx[:, m], in0=xm[:, m, tap:tap + T], scalar=conv_w[:, m, tap:tap + 1],
                                                         in1=cx[:, m], op0=ALU.mult, op1=ALU.add).then_inc(conv_s, 1)
                    if 3 in taps:
                        dve.wait_ge(conv_s, 4 * MB * (q + 1))
                        dve.tensor_copy(tail[:, b], xm[:, :, T:T + 3]).then_inc(tail_s, 1)

                def make_dt(q, b):
                    dve.wait_ge(dte_s, 3 * q + 3)
                    dve.scalar_tensor_tensor(out=dt[:, b], in0=r_dt[:], scalar=0.0, in1=ea[:], op0=ALU.max, op1=ALU.add).then_inc(dt_s, 1)

                def scan(s, b, n):
                    g = s * NS + n
                    h = hb[:, n % 2]
                    dve.wait_ge(bc_s, g + 1)
                    if n == 0:
                        dve.wait_ge(dtu_s, s + 1)
                    if not (is_first(s) and n == 0):
                        dve.wait_ge(yacc_s, g)
                    dve.tensor_tensor(h, dtu[:, b], bcast(bank[:, B_BANK], MB), ALU.mult).then_inc(dbu_s, 1)
                    dve.wait_ge(dbu_s, g + 2)
                    for m in range(MB):
                        dve.wait_ge(dA_s, MB * g + m + 1)
                        dve.tensor_tensor_scan(out=h[:, m], data0=dA[:, n % 2, m], data1=h[:, m],
                                               initial=state[:, b, n, m:m + 1], op0=ALU.mult, op1=ALU.add).then_inc(scan_s, 1)
                    dve.wait_ge(scan_s, MB * (g + 1) + 2 * MB)
                    dve.tensor_copy(state[:, b, n, :], h[:, :, T - 1]).then_inc(save_s, 1)
                    dve.wait_ge(save_s, g + 1)
                    dve.tensor_tensor(h, h, bcast(bank[:, C_BANK + n % 2], MB), ALU.mult).then_inc(hc_s, 1)

                def join(q, b):
                    dve.wait_ge(wo_s, KB * (q + 1))
                    dve.wait_ge(out_free, q + 1)
                    dve.tensor_tensor(y2[:], bank[:, ACC:ACC + KB], yn[:, b], ALU.add).then_inc(y2_s, 1)

                def finish(q):
                    dve.wait_ge(dn_s, 2 * q + 3)
                    dve.wait_ge(res_s, q + 1)
                    for ob in range(KB):
                        dve.scalar_tensor_tensor(out=y2[:, ob], in0=bank[:, ACC + ob], scalar=b_2[:, ob:ob + 1], in1=res[:, ob],
                                                 op0=ALU.add, op1=ALU.add).then_inc(x1_s, 1)

                def step(s, i, b, first, last):
                    o = 1 - b
                    for n in range(NS):
                        scan(s, b, n)
                        if not first:
                            if n == 2:
                                join(s - 1, o)
                            if n == 15:
                                finish(s - 1)
                        if not last:
                            if n in (0, 3):
                                centre(s + 1, o, n // 3)
                            if n in (2, 5):
                                scale(s + 1, n // 3)
                            if n == 8:
                                convolve(s + 1, o, (0, 1))
                            if n == 9:
                                convolve(s + 1, o, (2, 3))
                            if n == 14:
                                make_dt(s + 1, o)

                for k in range(2):
                    centre(0, 0, k)
                    scale(0, k)
                dve.wait_ge(weights_in, 16 * n_loads)
                convolve(0, 0, (0, 1, 2, 3))
                make_dt(0, 0)
                tiles(dve, step)
                join(LAST, 1)
                finish(LAST)
NB = M // P
HEADS, EXPERTS = 4, 4
HC = HEADS * EXPERTS
TW = HC + HEADS
EDGES = 1048576
EC = EDGES // P
FE = 512
FEB = FE // P
SUB = T // P
KEY_CHUNK = EC // (B * TI)
FAR_CHUNK, FAR_ROUNDS = EC // 32, 7
FAR_COLS = EC // FAR_CHUNK * 8 * FAR_ROUNDS
FAR_SUB = 16
PICK_CHUNK, PICK_ROUNDS = EC // 32, 2
PICKS = EC // PICK_CHUNK * 8 * PICK_ROUNDS
NEAR_ROUNDS = 22
NEAR_COLS = 8 * NEAR_ROUNDS
GROUPS = 16
NEAR_GROUP, FAR_GROUP = NEAR_COLS // GROUPS, FAR_COLS // GROUPS
FAR_SUBS = FAR_GROUP // FAR_SUB
REST_CHUNK, REST_ROUNDS = (EC + PICKS) // 4, 7
REST_COLS = 4 * 8 * REST_ROUNDS


class Graph:

    def __init__(self, nc, ctx, name):
        def sb(n, shape, dt=F32):
            return ctx.enter_context(nc.sbuf_tensor(f"{name}_{n}", shape, dt))
        self.h = sb("h", [P, NB, TW])
        self.a_dst = sb("a_dst", [P, NB, HEADS])
        self.top = sb("top", [P, HEADS])
        self.last = sb("last", [P, TW])
        self.count = sb("count", [P, NB])
        self.agg = sb("agg", [P, NB, TW])
        self.near_more = sb("near_more", [1, 1], I32)
        self.far_more = sb("far_more", [1, 1], I32)
        self.w_1, self.w_2 = sb("w_1", [P, EXPERTS, KB, FE]), sb("w_2", [P, EXPERTS, FEB, C])
        self.b_1, self.b_2 = sb("b_1", [P, EXPERTS, FEB]), sb("b_2", [P, EXPERTS, C])
        self.gate = sb("gate", [P, NB, EXPERTS])
        self.table = nc.dram_tensor(f"{name}_table", (M, TW), F32, kind="Internal").ap()
        self.dst_table = nc.dram_tensor(f"{name}_dst_table", (M, HEADS), F32, kind="Internal").ap()
        self.tn = nc.dram_tensor(f"{name}_tn", (B, C, L), F32, kind="Internal").ap()


def rows(ap, n=P):
    return ap.rearrange("(o n) -> o n", o=1).to_broadcast([n, ap.shape[0]])


def features_phase(nc, name, w, g, x_in, near_key, far_key):
    LAST = B * TI - 1
    with Phase(nc, name) as ph:
        sb, ps, sem = ph.sb, ph.ps, ph.sem
        w_gat = sb("w_gat", [P, KB, HC])
        att = sb("att", [P, 2, HC])
        ones_mean, eps = sb("ones_mean", [P, P]), sb("eps", [P, 1])
        xt, xc, sq, tn = (sb(n, [P, B, KB, T]) for n in ("xt", "xc", "sq", "tn"))
        lnv, rstd = sb("lnv", [P, T]), sb("rstd", [P, B, T])
        prod, part_top = sb("prod", [P, 2, SUB, HC]), sb("part_top", [P, HEADS])
        ends = sb("ends", [P, 2, 2, KEY_CHUNK], I32)
        packed, src_m, dst_1 = sb("packed", [P, KEY_CHUNK], I32), sb("src_m", [P, KEY_CHUNK]), sb("dst_1", [P, KEY_CHUNK])
        ends_in = [sem("ends_in0"), sem("ends_in1")]
        packed_s, clamped_s, near_s, far_s = (sem(n) for n in ("packed", "clamped", "near", "far"))
        edges = w["edge_index"].rearrange("e (p n) -> p e n", p=P)
        mean_b, var_b, h_b = (ps(n, [P, B, T]) for n in ("mean_b", "var_b", "h_b"))
        weights_in, consts, free = (sem(n) for n in ("weights_in", "consts", "free"))
        x_loaded, stored = [sem("x_loaded0"), sem("x_loaded1")], [sem("stored0"), sem("stored1")]
        mean, cent, sqd, var, lns, rst, tn_s = (sem(n) for n in ("mean", "cent", "sqd", "var", "lns", "rst", "tn"))
        hp_s, h_s, prod_s, a_s, top_s, all_top, tabled, last_s = (sem(n) for n in ("hp", "h", "prod", "a", "top", "all_top", "tabled", "last"))

        with nc.Block() as block:
            @block.sync
            def _(sp):
                sp.dma_start(w_gat[:], w["W_gat"].rearrange("(k p) n -> p k n", p=P)).then_inc(weights_in, 16)
                for k, n in enumerate(("att_src", "att_dst")):
                    sp.dma_start(att[:, k], rows(w[n].rearrange("h e -> (h e)"))).then_inc(weights_in, 16)
                with sp.Fori(0, TI) as i:
                    for b in range(B):
                        sp.wait_ge(cent, i * B + b + 1)
                        sp.wait_ge(sqd, i * B + b + 1)
                        sp.dma_start(xt[:, b], x_in[b].rearrange("(k p) t -> p k t", p=P)[:, :, bass.ds(i * T, T)]).then_inc(x_loaded[b], 16)
                        sp.wait_ge(near_s, i * B + b + 1)
                        sp.dma_start(ends[:, b], edges[:, :, bass.ds((i * B + b) * KEY_CHUNK, KEY_CHUNK)]).then_inc(ends_in[b], 16)
                sp.wait_ge(a_s, 2 * B * TI + 2)
                sp.wait_ge(h_s, B * TI + 2)
                sp.dma_start(g.table.rearrange("(n p) c -> p n c", p=P), g.h[:]).then_inc(tabled, 16)
                sp.dma_start(g.dst_table.rearrange("(n p) c -> p n c", p=P), g.a_dst[:]).then_inc(tabled, 16)
                sp.wait_ge(tabled, 32)
                sp.dma_start(g.last[:], g.table[M - 1:M, :].to_broadcast([P, TW])).then_inc(last_s, 16)
                sp.wait_ge(last_s, 16)

            @block.gpsimd
            def _(pool):
                pool.memset(ones_mean[:], 1.0 / C).then_inc(consts, 1)
                pool.memset(eps[:], 1e-5).then_inc(consts, 1)
                with pool.Fori(0, TI) as i:
                    for b in range(B):
                        pool.wait_ge(tn_s, i * B + b + 3)
                        pool.dma_start(g.tn[b].rearrange("(k p) t -> p k t", p=P)[:, :, bass.ds(i * T, T)], tn[:, b]).then_inc(stored[b], 16)
                        pool.wait_ge(stored[b], 16 * i + 16)
                        pool.sem_inc(free, 1)
                pool.wait_ge(top_s, 1)
                pool.partition_all_reduce(g.top[:], part_top[:], P, bass.bass_isa.ReduceOp.max).then_inc(all_top, 1)
                pool.wait_ge(all_top, 1)

            @block.tensor
            def _(pe):
                def mean_of(s, i, b):
                    pe.wait_ge(x_loaded[b], 16 * i + 16)
                    pe.wait_ge(cent, s + 1)
                    for kb in range(KB):
                        mm = pe.matmul(mean_b[:, b], ones_mean[:], xt[:, b, kb], start=kb == 0, stop=kb == KB - 1)
                    mm.then_inc(mean, 1)

                def features_of(s, b):
                    pe.wait_ge(tn_s, s + 3)
                    pe.wait_ge(prod_s, 2 * s + 2)
                    pe.wait_ge(h_s, s + 1)
                    for sub in range(SUB):
                        for kb in range(KB):
                            mm = pe.matmul(h_b[:, b, sub * HC:(sub + 1) * HC], tn[:, b, kb, sub * P:(sub + 1) * P], w_gat[:, kb],
                                           start=kb == 0, stop=kb == KB - 1)
                    mm.then_inc(hp_s, 1)

                def step(s, i, b, first, last):
                    if not last:
                        mean_of(s + 1, *after(i, b))
                    pe.wait_ge(sqd, s + 3)
                    pe.wait_ge(lns, s + 1)
                    for kb in range(KB):
                        mm = pe.matmul(var_b[:, b], ones_mean[:], sq[:, b, kb], start=kb == 0, stop=kb == KB - 1)
                    mm.then_inc(var, 1)
                    if not first:
                        features_of(s - 1, 1 - b)

                pe.wait_ge(weights_in, 48)
                pe.wait_ge(consts, 2)
                mean_of(0, 0, 0)
                tiles(pe, step)
                features_of(LAST, 1)

            @block.scalar
            def _(act):
                def square(s, b):
                    act.wait_ge(cent, s + 3)
                    act.wait_ge(var, s + 1)
                    act.activation(sq[:, b], xc[:, b], ACT.Square).then_inc(sqd, 1)

                def step(s, i, b, first, last):
                    act.wait_ge(var, s + 3)
                    act.wait_ge(rst, s + 2)
                    act.activation(lnv[:], var_b[:, b], ACT.Ln, bias=eps[:]).then_inc(lns, 1)
                    act.wait_ge(lns, s + 3)
                    act.wait_ge(tn_s, s + 1)
                    act.activation(rstd[:, b], lnv[:], ACT.Exp, scale=-0.5).then_inc(rst, 1)
                    if not last:
                        square(s + 1, 1 - b)

                act.wait_ge(consts, 2)
                act.sem_inc(sqd, 2)
                act.sem_inc(lns, 2)
                act.sem_inc(rst, 2)
                act.sem_inc(var, 2)
                square(0, 0)
                tiles(act, step)

            @block.vector
            def _(dve):
                def centre(s, b):
                    dve.wait_ge(mean, s + 1)
                    dve.wait_ge(tn_s, s + 1)
                    dve.wait_ge(sqd, s + 1)
                    dve.tensor_tensor(xc[:, b], xt[:, b], bcast(mean_b[:, b], KB), ALU.subtract).then_inc(cent, 1)

                def logits(s, i, b):
                    blocks = bass.ds(i * SUB + b * (NB // B), SUB)
                    dve.wait_ge(hp_s, s + 3)
                    dve.wait_ge(a_s, 2 * s + 2)
                    hp = h_b[:, b, 0:SUB * HC].rearrange("p (s c) -> p s c", s=SUB)
                    dve.tensor_copy(g.h[:, blocks, 0:HC], hp).then_inc(h_s, 1)
                    for k in range(2):
                        dve.tensor_tensor(prod[:, k], hp, bcast(att[:, k], SUB), ALU.mult).then_inc(prod_s, 1)
                    dve.wait_ge(prod_s, 2 * s + 6)
                    for k, dst in enumerate((g.h[:, blocks, HC:TW], g.a_dst[:, blocks, :])):
                        dve.tensor_reduce(dst, prod[:, k].rearrange("p s (h e) -> p s h e", h=HEADS), AX.X, ALU.add).then_inc(a_s, 1)

                def keys(s, i, b):
                    here = bass.ds(s * KEY_CHUNK, KEY_CHUNK)
                    src, dst = ends[:, b, 0], ends[:, b, 1]
                    dve.wait_ge(ends_in[b], 16 * i + 16)
                    dve.wait_ge(near_s, s + 2)
                    dve.wait_ge(far_s, s + 1)
                    dve.tensor_scalar(packed[:], dst, 13, 0x40000000, ALU.logical_shift_left, ALU.bitwise_or).then_inc(packed_s, 1)
                    dve.tensor_scalar(src_m[:], src, float(M - 1), None, ALU.is_lt).then_inc(packed_s, 1)
                    dve.tensor_scalar(dst_1[:], dst, 1.0, None, ALU.add).then_inc(packed_s, 1)
                    dve.wait_ge(packed_s, 5 * s + 3)
                    dve.tensor_tensor(packed[:], packed[:], src, ALU.bitwise_or).then_inc(clamped_s, 1)
                    dve.scalar_tensor_tensor(out=src_m[:], in0=dst, scalar=float(M), in1=src_m[:],
                                             op0=ALU.is_lt, op1=ALU.mult).then_inc(packed_s, 1)
                    dve.scalar_tensor_tensor(out=dst_1[:], in0=dst_1[:], scalar=float(M + 1), in1=dst_1[:],
                                             op0=ALU.is_lt, op1=ALU.mult).then_inc(packed_s, 1)
                    dve.wait_ge(clamped_s, s + 1)
                    dve.wait_ge(packed_s, 5 * s + 5)
                    dve.scalar_tensor_tensor(out=far_key[:, here], in0=src, scalar=float(M - 1), in1=dst_1[:],
                                             op0=ALU.is_ge, op1=ALU.mult).then_inc(far_s, 1)
                    dve.tensor_tensor(near_key[:, here], packed[:].bitcast(F32), src_m[:], ALU.mult).then_inc(near_s, 1)

                def step(s, i, b, first, last):
                    if not last:
                        centre(s + 1, 1 - b)
                    keys(s, i, b)
                    if not first:
                        logits(s - 1, *ahead_of(i, b))
                    dve.wait_ge(rst, s + 3)
                    dve.wait_ge(free, s + 1)
                    dve.wait_ge(hp_s, s + 1)
                    dve.wait_ge(cent, s + 3)
                    dve.tensor_tensor(tn[:, b], xc[:, b], bcast(rstd[:, b], KB), ALU.mult).then_inc(tn_s, 1)

                dve.wait_ge(weights_in, 48)
                dve.sem_inc(near_s, 2)
                dve.sem_inc(far_s, 1)
                dve.sem_inc(cent, 2)
                dve.sem_inc(tn_s, 2)
                dve.sem_inc(hp_s, 2)
                dve.sem_inc(a_s, 2)
                dve.sem_inc(free, 2)
                dve.sem_inc(h_s, 2)
                dve.sem_inc(prod_s, 4)
                centre(0, 0)
                tiles(dve, step)
                logits(LAST, TI - 1, 1)
                dve.wait_ge(a_s, 2 * B * TI + 2)
                dve.tensor_reduce(part_top[:], g.h[:, :, HC:TW].rearrange("p n c -> p c n"), AX.X, ALU.max).then_inc(top_s, 1)


def take_largest(dve, keys, taken, chunk, rounds, max_s, cleared_s):
    n = keys.shape[1] // chunk
    for r in range(rounds):
        for c in range(n):
            if r > 0:
                dve.wait_ge(cleared_s, (r - 1) * n + c + 1)
            dve.max(taken[:, c, 8 * r:8 * r + 8], keys[:, c * chunk:(c + 1) * chunk]).then_inc(max_s, 1)
        for c in range(n):
            dve.wait_ge(max_s, r * n + c + 1)
            part = keys[:, c * chunk:(c + 1) * chunk]
            dve.match_replace(part, taken[:, c, 8 * r:8 * r + 8], part, 0.0).then_inc(cleared_s, 1)
    dve.wait_ge(max_s, rounds * n)
    dve.wait_ge(cleared_s, rounds * n)


def passes(nc, n_passes, sems, more, programs):
    engines = (nc.tensor, nc.vector, nc.scalar, nc.gpsimd, nc.sync)
    left = nc.values_load(more, min_val=0, max_val=1)
    nc.all_engine_barrier()
    with nc.If(left != 0):
        with nc.Fori(0, n_passes):
            left_now = nc.values_load(more, min_val=0, max_val=1)
            nc.all_engine_barrier()
            with nc.If(left_now != 0):
                for eng, program in programs:
                    program(eng)
                nc.all_engine_barrier()
                for s in sems:
                    nc.sync.sem_clear(s)
                nc.all_engine_barrier()
            with nc.Else():
                for eng in engines:
                    eng.nop()
            nc.all_engine_barrier()
        nc.all_engine_barrier()
    with nc.Else():
        for eng in engines:
            eng.nop()
    nc.all_engine_barrier()


def far_rest_phase(nc, name, g, far_key):
    slots = 8 * FAR_ROUNDS
    n_passes = -(-FAR_CHUNK // slots)
    n_groups = FAR_COLS // FAR_SUB
    with Phase(nc, name) as ph:
        sb, ps, sem = ph.sb, ph.ps, ph.sem
        taken = sb("taken", [P, EC // FAR_CHUNK, slots])
        node = sb("node", [P, FAR_COLS], I32)
        field = sb("field", [P, 2, FAR_COLS], I32)
        field_b = sb("field_b", [P, 2, FAR_COLS], BF16)
        iota_i, iota_b = sb("iota_i", [P, P], I32), sb("iota_b", [P, P], BF16)
        lo, hi = sb("lo", [P, 2, FAR_SUB, P], BF16), sb("hi", [P, 2, FAR_SUB, NB], BF16)
        last_slot, any_last = sb("last_slot", [P, 1]), sb("any_last", [P, 1])
        bank = ps("bank", [P, NB])
        setup = sem("setup")
        names = ("max", "cleared", "last_slot", "any_last", "more", "node", "field", "field_b", "lo", "hi", "summed", "count")
        max_s, cleared_s, last_s, any_s, more_s, node_s, field_s, fb_s, lo_s, hi_s, sum_s, count_s = in_pass = [sem(n) for n in names]

        with nc.Block() as block:
            @block.gpsimd
            def _(pool):
                pool.iota(iota_i[:], pattern=[[1, P]], base=0, channel_multiplier=0).then_inc(setup, 1)

            @block.vector
            def _(dve):
                dve.wait_ge(setup, 1)
                dve.tensor_copy(iota_b[:], iota_i[:]).then_inc(setup, 1)
                dve.wait_ge(setup, 2)

        def vector_program(dve):
            take_largest(dve, far_key, taken, FAR_CHUNK, FAR_ROUNDS, max_s, cleared_s)
            dve.tensor_reduce(last_slot[:], taken[:, :, slots - 1], AX.X, ALU.max).then_inc(last_s, 1)
            dve.tensor_scalar(node[:], taken[:, :, :].rearrange("p c s -> p (c s)"), -1.0, None, ALU.add).then_inc(node_s, 1)
            dve.wait_ge(node_s, 1)
            dve.tensor_scalar(field[:, 0], node[:], P - 1, None, ALU.bitwise_and).then_inc(field_s, 1)
            dve.tensor_scalar(field[:, 1], node[:], 7, None, ALU.arith_shift_right).then_inc(field_s, 1)
            dve.wait_ge(field_s, 2)
            dve.tensor_copy(field_b[:], field[:]).then_inc(fb_s, 1)
            dve.wait_ge(fb_s, 1)
            dve.sem_inc(sum_s, 2)
            with dve.Fori(0, n_groups // 2) as i:
                for k in range(2):
                    q = i * 2 + k
                    here = bass.ds(q * FAR_SUB, FAR_SUB)
                    dve.wait_ge(sum_s, q + 1)
                    dve.tensor_tensor(lo[:, k], bcast(iota_b[:], FAR_SUB), spread(field_b[:, 0, here], P), ALU.is_equal).then_inc(lo_s, 1)
                    dve.tensor_tensor(hi[:, k], bcast(iota_b[:, 0:NB], FAR_SUB), spread(field_b[:, 1, here], NB), ALU.is_equal).then_inc(hi_s, 1)
            dve.wait_ge(sum_s, n_groups + 3)
            dve.tensor_tensor(g.count[:], g.count[:], bank[:], ALU.add).then_inc(count_s, 1)
            dve.wait_ge(any_s, 1)
            dve.tensor_scalar(g.far_more[:], any_last[0:1], 0.0, None, ALU.is_gt).then_inc(more_s, 1)
            dve.wait_ge(more_s, 1)

        def tensor_program(pe):
            pe.matmul(bank[:], zero_b[:], zero_b[:, 0:NB], start=True, stop=False)
            with pe.Fori(0, n_groups // 2) as i:
                for k in range(2):
                    q = i * 2 + k
                    pe.wait_ge(lo_s, q + 1)
                    pe.wait_ge(hi_s, q + 1)
                    for c in range(FAR_SUB):
                        mm = pe.matmul(bank[:], lo[:, k, c], hi[:, k, c], start=False, stop=False)
                    mm.then_inc(sum_s, 1)
            pe.matmul(bank[:], zero_b[:], zero_b[:, 0:NB], start=False, stop=True).then_inc(sum_s, 1)

        zero_b = sb("zero_b", [P, P], BF16)
        nc.vector.memset(zero_b[:], 0.0)
        nc.all_engine_barrier()

        def pool_program(pool):
            pool.wait_ge(last_s, 1)
            pool.partition_all_reduce(any_last[:], last_slot[:], P, bass.bass_isa.ReduceOp.max).then_inc(any_s, 1)

        passes(nc, n_passes, in_pass, g.far_more[0:1, 0:1],
               [(nc.vector, vector_program), (nc.tensor, tensor_program), (nc.gpsimd, pool_program)])


def spread(ap, n):
    return ap.rearrange("p (g o) -> p g o", o=1).to_broadcast([ap.shape[0], ap.shape[1], n])


def near_rest_phase(nc, name, g, near_key):
    slots = 8 * REST_ROUNDS
    n_passes = -(-REST_CHUNK // slots)
    with Phase(nc, name) as ph:
        sb, ps, sem = ph.sb, ph.ps, ph.sem
        taken = sb("taken", [P, 4, slots])
        keys = taken[:, :, :].rearrange("p c s -> p (c s)")
        bits = keys.bitcast(I32)
        src_i, dst_i = sb("src_i", [P, REST_COLS], I32), sb("dst_i", [P, REST_COLS], I32)
        lo_i, hi_i = sb("lo_i", [P, REST_COLS], I32), sb("hi_i", [P, REST_COLS], I32)
        lo_f, hi_f, there = sb("lo_f", [P, REST_COLS]), sb("hi_f", [P, REST_COLS]), sb("there", [P, REST_COLS])
        rows_g, dst_g = sb("rows_g", [P, REST_COLS, TW]), sb("dst_g", [P, REST_COLS, HEADS])
        logit, bound = sb("logit", [P, REST_COLS, HEADS]), sb("bound", [P, REST_COLS, HEADS])
        val = sb("val", [P, REST_COLS, TW])
        iota_i, iota_f = sb("iota_i", [P, P], I32), sb("iota_f", [P, P])
        lo, rhs = sb("lo", [P, 2, P]), sb("rhs", [P, 2, NB, TW])
        zero = sb("zero", [P, 512])
        last_slot, any_last = sb("last_slot", [P, 1]), sb("any_last", [P, 1])
        bank = ps("bank", [P, 3, 512])
        setup = sem("setup")
        names = ("max", "cleared", "last_slot", "any_last", "more", "field", "field_f", "hi_m", "rows", "dsts",
                 "logit", "lrelu", "diff", "weight", "val", "lo", "rhs", "summed", "agg")
        (max_s, cleared_s, last_s, any_s, more_s, field_s, ff_s, him_s, rows_s, dsts_s, logit_s, lrelu_s, diff_s, weight_s,
         val_s, lo_s, rhs_s, sum_s, agg_s) = in_pass = [sem(n) for n in names]

        with nc.Block() as block:
            @block.gpsimd
            def _(pool):
                pool.iota(iota_i[:], pattern=[[1, P]], base=0, channel_multiplier=0).then_inc(setup, 1)
                pool.memset(zero[:], 0.0).then_inc(setup, 1)

            @block.vector
            def _(dve):
                dve.wait_ge(setup, 2)
                dve.tensor_copy(iota_f[:], iota_i[:]).then_inc(setup, 1)
                dve.wait_ge(setup, 3)

        def vector_program(dve):
            take_largest(dve, near_key, taken, REST_CHUNK, REST_ROUNDS, max_s, cleared_s)
            dve.tensor_scalar(src_i[:], bits, M - 1, None, ALU.bitwise_and).then_inc(field_s, 1)
            dve.tensor_scalar(dst_i[:], bits, 13, M - 1, ALU.logical_shift_right, ALU.bitwise_and).then_inc(field_s, 1)
            dve.tensor_scalar(lo_i[:], bits, 13, P - 1, ALU.logical_shift_right, ALU.bitwise_and).then_inc(field_s, 1)
            dve.tensor_scalar(hi_i[:], bits, 20, NB - 1, ALU.logical_shift_right, ALU.bitwise_and).then_inc(field_s, 1)
            dve.tensor_reduce(last_slot[:], taken[:, :, slots - 1], AX.X, ALU.max).then_inc(last_s, 1)
            dve.wait_ge(field_s, 4)
            dve.tensor_copy(lo_f[:], lo_i[:]).then_inc(ff_s, 1)
            dve.tensor_scalar(hi_f[:], hi_i[:], 1.0, None, ALU.add).then_inc(ff_s, 1)
            dve.wait_ge(ff_s, 2)
            dve.scalar_tensor_tensor(out=hi_f[:], in0=keys, scalar=0.0, in1=hi_f[:], op0=ALU.is_gt, op1=ALU.mult).then_inc(him_s, 1)
            dve.wait_ge(him_s, 1)
            dve.tensor_scalar(hi_f[:], hi_f[:], -1.0, None, ALU.add).then_inc(him_s, 1)
            dve.wait_ge(rows_s, 16 * REST_COLS)
            dve.wait_ge(dsts_s, 16 * REST_COLS)
            dve.tensor_tensor(logit[:], rows_g[:, :, HC:TW], dst_g[:], ALU.add).then_inc(logit_s, 1)
            dve.tensor_tensor(bound[:], dst_g[:], bcast(g.top[:], REST_COLS), ALU.add).then_inc(logit_s, 1)
            dve.wait_ge(logit_s, 2)
            for a in (logit, bound):
                dve.scalar_tensor_tensor(out=a[:], in0=a[:], scalar=0.2, in1=a[:], op0=ALU.mult, op1=ALU.max).then_inc(lrelu_s, 1)
            dve.wait_ge(lrelu_s, 2)
            dve.tensor_tensor(logit[:], logit[:], bound[:], ALU.subtract).then_inc(diff_s, 1)
            dve.wait_ge(weight_s, 1)
            for h in range(HEADS):
                dve.tensor_tensor(val[:, :, EXPERTS * h:EXPERTS * (h + 1)], rows_g[:, :, EXPERTS * h:EXPERTS * (h + 1)],
                                  val[:, :, HC + h:HC + h + 1].to_broadcast([P, REST_COLS, EXPERTS]), ALU.mult).then_inc(val_s, 1)
            dve.wait_ge(val_s, HEADS)
            dve.wait_ge(him_s, 2)
            dve.sem_inc(sum_s, 2)
            with dve.Fori(0, REST_COLS // 2) as i:
                for k in range(2):
                    q = i * 2 + k
                    dve.wait_ge(sum_s, q + 1)
                    dve.tensor_scalar(lo[:, k], iota_f[:], lo_f[:, bass.ds(q, 1)], None, ALU.is_equal).then_inc(lo_s, 1)
                    dve.scalar_tensor_tensor(out=rhs[:, k], in0=spread(iota_f[:, 0:NB], TW), scalar=hi_f[:, bass.ds(q, 1)],
                                             in1=val[:, bass.ds(q, 1), :].to_broadcast([P, NB, TW]),
                                             op0=ALU.is_equal, op1=ALU.mult).then_inc(rhs_s, 1)
            dve.wait_ge(sum_s, REST_COLS + 3)
            for k, (a, b) in enumerate(SPLITS):
                dve.tensor_tensor(g.agg[:, a:b, :], g.agg[:, a:b, :], bank[:, k, 0:(b - a) * TW].rearrange("p (n c) -> p n c", c=TW),
                                  ALU.add).then_inc(agg_s, 1)
            dve.wait_ge(any_s, 1)
            dve.tensor_scalar(g.near_more[:], any_last[0:1], 0.0, None, ALU.is_gt).then_inc(more_s, 1)
            dve.wait_ge(more_s, 1)

        def tensor_program(pe):
            for n, (a, b) in enumerate(SPLITS):
                pe.matmul(bank[:, n, 0:(b - a) * TW], zero[:, 0:P], zero[:, 0:(b - a) * TW], start=True, stop=False)
            with pe.Fori(0, REST_COLS // 2) as i:
                for k in range(2):
                    q = i * 2 + k
                    pe.wait_ge(lo_s, q + 1)
                    pe.wait_ge(rhs_s, q + 1)
                    for n, (a, b) in enumerate(SPLITS):
                        mm = pe.matmul(bank[:, n, 0:(b - a) * TW], lo[:, k], rhs[:, k, a:b].rearrange("p n c -> p (n c)"),
                                       start=False, stop=False)
                    mm.then_inc(sum_s, 1)
            for n, (a, b) in enumerate(SPLITS):
                mm = pe.matmul(bank[:, n, 0:(b - a) * TW], zero[:, 0:P], zero[:, 0:(b - a) * TW], start=False, stop=True)
            mm.then_inc(sum_s, 1)

        def scalar_program(act):
            act.wait_ge(diff_s, 1)
            act.activation(val[:, :, HC:TW], logit[:], ACT.Exp).then_inc(weight_s, 1)

        def pool_program(pool):
            pool.wait_ge(field_s, 4)
            pool.wait_ge(last_s, 1)
            pool.partition_all_reduce(any_last[:], last_slot[:], P, bass.bass_isa.ReduceOp.max).then_inc(any_s, 1)
            for q in range(REST_COLS):
                pool.indirect_dma_start(out=rows_g[:, q], out_offset=None, in_=g.table,
                                        in_offset=bass.IndirectOffsetOnAxis(ap=src_i[:, q:q + 1].bitcast(U32), axis=0)).then_inc(rows_s, 16)
                pool.indirect_dma_start(out=dst_g[:, q], out_offset=None, in_=g.dst_table,
                                        in_offset=bass.IndirectOffsetOnAxis(ap=dst_i[:, q:q + 1].bitcast(U32), axis=0)).then_inc(dsts_s, 16)
            pool.wait_ge(rows_s, 16 * REST_COLS)
            pool.wait_ge(dsts_s, 16 * REST_COLS)
            pool.dma_reset()

        passes(nc, n_passes, in_pass, g.near_more[0:1, 0:1],
               [(nc.vector, vector_program), (nc.tensor, tensor_program), (nc.scalar, scalar_program), (nc.gpsimd, pool_program)])


SPLITS = [(0, 25), (25, 50), (50, NB)]


def edges_phase(nc, name, w, g, near_key, far_key):
    NG = NEAR_GROUP
    SHARED_AFTER = (6, 8)
    SHARED = len(SHARED_AFTER)
    OWN = FAR_SUBS - SHARED
    with Phase(nc, name) as ph:
        sb, ps, sem = ph.sb, ph.ps, ph.sem
        near_taken, far_taken = sb("near_taken", [P, 1, NEAR_COLS]), sb("far_taken", [P, EC // FAR_CHUNK, 8 * FAR_ROUNDS])
        picks = near_key[:, EC:EC + PICKS].rearrange("p (c s) -> p c s", c=EC // PICK_CHUNK)
        near_keys = near_taken[:, 0]
        bits = near_keys.bitcast(I32)
        ends = sb("ends", [P, 2, NEAR_COLS], I32)
        lo_i, hi_i = sb("lo_i", [P, NEAR_COLS], I32), sb("hi_i", [P, NEAR_COLS], I32)
        lo_f, hi_f = sb("lo_f", [P, NEAR_COLS]), sb("hi_f", [P, NEAR_COLS])
        far_node, far_field = sb("far_node", [P, FAR_COLS], I32), sb("far_field", [P, 2, FAR_COLS], I32)
        far_field_b = sb("far_field_b", [P, 2, FAR_COLS], BF16)
        iota_i, iota_f, iota_b = sb("iota_i", [P, P], I32), sb("iota_f", [P, P]), sb("iota_b", [P, P], BF16)
        one = sb("one", [P, 1])
        zero, zero_b = sb("zero", [P, 512]), sb("zero_b", [P, P], BF16)
        index = sb("index", [P, 2, 2, NG], I32)
        rows_g, dst_g = sb("rows_g", [P, 2, NG, TW]), sb("dst_g", [P, 2, NG, HEADS])
        logit, bound = sb("logit", [P, 2, NG, HEADS]), sb("bound", [P, 2, NG, HEADS])
        val = sb("val", [P, 2, NG, TW])
        lo, rhs = sb("lo", [P, 2, P]), sb("rhs", [P, 2, NB, TW])
        far_lo, far_hi = sb("far_lo", [P, 2, FAR_SUB, P], BF16), sb("far_hi", [P, 2, FAR_SUB, NB], BF16)
        both = sb("both", [P, 2, FAR_SUB, P + NB], BF16)
        full, any_full = sb("full", [P, 3]), sb("any_full", [P, 3])
        near_sum, far_sum = ps("near_sum", [P, 3, 512]), ps("far_sum", [P, NB])
        setup, pick_max, pick_cleared, near_max, near_cleared, far_max, far_cleared = (
            sem(n) for n in ("setup", "pick_max", "pick_cleared", "near_max", "near_cleared", "far_max", "far_cleared"))
        full_s, any_s, more_s, field_s, ff_s, him_s, node_s, far_field_s, fb_s = (
            sem(n) for n in ("full", "any", "more", "field", "ff", "him", "node", "far_field", "fb"))
        rows_s = [sem("rows0"), sem("rows1")]
        index_s, go_s, logit_s, lrelu_s, diff_s, weight_s, val_s = (sem(n) for n in ("index", "go", "logit", "lrelu", "diff", "weight", "val"))
        lo_s, rhs_s, near_sum_s, far_lo_s, far_hi_s, far_sum_s, done_s, apart_s, square_s, both_s, both_used = (
            sem(n) for n in ("lo", "rhs", "near_sum", "far_lo", "far_hi", "far_sum", "done", "apart", "square", "both", "both_used"))

        def groups(eng, step):
            with eng.Fori(0, GROUPS // 2 - 1) as i:
                step(i, 0, False)
                step(i, 1, False)
            step(GROUPS // 2 - 1, 0, False)
            step(GROUPS // 2 - 1, 1, True)

        weights_in = sem("weights_in")

        order = []
        for c in range(NG):
            order.append(("near", c))
            if c % 2 == 1 and c // 2 < OWN:
                order.append(("far", c // 2))
            if c in SHARED_AFTER:
                order.append(("shared", SHARED_AFTER.index(c)))

        with nc.Block() as block:
            @block.sync
            def _(sp):
                for e in range(EXPERTS):
                    sp.dma_start(g.w_1[:, e], w["W1"][e].rearrange("(k p) n -> p k n", p=P)).then_inc(weights_in, 16)
                    sp.dma_start(g.w_2[:, e], w["W2"][e].rearrange("(k p) n -> p k n", p=P)).then_inc(weights_in, 16)
                with nc.allow_non_contiguous_dma(reason="short vectors"):
                    sp.dma_start(g.b_1[:], w["b1"].rearrange("e (k p) -> p e k", p=P)).then_inc(weights_in, 16)
                sp.dma_start(g.b_2[:].rearrange("p e n -> p (e n)"), rows(w["b2"].rearrange("e n -> (e n)"))).then_inc(weights_in, 16)
                sp.wait_ge(weights_in, 16 * (2 * EXPERTS + 2))

            @block.gpsimd
            def _(pool):
                pool.iota(iota_i[:], pattern=[[1, P]], base=0, channel_multiplier=0).then_inc(setup, 1)
                pool.memset(zero[:], 0.0).then_inc(setup, 1)
                pool.memset(zero_b[:], 0.0).then_inc(setup, 1)
                pool.memset(one[:], 1.0).then_inc(setup, 1)

                def gather(i, k):
                    g_ = 2 * i + k
                    pool.wait_ge(index_s, g_ + 1)
                    if not (isinstance(i, int) and i == 0):
                        pool.wait_ge(val_s, HEADS * (g_ - 1))
                    pool.sem_inc(go_s, 1)
                    for q in range(NG):
                        for e, (out, table) in enumerate(((rows_g, g.table), (dst_g, g.dst_table))):
                            pool.indirect_dma_start(out=out[:, k, q], out_offset=None, in_=table,
                                                    in_offset=bass.IndirectOffsetOnAxis(ap=index[:, k, e, q:q + 1].bitcast(U32), axis=0)
                                                    ).then_inc(rows_s[k], 16)

                def values(i, k):
                    for h in range(HEADS):
                        pool.wait_ge(weight_s, 2 * i + k + 1)
                        pool.tensor_tensor(val[:, k, :, EXPERTS * h:EXPERTS * (h + 1)], rows_g[:, k, :, EXPERTS * h:EXPERTS * (h + 1)],
                                           val[:, k, :, HC + h:HC + h + 1].to_broadcast([P, NG, EXPERTS]), ALU.mult).then_inc(val_s, 1)

                def differences(i, k):
                    for c in range(SHARED):
                        q, turn = (2 * i + k) * SHARED + c, (k * SHARED + c) % 2
                        here = bass.ds((2 * i + k) * FAR_GROUP + (OWN + c) * FAR_SUB, FAR_SUB)
                        pool.wait_ge(both_used, q + 1)
                        for f, (a, n) in enumerate(((0, P), (P, NB))):
                            pool.tensor_tensor(both[:, turn, :, a:a + n], bcast(iota_b[:, 0:n], FAR_SUB), spread(far_field_b[:, f, here], n),
                                               ALU.subtract).then_inc(apart_s, 1)

                def step(i, k, last):
                    differences(i, k)
                    if not (isinstance(i, int) and i == GROUPS // 2 - 1):
                        gather(i + 1, k)
                    if not last:
                        values(i + k, 1 - k)

                gather(0, 0)
                gather(0, 1)
                values(0, 0)
                pool.wait_ge(fb_s, 1)
                groups(pool, step)
                pool.wait_ge(full_s, 3)
                pool.partition_all_reduce(any_full[:], full[:], P, bass.bass_isa.ReduceOp.max).then_inc(any_s, 1)

            @block.scalar
            def _(act):
                def copy_index(i, k):
                    act.copy(index[:, k], ends[:, :, bass.ds((2 * i + k) * NG, NG)]).then_inc(index_s, 1)

                def weights(i, k):
                    act.wait_ge(diff_s, 2 * i + k + 1)
                    act.wait_ge(near_sum_s, NG * (2 * i + k + 1))
                    act.activation(val[:, k, :, HC:TW], logit[:, k], ACT.Exp).then_inc(weight_s, 1)

                def ones_of(i, k):
                    for c in range(SHARED):
                        q, turn = (2 * i + k) * SHARED + c, (k * SHARED + c) % 2
                        act.wait_ge(apart_s, 2 * q + 2)
                        act.activation(both[:, turn], both[:, turn], ACT.Square).then_inc(square_s, 1)
                        act.wait_ge(square_s, q + 1)
                        act.activation(both[:, turn], both[:, turn], ACT.Relu, scale=-1.0, bias=one[:]).then_inc(both_s, 1)

                def step(i, k, last):
                    if not (isinstance(i, int) and i == GROUPS // 2 - 1):
                        act.wait_ge(rows_s[k], 16 * 2 * NG * (i + 1))
                        copy_index(i + 1, k)
                    ones_of(i, k)
                    if not last:
                        weights(i + k, 1 - k)

                act.wait_ge(setup, 6)
                act.wait_ge(field_s, 4)
                act.sem_inc(near_sum_s, 2 * NG)
                copy_index(0, 0)
                copy_index(0, 1)
                weights(0, 0)
                groups(act, step)

            @block.vector
            def _(dve):
                dve.wait_ge(setup, 4)
                dve.tensor_copy(iota_f[:], iota_i[:]).then_inc(setup, 1)
                dve.tensor_copy(iota_b[:], iota_i[:]).then_inc(setup, 1)
                dve.wait_ge(setup, 6)
                take_largest(dve, near_key[:, 0:EC], picks, PICK_CHUNK, PICK_ROUNDS, pick_max, pick_cleared)
                dve.tensor_reduce(full[:, 0:1], picks[:, :, 8 * PICK_ROUNDS - 1], AX.X, ALU.max).then_inc(full_s, 1)
                dve.wait_ge(full_s, 1)
                take_largest(dve, near_key[:, EC:EC + PICKS], near_taken, PICKS, NEAR_ROUNDS, near_max, near_cleared)
                dve.tensor_copy(full[:, 1:2], near_taken[:, 0, NEAR_COLS - 1:NEAR_COLS]).then_inc(full_s, 1)
                dve.tensor_scalar(ends[:, 0], bits, M - 1, None, ALU.bitwise_and).then_inc(field_s, 1)
                dve.tensor_scalar(ends[:, 1], bits, 13, M - 1, ALU.logical_shift_right, ALU.bitwise_and).then_inc(field_s, 1)
                dve.tensor_scalar(lo_i[:], bits, 13, P - 1, ALU.logical_shift_right, ALU.bitwise_and).then_inc(field_s, 1)
                dve.tensor_scalar(hi_i[:], bits, 20, NB - 1, ALU.logical_shift_right, ALU.bitwise_and).then_inc(field_s, 1)
                dve.wait_ge(field_s, 4)
                dve.tensor_copy(lo_f[:], lo_i[:]).then_inc(ff_s, 1)
                dve.tensor_scalar(hi_f[:], hi_i[:], 1.0, None, ALU.add).then_inc(ff_s, 1)
                dve.wait_ge(ff_s, 2)
                dve.scalar_tensor_tensor(out=hi_f[:], in0=near_keys, scalar=0.0, in1=hi_f[:], op0=ALU.is_gt, op1=ALU.mult).then_inc(him_s, 1)
                dve.wait_ge(him_s, 1)
                dve.tensor_scalar(hi_f[:], hi_f[:], -1.0, None, ALU.add).then_inc(him_s, 1)
                take_largest(dve, far_key[:, :], far_taken, FAR_CHUNK, FAR_ROUNDS, far_max, far_cleared)
                dve.tensor_reduce(full[:, 2:3], far_taken[:, :, 8 * FAR_ROUNDS - 1], AX.X, ALU.max).then_inc(full_s, 1)
                dve.tensor_scalar(far_node[:], far_taken[:, :, :].rearrange("p c s -> p (c s)"), -1.0, None, ALU.add).then_inc(node_s, 1)
                dve.wait_ge(node_s, 1)
                dve.tensor_scalar(far_field[:, 0], far_node[:], P - 1, None, ALU.bitwise_and).then_inc(far_field_s, 1)
                dve.tensor_scalar(far_field[:, 1], far_node[:], 7, None, ALU.arith_shift_right).then_inc(far_field_s, 1)
                dve.wait_ge(far_field_s, 2)
                dve.tensor_copy(far_field_b[:], far_field[:]).then_inc(fb_s, 1)
                dve.wait_ge(fb_s, 1)
                dve.wait_ge(him_s, 2)
                dve.sem_inc(far_sum_s, 2)
                dve.sem_inc(both_used, 2)

                def exponents(i, k):
                    dve.wait_ge(rows_s[k], 16 * 2 * NG * (i + 1))
                    if not (isinstance(i, int) and i == 0 and k == 0):
                        dve.wait_ge(weight_s, 2 * i + k)
                    dve.tensor_tensor(logit[:, k], rows_g[:, k, :, HC:TW], dst_g[:, k], ALU.add).then_inc(logit_s, 1)
                    dve.tensor_tensor(bound[:, k], dst_g[:, k], bcast(g.top[:], NG), ALU.add).then_inc(logit_s, 1)
                    dve.wait_ge(logit_s, 2 * (2 * i + k + 1))
                    for a in (logit, bound):
                        dve.scalar_tensor_tensor(out=a[:, k], in0=a[:, k], scalar=0.2, in1=a[:, k], op0=ALU.mult, op1=ALU.max).then_inc(lrelu_s, 1)
                    dve.wait_ge(lrelu_s, 2 * (2 * i + k + 1))
                    dve.tensor_tensor(logit[:, k], logit[:, k], bound[:, k], ALU.subtract).then_inc(diff_s, 1)

                def step(i, k, last):
                    g_ = 2 * i + k
                    dve.wait_ge(val_s, HEADS * (g_ + 1))
                    for kind, c in order:
                        if kind == "near":
                            q, turn = g_ * NG + c, (k * NG + c) % 2
                            dve.wait_ge(near_sum_s, q + 2 * NG - 1)
                            dve.tensor_scalar(lo[:, turn], iota_f[:], lo_f[:, bass.ds(q, 1)], None, ALU.is_equal).then_inc(lo_s, 1)
                            dve.scalar_tensor_tensor(out=rhs[:, turn], in0=spread(iota_f[:, 0:NB], TW), scalar=hi_f[:, bass.ds(q, 1)],
                                                     in1=val[:, k, c:c + 1, :].to_broadcast([P, NB, TW]),
                                                     op0=ALU.is_equal, op1=ALU.mult).then_inc(rhs_s, 1)
                        elif kind == "far":
                            q, turn = g_ * OWN + c, (k * OWN + c) % 2
                            here = bass.ds(g_ * FAR_GROUP + c * FAR_SUB, FAR_SUB)
                            dve.wait_ge(far_sum_s, q + 1)
                            dve.tensor_tensor(far_lo[:, turn], bcast(iota_b[:], FAR_SUB), spread(far_field_b[:, 0, here], P), ALU.is_equal).then_inc(far_lo_s, 1)
                            dve.tensor_tensor(far_hi[:, turn], bcast(iota_b[:, 0:NB], FAR_SUB), spread(far_field_b[:, 1, here], NB),
                                              ALU.is_equal).then_inc(far_hi_s, 1)
                        if kind == "near" and c == NG - 4 and not last:
                            exponents(i + k, 1 - k)

                exponents(0, 0)
                groups(dve, step)
                dve.wait_ge(near_sum_s, NEAR_COLS + 2 * NG + 1)
                for k, (a, b) in enumerate(SPLITS):
                    dve.tensor_copy(g.agg[:, a:b, :], near_sum[:, k, 0:(b - a) * TW].rearrange("p (n c) -> p n c", c=TW)).then_inc(done_s, 1)
                dve.wait_ge(far_sum_s, GROUPS * OWN + 3)
                dve.tensor_copy(g.count[:], far_sum[:]).then_inc(done_s, 1)
                dve.wait_ge(any_s, 1)
                dve.tensor_scalar(g.far_more[:], any_full[0:1, 2:3], 0.0, None, ALU.is_gt).then_inc(more_s, 1)
                dve.tensor_tensor(full[0:1, 0:1], any_full[0:1, 0:1], any_full[0:1, 1:2], ALU.max).then_inc(more_s, 1)
                dve.wait_ge(more_s, 2)
                dve.tensor_scalar(g.near_more[:], full[0:1, 0:1], 0.0, None, ALU.is_gt).then_inc(more_s, 1)
                dve.wait_ge(more_s, 3)
                dve.wait_ge(done_s, 4)

            @block.tensor
            def _(pe):
                pe.wait_ge(setup, 4)
                for n, (a, b) in enumerate(SPLITS):
                    pe.matmul(near_sum[:, n, 0:(b - a) * TW], zero[:, 0:P], zero[:, 0:(b - a) * TW], start=True, stop=False)
                pe.matmul(far_sum[:], zero_b[:], zero_b[:, 0:NB], start=True, stop=False)

                def step(i, k, last):
                    g_ = 2 * i + k
                    for kind, c in order:
                        if kind == "near":
                            q, turn = g_ * NG + c, (k * NG + c) % 2
                            pe.wait_ge(lo_s, q + 1)
                            pe.wait_ge(rhs_s, q + 1)
                            for n, (a, b) in enumerate(SPLITS):
                                mm = pe.matmul(near_sum[:, n, 0:(b - a) * TW], lo[:, turn], rhs[:, turn, a:b].rearrange("p n c -> p (n c)"),
                                               start=False, stop=False)
                            mm.then_inc(near_sum_s, 1)
                        elif kind == "shared":
                            q, turn = g_ * SHARED + c, (k * SHARED + c) % 2
                            pe.wait_ge(both_s, q + 1)
                            for e in range(FAR_SUB):
                                mm = pe.matmul(far_sum[:], both[:, turn, e, 0:P], both[:, turn, e, P:P + NB], start=False, stop=False)
                            mm.then_inc(both_used, 1)
                        else:
                            q, turn = g_ * OWN + c, (k * OWN + c) % 2
                            pe.wait_ge(far_lo_s, q + 1)
                            pe.wait_ge(far_hi_s, q + 1)
                            for e in range(FAR_SUB):
                                mm = pe.matmul(far_sum[:], far_lo[:, turn, e], far_hi[:, turn, e], start=False, stop=False)
                            mm.then_inc(far_sum_s, 1)

                groups(pe, step)
                for n, (a, b) in enumerate(SPLITS):
                    mm = pe.matmul(near_sum[:, n, 0:(b - a) * TW], zero[:, 0:P], zero[:, 0:(b - a) * TW], start=False, stop=True)
                mm.then_inc(near_sum_s, 1)
                pe.matmul(far_sum[:], zero_b[:], zero_b[:, 0:NB], start=False, stop=True).then_inc(far_sum_s, 1)


def gate_phase(nc, name, w, g):
    with Phase(nc, name) as ph:
        sb, sem = ph.sb, ph.sem
        b_gat, ln_g, ln_b = sb("b_gat", [P, HC]), sb("ln_g", [P, HC]), sb("ln_b", [P, HC])
        loop, far, bound = (sb(n, [P, NB, HEADS]) for n in ("loop", "far", "bound"))
        den, s4, e4, t4, rank = (sb(n, [P, NB, HEADS]) for n in ("den", "s4", "e4", "t4", "rank"))
        tmp, a = sb("tmp", [P, NB, HC]), sb("a", [P, NB, HC])
        mu, var, m1 = sb("mu", [P, NB]), sb("var", [P, NB]), sb("m1", [P, NB])
        eps = sb("eps", [P, 1])
        loaded, consts, step, exp_in, exp_out, var_in, lnv_s, rstd_s, sh_in, sh_out = (
            sem(n) for n in ("loaded", "consts", "step", "exp_in", "exp_out", "var_in", "lnv", "rstd", "sh_in", "sh_out"))
        h = g.h[:, :, 0:HC]

        def col(t):
            return t.rearrange("p (n o) -> p n o", o=1)

        def heads(t):
            return t

        with nc.Block() as block:
            @block.sync
            def _(sp):
                for t, n in ((b_gat, "b_gat"), (ln_g, "ln_gamma"), (ln_b, "ln_beta")):
                    sp.dma_start(t[:], rows(w[n])).then_inc(loaded, 16)

            @block.gpsimd
            def _(pool):
                pool.memset(eps[:], 1e-5).then_inc(consts, 1)

            @block.scalar
            def _(act):
                act.wait_ge(consts, 1)
                act.wait_ge(exp_in, 1)
                act.activation(loop[:], loop[:], ACT.Exp).then_inc(exp_out, 1)
                act.activation(far[:], far[:], ACT.Exp).then_inc(exp_out, 1)
                act.wait_ge(var_in, 1)
                act.activation(var[:], var[:], ACT.Ln, bias=eps[:], scale=1.0 / HC).then_inc(lnv_s, 1)
                act.wait_ge(lnv_s, 1)
                act.activation(var[:], var[:], ACT.Exp, scale=-0.5).then_inc(rstd_s, 1)
                act.wait_ge(sh_in, 1)
                act.activation(e4[:], e4[:], ACT.Exp).then_inc(sh_out, 1)

            @block.vector
            def _(dve):
                done = [0]

                def then(ins, s=step):
                    ins.then_inc(step, 1)
                    done[0] += 1
                    dve.wait_ge(step, done[0])

                dve.wait_ge(loaded, 48)
                then(dve.tensor_tensor(loop[:], g.h[:, :, HC:TW], g.a_dst[:], ALU.add))
                then(dve.tensor_tensor(far[:], g.a_dst[:], bcast(g.last[:, HC:TW], NB), ALU.add))
                then(dve.tensor_tensor(bound[:], g.a_dst[:], bcast(g.top[:], NB), ALU.add))
                for t in (loop, far, bound):
                    then(dve.scalar_tensor_tensor(out=t[:], in0=t[:], scalar=0.2, in1=t[:], op0=ALU.mult, op1=ALU.max))
                then(dve.tensor_tensor(loop[:], loop[:], bound[:], ALU.subtract))
                then(dve.tensor_tensor(far[:], far[:], bound[:], ALU.subtract))
                dve.sem_inc(exp_in, 1)
                dve.wait_ge(exp_out, 2)
                then(dve.tensor_tensor(far[:], far[:], col(g.count[:]).to_broadcast([P, NB, HEADS]), ALU.mult))
                then(dve.tensor_tensor(den[:], g.agg[:, :, HC:TW], loop[:], ALU.add))
                then(dve.scalar_tensor_tensor(out=den[:], in0=den[:], scalar=1e-16, in1=far[:], op0=ALU.add, op1=ALU.add))
                then(dve.reciprocal(den[:], den[:]))
                for k in range(HEADS):
                    e = slice(EXPERTS * k, EXPERTS * (k + 1))
                    wide = [P, NB, EXPERTS]
                    then(dve.tensor_tensor(tmp[:, :, e], h[:, :, e], loop[:, :, k:k + 1].to_broadcast(wide), ALU.mult))
                    then(dve.tensor_tensor(a[:, :, e], g.agg[:, :, e], tmp[:, :, e], ALU.add))
                    then(dve.tensor_tensor(tmp[:, :, e], bcast(g.last[:, e], NB), far[:, :, k:k + 1].to_broadcast(wide), ALU.mult))
                    then(dve.tensor_tensor(a[:, :, e], a[:, :, e], tmp[:, :, e], ALU.add))
                    then(dve.tensor_tensor(a[:, :, e], a[:, :, e], den[:, :, k:k + 1].to_broadcast(wide), ALU.mult))
                then(dve.tensor_tensor(a[:], a[:], bcast(b_gat[:], NB), ALU.add))
                then(dve.tensor_reduce(mu[:], a[:], AX.X, ALU.add))
                then(dve.tensor_scalar(mu[:], mu[:], 1.0 / HC, None, ALU.mult))
                then(dve.tensor_tensor(a[:], a[:], col(mu[:]).to_broadcast([P, NB, HC]), ALU.subtract))
                then(dve.tensor_tensor(tmp[:], a[:], a[:], ALU.mult))
                then(dve.tensor_reduce(var[:], tmp[:], AX.X, ALU.add))
                dve.sem_inc(var_in, 1)
                dve.wait_ge(rstd_s, 1)
                then(dve.tensor_tensor(a[:], a[:], col(var[:]).to_broadcast([P, NB, HC]), ALU.mult))
                then(dve.tensor_tensor(a[:], a[:], bcast(ln_g[:], NB), ALU.mult))
                then(dve.tensor_tensor(a[:], a[:], bcast(ln_b[:], NB), ALU.add))
                then(dve.tensor_reduce(s4[:], a[:, :, :].rearrange("p n (h e) -> p n e h", h=HEADS), AX.X, ALU.add))
                then(dve.tensor_scalar(s4[:], s4[:], 1.0 / HEADS, None, ALU.mult))
                then(dve.memset(rank[:], 0.0))
                for j in range(EXPERTS):
                    for k in range(EXPERTS):
                        if j != k:
                            op = ALU.is_ge if j < k else ALU.is_gt
                            then(dve.tensor_tensor(m1[:], s4[:, :, j], s4[:, :, k], op))
                            then(dve.tensor_tensor(rank[:, :, k], rank[:, :, k], m1[:], ALU.add))
                then(dve.tensor_reduce(m1[:], s4[:], AX.X, ALU.max))
                then(dve.tensor_tensor(e4[:], s4[:], col(m1[:]).to_broadcast([P, NB, EXPERTS]), ALU.subtract))
                dve.sem_inc(sh_in, 1)
                dve.wait_ge(sh_out, 1)
                then(dve.scalar_tensor_tensor(out=e4[:], in0=rank[:], scalar=1.5, in1=e4[:], op0=ALU.is_lt, op1=ALU.mult))
                then(dve.tensor_reduce(m1[:], e4[:], AX.X, ALU.add))
                then(dve.reciprocal(m1[:], m1[:]))
                then(dve.tensor_tensor(g.gate[:], e4[:], col(m1[:]).to_broadcast([P, NB, EXPERTS]), ALU.mult))


def experts_phase(nc, name, g, x_in, x_out):
    with Phase(nc, name) as ph:
        sb, ps, sem = ph.sb, ph.ps, ph.sem
        w_1, w_2, b_1, b_2 = g.w_1, g.w_2, g.b_1, g.b_2
        ident = sb("ident", [P, P])
        tn, xt, xo = (sb(n, [P, 2, KB, T]) for n in ("tn", "xt", "xo"))
        gt = sb("gt", [P, 2, SUB, EXPERTS])
        hid = sb("hid", [P, 2, FEB, T])
        acc = sb("acc", [P, SUB, C])
        up = ps("up", [P, FEB, T])
        down = ps("down", [P, 2, 2, C])
        turned = ps("turned", [P, KB, T])
        consts = sem("consts")
        in_s, stored = [sem("in0"), sem("in1")], [sem("stored0"), sem("stored1")]
        free, gt_s, up_s, hid_s, down_s, bias_s, acc_s, turn_s, out_s = (
            sem(n) for n in ("free", "gt", "up", "hid", "down", "bias", "acc", "turn", "out"))
        E_ = EXPERTS
        with nc.Block() as block:
            @block.sync
            def _(sp):
                with sp.Fori(0, TI) as i:
                    for b in range(B):
                        s = i * B + b
                        at = bass.ds(i * T, T)
                        sp.wait_ge(out_s, s + 1)
                        sp.dma_start(tn[:, b], g.tn[b].rearrange("(k p) t -> p k t", p=P)[:, :, at]).then_inc(in_s[b], 16)
                        sp.dma_start(xt[:, b], x_in[b].rearrange("(k p) t -> p k t", p=P)[:, :, at]).then_inc(in_s[b], 16)

            @block.gpsimd
            def _(pool):
                pool.memset(ident[:], 0.0).then_inc(consts, 1)
                pool.wait_ge(consts, 1)
                pool.affine_select(out=ident[:], in_=ident[:], compare_op=ALU.not_equal, fill=1.0, base=0,
                                   pattern=[[-1, P]], channel_multiplier=1).then_inc(consts, 1)
                with pool.Fori(0, TI) as i:
                    for b in range(B):
                        s = i * B + b
                        pool.wait_ge(out_s, s + 3)
                        pool.dma_start(x_out[b].rearrange("(k p) t -> p k t", p=P)[:, :, bass.ds(i * T, T)], xo[:, b]).then_inc(stored[b], 16)
                        pool.wait_ge(stored[b], 16 * i + 16)
                        pool.sem_inc(free, 1)

            @block.tensor
            def _(pe):
                pe.wait_ge(consts, 2)
                with pe.Fori(0, TI) as i:
                    for b in range(B):
                        s = i * B + b
                        pe.wait_ge(in_s[b], 32 * i + 32)
                        for e in range(E_ + 1):
                            if e < E_:
                                for f in range(FEB):
                                    pe.wait_ge(hid_s, FEB * (E_ * s + e - 1) + f + 1 + FEB)
                                    for kb in range(KB):
                                        mm = pe.matmul(up[:, f], w_1[:, e, kb, f * P:(f + 1) * P], tn[:, b, kb], start=kb == 0, stop=kb == KB - 1)
                                    mm.then_inc(up_s, 1)
                            if e > 0:
                                pe.wait_ge(hid_s, FEB * (E_ * s + e) + FEB)
                                for sub in range(SUB):
                                    n = SUB * (E_ * s + e - 1) + sub
                                    pe.wait_ge(acc_s, n - 1 + SUB)
                                    half = down[:, sub % 2, 0]
                                    for f in range(FEB):
                                        mm = pe.matmul(half, hid[:, (e - 1) % 2, f, sub * P:(sub + 1) * P], w_2[:, e - 1, f], start=f == 0, stop=f == FEB - 1)
                                    mm.then_inc(down_s, 1)
                        pe.wait_ge(acc_s, SUB * E_ * (s + 1) + SUB)
                        pe.wait_ge(out_s, s + 2)
                        for sub in range(SUB):
                            for kb in range(KB):
                                mm = pe.transpose(turned[:, kb, sub * P:(sub + 1) * P], acc[:, sub, kb * P:(kb + 1) * P], ident[:])
                        mm.then_inc(turn_s, 1)

            @block.scalar
            def _(act):
                act.sem_inc(hid_s, FEB)
                with act.Fori(0, TI) as i:
                    for b in range(B):
                        s = i * B + b
                        for e in range(E_):
                            act.wait_ge(down_s, SUB * (E_ * s + e - 2) + SUB + 2 * SUB)
                            for f in range(FEB):
                                act.wait_ge(up_s, FEB * (E_ * s + e) + f + 1)
                                act.activation(hid[:, e % 2, f], up[:, f], ACT.Gelu, bias=b_1[:, e, f:f + 1]).then_inc(hid_s, 1)

            @block.vector
            def _(dve):
                dve.sem_inc(out_s, 2)
                dve.sem_inc(acc_s, SUB)
                dve.sem_inc(free, 2)
                dve.sem_inc(down_s, 2 * SUB)
                with dve.Fori(0, TI) as i:
                    for b in range(B):
                        s = i * B + b
                        dve.tensor_copy(gt[:, b], g.gate[:, bass.ds(i * SUB + b * (NB // B), SUB), :]).then_inc(gt_s, 1)
                        dve.wait_ge(gt_s, s + 1)
                        for sub in range(SUB):
                            for e in range(E_):
                                if e == 0:
                                    dve.tensor_scalar(acc[:, sub], b_2[:, e], gt[:, b, sub, e:e + 1], None, ALU.mult).then_inc(bias_s, 1)
                                else:
                                    dve.wait_ge(bias_s, E_ * (SUB * s + sub) + e)
                                    dve.scalar_tensor_tensor(out=acc[:, sub], in0=b_2[:, e], scalar=gt[:, b, sub, e:e + 1], in1=acc[:, sub],
                                                             op0=ALU.mult, op1=ALU.add).then_inc(bias_s, 1)
                        dve.wait_ge(bias_s, E_ * SUB * (s + 1))
                        for e in range(E_):
                            for sub in range(SUB):
                                n = SUB * (E_ * s + e) + sub
                                dve.wait_ge(down_s, n + 1 + 2 * SUB)
                                if e > 0:
                                    dve.wait_ge(acc_s, n - SUB + 1 + SUB)
                                dve.scalar_tensor_tensor(out=acc[:, sub], in0=down[:, sub % 2, 0], scalar=gt[:, b, sub, e:e + 1], in1=acc[:, sub],
                                                         op0=ALU.mult, op1=ALU.add).then_inc(acc_s, 1)
                        dve.wait_ge(turn_s, s + 1)
                        dve.wait_ge(in_s[b], 32 * i + 32)
                        dve.wait_ge(free, s + 1)
                        dve.tensor_tensor(xo[:, b], turned[:], xt[:, b], ALU.add).then_inc(out_s, 1)
TILE_OUT, TILE_IN, KERNEL = 4, 6, 3
NT = HW // TILE_OUT
TP = TILE_IN * TILE_IN
HALF_T = NT // 2
HALF_R = HW // 2
N_T = HALF_T * NT
ROWS = HALF_R + 2
WIDE = HW + 2


def kernel_points_phase(nc, name, w, points):
    with Phase(nc, name) as ph:
        sb, sem = ph.sb, ph.sem
        k9 = sb("k9", [P, KB, KERNEL, KERNEL, C])
        half = sb("half", [P, TILE_IN, KERNEL, C])
        mask = sb("mask", [P, TILE_IN, TILE_IN, C])
        s0, s1 = sb("s0", [P, TILE_IN, C]), sb("s1", [P, TILE_IN, C])
        one = sb("one", [P, 1])
        loaded, mask_in, step, masked = sem("loaded"), [sem(f"mask_in{k}") for k in range(TILE_IN)], sem("step"), sem("masked")
        one_s, kept = sem("one"), sem("kept")
        mask_d = w["mask"].rearrange("(k p) t u o -> p k t u o", p=P)
        k_d = w["weight"].rearrange("(k p) i j o -> p k (i j o)", p=P)
        chunks = [(kb, t) for kb in range(KB) for t in range(TILE_IN)]

        with nc.Block() as block:
            @block.sync
            def _(sp):
                for kb in range(KB):
                    sp.dma_start(k9[:, kb].rearrange("p i j o -> p (i j o)"), k_d[:, kb]).then_inc(loaded, 16)
                for n, (kb, t) in enumerate(chunks):
                    if kb:
                        sp.wait_ge(masked, n - TILE_IN + 1)
                    sp.dma_start(mask[:, t], mask_d[:, kb, t]).then_inc(mask_in[t], 16)

            @block.gpsimd
            def _(pool):
                pool.memset(one[:], 1.0).then_inc(one_s, 1)

            @block.scalar
            def _(act):
                act.wait_ge(one_s, 1)
                for kb, t in chunks:
                    act.wait_ge(mask_in[t], 16 * kb + 16)
                    act.activation(mask[:, t], mask[:, t], ACT.Identity, scale=-1.0, bias=one[:]).then_inc(kept, 1)

            @block.vector
            def _(dve):
                done = [0]

                def then(ins):
                    ins.then_inc(step, 1)
                    done[0] += 1
                    dve.wait_ge(step, done[0])

                def expand(w0, w1, w2, out, n):
                    a, b = s0[:, 0:n], s1[:, 0:n]
                    then(dve.tensor_scalar(out(0), w0, 0.25, None, ALU.mult))
                    then(dve.tensor_copy(out(5), w2))
                    then(dve.tensor_tensor(a, w0, w2, ALU.add))
                    for k, op in ((1, ALU.add), (2, ALU.subtract)):
                        then(dve.tensor_tensor(b, a, w1, op))
                        then(dve.tensor_scalar(out(k), b, -1.0 / 6, None, ALU.mult))
                    then(dve.scalar_tensor_tensor(out=a, in0=w0, scalar=0.25, in1=w2, op0=ALU.mult, op1=ALU.add))
                    for k, f in ((3, 0.5), (4, -0.5)):
                        then(dve.scalar_tensor_tensor(out=b, in0=w1, scalar=f, in1=a, op0=ALU.mult, op1=ALU.add))
                        then(dve.tensor_scalar(out(k), b, 1.0 / 6, None, ALU.mult))

                dve.wait_ge(loaded, 16 * KB)
                for kb in range(KB):
                    expand(k9[:, kb, 0], k9[:, kb, 1], k9[:, kb, 2], lambda t: half[:, t], KERNEL)
                    expand(half[:, :, 0], half[:, :, 1], half[:, :, 2], lambda u: points[:, kb, u], TILE_IN)
                    for t in range(TILE_IN):
                        n = kb * TILE_IN + t
                        dve.wait_ge(kept, n + 1)
                        dve.tensor_tensor(points[:, kb, :, t], points[:, kb, :, t], mask[:, t], ALU.mult).then_inc(masked, 1)
                dve.wait_ge(masked, KB * TILE_IN)


def winograd_phase(nc, name, w, points, x_in, x_out):
    with Phase(nc, name) as ph:
        sb, ps, sem = ph.sb, ph.ps, ph.sem
        ones_mean, eps, bias = sb("ones_mean", [P, P]), sb("eps", [P, 1]), sb("bias", [P, KB])
        v = sb("v", [P, KB, ROWS, WIDE])
        xt, sq = sb("xt", [P, 2, KB, T]), sb("sq", [P, KB, T])
        r = sb("r", [P, TILE_IN, HALF_T, WIDE])
        pts = sb("pts", [P, KB, TILE_IN, TILE_IN, N_T])
        prod = sb("prod", [P, TILE_IN, TILE_IN, N_T])
        s1 = sb("s1", [P, TILE_OUT, TILE_IN, N_T])
        rstd = s1[:, :, :, :].rearrange("p a u n -> p (a u n)")
        y = sb("y", [P, HALF_R, HW])
        res = sb("res", [P, HALF_R * HW])
        tmp = [sb(f"tmp{k}", [P, TILE_IN * N_T]) for k in range(2)]
        bank = ps("bank", [P, 8, T])
        G4 = 4
        n_g = TP // G4
        consts, weights_in, res_in, stored = (sem(n) for n in ("consts", "weights_in", "res_in", "stored"))
        x_loaded = [sem("x_loaded0"), sem("x_loaded1")]
        mean, cent, sqd, var, lns, rst, v_s, clean = (sem(n) for n in ("mean", "cent", "sqd", "var", "lns", "rst", "v", "clean"))
        rows_s, pts_s, prod_s, copied, out_s, step = (sem(n) for n in ("rows", "pts", "prod", "copied", "out", "step"))
        pieces = [[(0, 8), (8, 8), (16, 8), (24, 8), (32, 1)], [(31, 1), (32, 8), (40, 8), (48, 8), (56, 8)]]
        NP_ = len(pieces[0])
        N_PX = sum(n for _, n in pieces[0]) * HW

        def piece(s, k):
            row, n = pieces[s % 2][k]
            at = row + 1 - (s % 2) * HALF_R
            begin = sum(m for _, m in pieces[s % 2][:k]) * HW
            return s * NP_ + k, n * HW, slice(at, at + n), slice(begin, begin + n * HW)
        n_steps = 2 * B
        x_px = x_in.rearrange("b (k p) t -> b p k t", p=P)
        o_px = x_out.rearrange("b (k p) t -> b p k t", p=P)

        with nc.Block() as block:
            @block.sync
            def _(sp):
                with nc.allow_non_contiguous_dma(reason="a short vector"):
                    sp.dma_start(bias[:], w["bias"].rearrange("(k p) -> p k", p=P)).then_inc(weights_in, 16)
                def load(s):
                    for k, (row, n) in enumerate(pieces[s % 2]):
                        q = s * NP_ + k
                        if q > 1:
                            sp.wait_ge(cent, q - 1)
                        sp.dma_start(xt[:, q % 2, :, 0:n * HW], x_px[s // 2, :, :, row * HW:(row + n) * HW]).then_inc(x_loaded[q % 2], 16)

                load(0)
                for s in range(n_steps):
                    b, h = s // 2, s % 2
                    if s + 1 < n_steps:
                        load(s + 1)
                    for ob in range(KB):
                        if s or ob:
                            sp.wait_ge(out_s, KB * s + ob)
                        sp.dma_start(res[:], x_px[b, :, ob, h * HALF_R * HW:(h + 1) * HALF_R * HW]).then_inc(res_in, 16)

            @block.gpsimd
            def _(pool):
                pool.memset(ones_mean[:], 1.0 / C).then_inc(consts, 1)
                pool.memset(eps[:], 1e-6).then_inc(consts, 1)
                pool.memset(v[:], 0.0).then_inc(consts, 1)
                for s in range(n_steps):
                    b, h = s // 2, s % 2
                    for ob in range(KB):
                        pool.wait_ge(out_s, KB * s + ob + 1)
                        pool.dma_start(o_px[b, :, ob, h * HALF_R * HW:(h + 1) * HALF_R * HW],
                                       y[:].rearrange("p r c -> p (r c)")).then_inc(stored, 16)
                pool.wait_ge(stored, 16 * KB * n_steps)

            @block.tensor
            def _(pe):
                def mean_of(s, k):
                    q, w_, _, _ = piece(s, k)
                    pe.wait_ge(x_loaded[q % 2], 16 * (q // 2) + 16)
                    if q:
                        pe.wait_ge(cent, q)
                    for kb in range(KB):
                        mm = pe.matmul(bank[:, 6, 0:w_], ones_mean[:], xt[:, q % 2, kb, 0:w_], start=kb == 0, stop=kb == KB - 1)
                    mm.then_inc(mean, 1)

                def statistics(s, beside):
                    mean_of(s, 0)
                    for k in range(NP_):
                        q, w_, _, _ = piece(s, k)
                        beside(2 * k)
                        if k + 1 < NP_:
                            mean_of(s, k + 1)
                        pe.wait_ge(sqd, q + 1)
                        if q:
                            pe.wait_ge(lns, q)
                        for kb in range(KB):
                            mm = pe.matmul(bank[:, 7, 0:w_], ones_mean[:], sq[:, kb, 0:w_], start=kb == 0, stop=kb == KB - 1)
                        mm.then_inc(var, 1)
                        beside(2 * k + 1)

                def products(s, ob, groups):
                    pe.wait_ge(pts_s, 12 * KB * (s + 1))
                    for gr in groups:
                        c = (s * KB + ob) * n_g + gr
                        if c >= 6:
                            pe.wait_ge(copied, c - 5)
                        for j in range(G4):
                            u, t = divmod(gr * G4 + j, TILE_IN)
                            for kb in range(KB):
                                mm = pe.matmul(bank[:, c % 6, j * N_T:(j + 1) * N_T], points[:, kb, u, t, ob * P:(ob + 1) * P],
                                               pts[:, kb, u, t], start=kb == 0, stop=kb == KB - 1)
                        mm.then_inc(prod_s, 1)

                pe.wait_ge(consts, 3)
                statistics(0, lambda gr: None)
                for s in range(n_steps):
                    if s + 1 < n_steps:
                        statistics(s + 1, lambda gr: products(s, 0, range(gr, min(gr + 1, n_g))))
                    else:
                        products(s, 0, range(n_g))
                    products(s, 1, range(n_g))

            @block.scalar
            def _(act):
                flat = prod[:].rearrange("p u t n -> p (u t n)")

                def statistics(s, beside):
                    if s > 1:
                        act.wait_ge(out_s, KB * (s - 1))
                    for k in range(NP_):
                        q, w_, at, px = piece(s, k)
                        act.wait_ge(cent, q + 1)
                        act.activation(sq[:, :, 0:w_].rearrange("p k (r c) -> p k r c", c=HW), v[:, :, at, 1:1 + HW], ACT.Square).then_inc(sqd, 1)
                        beside(2 * k)
                        act.wait_ge(var, q + 1)
                        act.activation(rstd[:, px], bank[:, 7, 0:w_], ACT.Ln, bias=eps[:]).then_inc(lns, 1)
                        beside(2 * k + 1)
                    act.wait_ge(lns, NP_ * (s + 1))
                    act.activation(rstd[:, 0:N_PX], rstd[:, 0:N_PX], ACT.Exp, scale=-0.5).then_inc(rst, 1)

                def copies(s, ob, groups):
                    if s or ob:
                        act.wait_ge(out_s, KB * s + ob)
                    for gr in groups:
                        c = (s * KB + ob) * n_g + gr
                        act.wait_ge(prod_s, c + 1)
                        act.copy(flat[:, gr * G4 * N_T:(gr + 1) * G4 * N_T], bank[:, c % 6]).then_inc(copied, 1)

                act.wait_ge(consts, 3)
                statistics(0, lambda gr: None)
                for s in range(n_steps):
                    if s + 1 < n_steps:
                        statistics(s + 1, lambda gr: copies(s, 0, range(gr, min(gr + 1, n_g))))
                    else:
                        copies(s, 0, range(n_g))
                    copies(s, 1, range(n_g))

            @block.vector
            def _(dve):
                dve.wait_ge(consts, 3)
                dve.wait_ge(weights_in, 16)
                done = [0]

                def then(ins):
                    ins.then_inc(step, 1)
                    done[0] += 1
                    dve.wait_ge(step, done[0])

                def input_points(d, out, a, b, last):
                    then(dve.scalar_tensor_tensor(out=a, in0=d(2), scalar=-4.0, in1=d(4), op0=ALU.mult, op1=ALU.add))
                    then(dve.scalar_tensor_tensor(out=b, in0=d(1), scalar=-4.0, in1=d(3), op0=ALU.mult, op1=ALU.add))
                    dve.tensor_tensor(out(1), a, b, ALU.add).then_inc(last, 1)
                    dve.tensor_tensor(out(2), a, b, ALU.subtract).then_inc(last, 1)
                    dve.wait_ge(last, marks[last] + 2)
                    then(dve.tensor_tensor(a, d(4), d(2), ALU.subtract))
                    then(dve.tensor_tensor(b, d(3), d(1), ALU.subtract))
                    dve.scalar_tensor_tensor(out=out(3), in0=b, scalar=2.0, in1=a, op0=ALU.mult, op1=ALU.add).then_inc(last, 1)
                    dve.scalar_tensor_tensor(out=out(4), in0=b, scalar=-2.0, in1=a, op0=ALU.mult, op1=ALU.add).then_inc(last, 1)
                    dve.wait_ge(last, marks[last] + 4)
                    then(dve.scalar_tensor_tensor(out=a, in0=d(2), scalar=-5.0, in1=d(4), op0=ALU.mult, op1=ALU.add))
                    then(dve.scalar_tensor_tensor(out=b, in0=d(3), scalar=-5.0, in1=d(5), op0=ALU.mult, op1=ALU.add))
                    dve.scalar_tensor_tensor(out=out(0), in0=d(0), scalar=4.0, in1=a, op0=ALU.mult, op1=ALU.add).then_inc(last, 1)
                    dve.scalar_tensor_tensor(out=out(5), in0=d(1), scalar=4.0, in1=b, op0=ALU.mult, op1=ALU.add).then_inc(last, 1)
                    marks[last] += 6
                    dve.wait_ge(last, marks[last])

                def output_rows(m, out, a, b):
                    then(dve.tensor_tensor(a, m(1), m(2), ALU.add))
                    then(dve.tensor_tensor(b, m(3), m(4), ALU.add))
                    then(dve.tensor_tensor(out(0), a, b, ALU.add))
                    then(dve.tensor_tensor(out(0), out(0), m(0), ALU.add))
                    then(dve.tensor_scalar(b, b, 4.0, None, ALU.mult))
                    then(dve.tensor_tensor(out(2), a, b, ALU.add))
                    then(dve.tensor_tensor(a, m(1), m(2), ALU.subtract))
                    then(dve.tensor_tensor(b, m(3), m(4), ALU.subtract))
                    then(dve.tensor_scalar(b, b, 2.0, None, ALU.mult))
                    then(dve.tensor_tensor(out(1), a, b, ALU.add))
                    then(dve.tensor_tensor(a, a, m(5), ALU.add))
                    then(dve.tensor_scalar(b, b, 4.0, None, ALU.mult))
                    then(dve.tensor_tensor(out(3), a, b, ALU.add))

                marks = {rows_s: 0, pts_s: 0}
                def norm(s):
                    h = s % 2
                    if s:
                        border = 0 if h == 0 else ROWS - 1
                        then(dve.memset(v[:, :, border, :], 0.0))
                    for k in range(NP_):
                        q, w_, at, px = piece(s, k)
                        dve.wait_ge(mean, q + 1)
                        dve.wait_ge(x_loaded[q % 2], 16 * (q // 2) + 16)
                        for kb in range(KB):
                            centred = dve.tensor_tensor(v[:, kb, at, 1:1 + HW], xt[:, q % 2, kb, 0:w_].rearrange("p (r c) -> p r c", c=HW),
                                                   bank[:, 6, 0:w_].rearrange("p (r c) -> p r c", c=HW), ALU.subtract)
                            if kb == KB - 1:
                                centred.then_inc(cent, 1)
                    dve.wait_ge(cent, NP_ * (s + 1))
                    dve.wait_ge(rst, s + 1)
                    top = 1 if h == 0 else 0
                    inner = v[:, :, top:top + N_PX // HW, 1:1 + HW]
                    for kb in range(KB):
                        dve.tensor_tensor(inner[:, kb], inner[:, kb], rstd[:, 0:N_PX].rearrange("p (r c) -> p r c", c=HW), ALU.mult).then_inc(v_s, 1)
                    dve.wait_ge(v_s, KB * (s + 1))

                norm(0)
                for s in range(n_steps):
                    for kb in range(KB):
                        n1, n2 = HALF_T * WIDE, TILE_IN * N_T
                        ta, tb = (t[:, 0:n1].rearrange("p (r c) -> p r c", c=WIDE) for t in tmp)
                        input_points(lambda i: v[:, kb, i:i + TILE_OUT * (HALF_T - 1) + 1:TILE_OUT, :], lambda t: r[:, t], ta, tb, rows_s)
                        ta, tb = (t[:, 0:n2].rearrange("p (r c) -> p r c", c=NT) for t in tmp)
                        rr = r[:].rearrange("p t h c -> p (t h) c")
                        pp = pts[:, kb].rearrange("p u t (h c) -> p u (t h) c", c=NT)
                        input_points(lambda j: rr[:, :, j:j + TILE_OUT * (NT - 1) + 1:TILE_OUT], lambda u: pp[:, u], ta, tb, pts_s)
                        dve.sem_inc(pts_s, 6)
                        marks[pts_s] += 6
                    if s + 1 < n_steps:
                        norm(s + 1)
                    for ob in range(KB):
                        dve.wait_ge(copied, ((s * KB) + ob + 1) * n_g)
                        ta, tb = (t[:, 0:TILE_IN * N_T].rearrange("p (u n) -> p u n", n=N_T) for t in tmp)
                        output_rows(lambda t: prod[:, :, t], lambda p: s1[:, p], ta, tb)
                        if s or ob:
                            dve.wait_ge(stored, 16 * (KB * s + ob))
                        ta, tb = (t[:, 0:TILE_OUT * N_T].rearrange("p (q h c) -> p q h c", q=TILE_OUT, c=NT) for t in tmp)
                        yv = y[:].rearrange("p (h a) (c q) -> p a h c q", a=TILE_OUT, q=TILE_OUT)
                        output_rows(lambda u: s1[:, :, u].rearrange("p a (h c) -> p a h c", c=NT), lambda q: yv[:, :, :, :, q], ta, tb)
                        dve.wait_ge(res_in, 16 * (KB * s + ob) + 16)
                        dve.scalar_tensor_tensor(out=y[:].rearrange("p r c -> p (r c)"), in0=y[:].rearrange("p r c -> p (r c)"),
                                                 scalar=bias[:, ob:ob + 1], in1=res[:], op0=ALU.add, op1=ALU.add).then_inc(out_s, 1)


def graph_experts(nc, name, w, x_in, x_out):
    with ExitStack() as ctx:
        g = Graph(nc, ctx, name)
        with nc.sbuf_tensor(f"{name}_near_key", [P, EC + PICKS], F32) as near_key, nc.sbuf_tensor(f"{name}_far_key", [P, EC], F32) as far_key:
            features_phase(nc, f"{name}_features", w, g, x_in, near_key, far_key)
            edges_phase(nc, f"{name}_edges", w, g, near_key, far_key)
            far_rest_phase(nc, f"{name}_far_rest", g, far_key)
            near_rest_phase(nc, f"{name}_near_rest", g, near_key)
        gate_phase(nc, f"{name}_gate", w, g)
        experts_phase(nc, f"{name}_experts", g, x_in, x_out)


def build(nc, a, out):
    x1, x2, x3 = (nc.dram_tensor(n, (B, C, L), F32, kind="Internal").ap() for n in ("x1", "x2", "x3"))

    def layer(prefix):
        return {k[len(prefix):]: v for k, v in a.items() if k.startswith(prefix)}

    mamba_phase(nc, layer("L0_conv_"), a["x"], x1)
    graph_experts(nc, "g0", layer("L0_ffn_"), x1, x2)
    conv = layer("L1_conv_")
    with nc.sbuf_tensor("points", [P, KB, TILE_IN, TILE_IN, C], F32) as points:
        kernel_points_phase(nc, "kernels", conv, points)
        winograd_phase(nc, "winograd", conv, points, x2, x3)
    graph_experts(nc, "g1", layer("L1_ffn_"), x3, out)


TRANSPOSED = ("W_in", "W_xp", "W_dt", "W_out", "W1", "W2")


def kernel(**inputs):
    import concourse.bacc as _bacc
    from concourse.bass_utils import run_bass_kernel_spmd as _run

    laid = {}
    for name, value in inputs.items():
        v = np.asarray(value)
        if name == "x":
            v = v.reshape(B, C, L)
        elif name.startswith("L0_conv_") and name[8:] in TRANSPOSED:
            name, v = name + "T", v.T
        elif name in ("L1_conv_weight", "L1_conv_mask"):
            v = v.transpose(1, 2, 3, 0)
        laid[name] = np.ascontiguousarray(v)

    nc = _bacc.Bacc("TRN2", target_bir_lowering=False, num_devices=1)
    arrays, aps = {}, {}
    for name, v in laid.items():
        arrays[f"in_{name}"] = v
        aps[name] = nc.dram_tensor(f"in_{name}", v.shape, mybir.dt.from_np(v.dtype), kind="ExternalInput").ap()
    out = nc.dram_tensor("out", (B, C, L), F32, kind="ExternalOutput").ap()
    build(nc, aps, out)
    r = _run(nc, [arrays], core_ids=[0])
    return r.results[0]["out"].reshape(B, C, HW, HW)
```
